# Optimizing a Trainium2 kernel written in Bass

```python
import numpy as np
import jax
import jax.numpy as jnp

def _softmax(x, axis=-1):
    return jax.nn.softmax(x, axis=axis)

def _gelu(x):
    return jax.nn.gelu(x, approximate=True)

def _silu(x):
    return jax.nn.silu(x)

def _sigmoid(x):
    return jax.nn.sigmoid(x)

def _layernorm(x, axis=-1, eps=1e-05):
    m = jnp.mean(x, axis=axis, keepdims=True)
    v = jnp.var(x, axis=axis, keepdims=True)
    return (x - m) / jnp.sqrt(v + eps)

def _scatter_add(tgt, idx, src, axis=0):
    return tgt.at[idx].add(src)

def _segment_sum(src, seg, n):
    return jax.ops.segment_sum(src, seg, n)
kernel_name = 'mk_decoder_preln_d1_seqx_r4_ba63ad'

def setup_inputs(seed: int=0):
    np.random.seed(seed)
    _w = jnp.asarray

    def _rec_inputs():
        import jax
        import jax.numpy as jnp
        _rk = jax.random.key(seed)
        x = -0.0002928 + 1 * jax.random.normal(jax.random.fold_in(_rk, 1), (2, 512, 256), jnp.float32)
        _lenS = 512 - jax.random.randint(jax.random.fold_in(_rk, 7), (2,), 0, max(1, 512 // 4) + 1, jnp.int32)
        _lenS2 = 1024 - jax.random.randint(jax.random.fold_in(_rk, 8), (2,), 0, max(1, 1024 // 4) + 1, jnp.int32)
        _ctx_1024P = jax.random.normal(jax.random.fold_in(_rk, 11), (2, 16, 256), jnp.float32)
        _ctx_1024c = jax.random.dirichlet(jax.random.fold_in(_rk, 511), 0.3 * jnp.ones((16,), jnp.float32), (2, 1024))
        _ctx_1024t = jnp.einsum('bsk,bkd->bsd', _ctx_1024c, _ctx_1024P)
        _ctx_1024t = _ctx_1024t * jax.lax.rsqrt(jnp.mean(jnp.square(_ctx_1024t)) + 1e-12) * 0.953939
        ctx_1024 = -1.39393e-06 + 0.999914 * (_ctx_1024t + 0.3 * jax.random.normal(jax.random.fold_in(_rk, 611), (2, 1024, 256), jnp.float32))
        _validS = jnp.arange(512)[None, :] < _lenS[:, None]
        _validS2 = jnp.arange(1024)[None, :] < _lenS2[:, None]
        _causal = jnp.tril(jnp.ones((512, 512), dtype=bool))
        mask_BxS2_if1 = jnp.where(jnp.ones((2, 1024), dtype=bool), 1, 0).astype(jnp.int32)
        return (x, ctx_1024, mask_BxS2_if1)
    x, ctx_1024, mask_BxS2_if1 = _rec_inputs()

    def _L0_attn_setup():
        import jax, jax.numpy as jnp
        import numpy as np
        H, DK, DV, D, K = (8, 128, 128, 256, 4)

        def _dconv(x, w, b):
            B, L, C = x.shape
            xp = jnp.pad(x, ((0, 0), (K - 1, 0), (0, 0)))
            acc = xp[:, 0:L, :] * w[:, 0]
            for j in range(1, K):
                acc = acc + xp[:, j:j + L, :] * w[:, j]
            return acc + b

        def _forward(x, Wq, Wk, Wv, Wa, ba, Wb, bb, Wg, Wo, cqw, cqb, ckw, ckb, cvw, cvb, ln_g, ln_b):
            B, L, _ = x.shape
            q = jax.nn.silu(_dconv(x @ Wq, cqw, cqb)).reshape(B, L, H, DK)
            k = jax.nn.silu(_dconv(x @ Wk, ckw, ckb)).reshape(B, L, H, DK) * DK ** (-0.5)
            v = jax.nn.silu(_dconv(x @ Wv, cvw, cvb)).reshape(B, L, H, DV)
            a = jax.nn.sigmoid(x @ Wa + ba).reshape(B, L, H, DV)
            beta = jax.nn.sigmoid(x @ Wb + bb)
            tm = lambda t: jnp.moveaxis(t, 1, 0)

            def step(S, ins):
                qt, kt, vt, at, bt = ins
                err = jnp.einsum('bhvk,bhk->bhv', S, kt) - vt
                Sn = at[..., None] * S - bt[..., None, None] * err[..., None] * kt[:, :, None, :]
                ot = jnp.einsum('bhvk,bhk->bhv', Sn, qt)
                return (Sn, ot)
            S0 = jnp.zeros((B, H, DV, DK), x.dtype)
            _, oT = jax.lax.scan(step, S0, (tm(q), tm(k), tm(v), tm(a), tm(beta)))
            o = jnp.moveaxis(oT, 0, 1)
            mu = o.mean(-1, keepdims=True)
            var = o.var(-1, keepdims=True)
            o = (o - mu) / jnp.sqrt(var + 1e-05) * ln_g + ln_b
            g = jax.nn.sigmoid(x @ Wg).reshape(B, L, H, DV)
            o = (o * g).reshape(B, L, H * DV)
            return o @ Wo
        key = jax.random.key(seed)
        ks = jax.random.split(key, 16)
        B, L = (4, 512)
        s = 0.02
        f32 = jnp.float32
        return {'x': jax.random.normal(ks[0], (B, L, D), f32), 'Wq': jax.random.normal(ks[1], (D, H * DK), f32) * s, 'Wk': jax.random.normal(ks[2], (D, H * DK), f32) * s, 'Wv': jax.random.normal(ks[3], (D, H * DV), f32) * s, 'Wa': jax.random.normal(ks[4], (D, H * DV), f32) * s, 'ba': jnp.zeros((H * DV,), f32), 'Wb': jax.random.normal(ks[5], (D, H), f32) * s, 'bb': jnp.zeros((H,), f32), 'Wg': jax.random.normal(ks[6], (D, H * DV), f32) * s, 'Wo': jax.random.normal(ks[7], (H * DV, D), f32) * s, 'cqw': jax.random.normal(ks[8], (H * DK, K), f32) * 0.2, 'cqb': jnp.zeros((H * DK,), f32), 'ckw': jax.random.normal(ks[9], (H * DK, K), f32) * 0.2, 'ckb': jnp.zeros((H * DK,), f32), 'cvw': jax.random.normal(ks[10], (H * DV, K), f32) * 0.2, 'cvb': jnp.zeros((H * DV,), f32), 'ln_g': jnp.ones((DV,), f32), 'ln_b': jnp.zeros((DV,), f32)}
    _L0_attn_all = _L0_attn_setup()
    _L0_attn_in = {k: v for k, v in _L0_attn_all.items() if k in ('Wq', 'Wk', 'Wv', 'Wa', 'ba', 'Wb', 'bb', 'Wg', 'Wo', 'cqw', 'cqb', 'ckw', 'ckb', 'cvw', 'cvb', 'ln_g', 'ln_b')}
    del _L0_attn_all

    def _L0_xattn_setup():
        import jax, jax.numpy as jnp
        import numpy as np
        D_MODEL = 256
        N_HEADS = 16
        B, S = (2, 512)
        key = jax.random.key(seed)
        ks = jax.random.split(key, 7)
        scale = 1.0 / np.sqrt(D_MODEL)
        return {'x_query': jax.random.normal(ks[0], (B, S, D_MODEL), dtype=jnp.float32), 'x_key': jax.random.normal(ks[1], (B, S, D_MODEL), dtype=jnp.float32), 'x_value': jax.random.normal(ks[2], (B, S, D_MODEL), dtype=jnp.float32), 'attention_mask': jnp.ones((B, S), dtype=jnp.int32), 'Wq': jax.random.normal(ks[3], (D_MODEL, D_MODEL), dtype=jnp.float32) * scale, 'Wk': jax.random.normal(ks[4], (D_MODEL, D_MODEL), dtype=jnp.float32) * scale, 'Wv': jax.random.normal(ks[5], (D_MODEL, D_MODEL), dtype=jnp.float32) * scale, 'Wo': jax.random.normal(ks[6], (D_MODEL, D_MODEL), dtype=jnp.float32) * scale}
    _L0_xattn_all = _L0_xattn_setup()
    _L0_xattn_in = {k: v for k, v in _L0_xattn_all.items() if k in ('Wq', 'Wk', 'Wv', 'Wo')}
    del _L0_xattn_all

    def _L0_ffn_setup():
        import jax, jax.numpy as jnp
        import numpy as np
        B, N, D = (4, 1024, 256)
        E, S, F = (16, 64, 512)
        DO = 256
        EPS = 1e-05

        def _layernorm(x, g, b):
            mu = jnp.mean(x, axis=-1, keepdims=True)
            var = jnp.mean(jnp.square(x - mu), axis=-1, keepdims=True)
            return (x - mu) * jax.lax.rsqrt(var + EPS) * g + b
        key = jax.random.key(seed)
        ks = jax.random.split(key, 8)
        d = {'x': jax.random.normal(ks[0], (B, N, D), dtype=jnp.float32), 'norm_g': jnp.ones((D,), jnp.float32), 'norm_b': jnp.zeros((D,), jnp.float32), 'slot_g': jnp.ones((D,), jnp.float32), 'slot_b': jnp.zeros((D,), jnp.float32), 'scale': jnp.ones((1,), jnp.float32), 'slot_embeds': jax.random.normal(ks[1], (E, S, D), jnp.float32) / np.sqrt(D), 'Wg': jax.random.normal(ks[2], (E, D, F), jnp.float32) * np.sqrt(2.0 / (D + F)), 'bg': jnp.zeros((E, F), jnp.float32), 'Wu': jax.random.normal(ks[3], (E, D, F), jnp.float32) * np.sqrt(2.0 / (D + F)), 'bu': jnp.zeros((E, F), jnp.float32), 'Wd': jax.random.normal(ks[4], (E, F, DO), jnp.float32) * np.sqrt(2.0 / (F + DO)), 'bd': jnp.zeros((E, DO), jnp.float32)}
        return d
    _L0_ffn_all = _L0_ffn_setup()
    _L0_ffn_in = {k: v for k, v in _L0_ffn_all.items() if k in ('norm_g', 'norm_b', 'slot_g', 'slot_b', 'scale', 'slot_embeds', 'Wg', 'bg', 'Wu', 'bu', 'Wd', 'bd')}
    del _L0_ffn_all
    return {'x': x, 'ctx_1024': ctx_1024, 'mask_BxS2_if1': mask_BxS2_if1, 'L0_attn_Wq': _L0_attn_in['Wq'], 'L0_attn_Wk': _L0_attn_in['Wk'], 'L0_attn_Wv': _L0_attn_in['Wv'], 'L0_attn_Wa': _L0_attn_in['Wa'], 'L0_attn_ba': _L0_attn_in['ba'], 'L0_attn_Wb': _L0_attn_in['Wb'], 'L0_attn_bb': _L0_attn_in['bb'], 'L0_attn_Wg': _L0_attn_in['Wg'], 'L0_attn_Wo': _L0_attn_in['Wo'], 'L0_attn_cqw': _L0_attn_in['cqw'], 'L0_attn_cqb': _L0_attn_in['cqb'], 'L0_attn_ckw': _L0_attn_in['ckw'], 'L0_attn_ckb': _L0_attn_in['ckb'], 'L0_attn_cvw': _L0_attn_in['cvw'], 'L0_attn_cvb': _L0_attn_in['cvb'], 'L0_attn_ln_g': _L0_attn_in['ln_g'], 'L0_attn_ln_b': _L0_attn_in['ln_b'], 'L0_xattn_Wq': _L0_xattn_in['Wq'], 'L0_xattn_Wk': _L0_xattn_in['Wk'], 'L0_xattn_Wv': _L0_xattn_in['Wv'], 'L0_xattn_Wo': _L0_xattn_in['Wo'], 'L0_ffn_norm_g': _L0_ffn_in['norm_g'], 'L0_ffn_norm_b': _L0_ffn_in['norm_b'], 'L0_ffn_slot_g': _L0_ffn_in['slot_g'], 'L0_ffn_slot_b': _L0_ffn_in['slot_b'], 'L0_ffn_scale': _L0_ffn_in['scale'], 'L0_ffn_slot_embeds': _L0_ffn_in['slot_embeds'], 'L0_ffn_Wg': _L0_ffn_in['Wg'], 'L0_ffn_bg': _L0_ffn_in['bg'], 'L0_ffn_Wu': _L0_ffn_in['Wu'], 'L0_ffn_bu': _L0_ffn_in['bu'], 'L0_ffn_Wd': _L0_ffn_in['Wd'], 'L0_ffn_bd': _L0_ffn_in['bd']}

def reference(x, ctx_1024, mask_BxS2_if1, L0_attn_Wq, L0_attn_Wk, L0_attn_Wv, L0_attn_Wa, L0_attn_ba, L0_attn_Wb, L0_attn_bb, L0_attn_Wg, L0_attn_Wo, L0_attn_cqw, L0_attn_cqb, L0_attn_ckw, L0_attn_ckb, L0_attn_cvw, L0_attn_cvb, L0_attn_ln_g, L0_attn_ln_b, L0_xattn_Wq, L0_xattn_Wk, L0_xattn_Wv, L0_xattn_Wo, L0_ffn_norm_g, L0_ffn_norm_b, L0_ffn_slot_g, L0_ffn_slot_b, L0_ffn_scale, L0_ffn_slot_embeds, L0_ffn_Wg, L0_ffn_bg, L0_ffn_Wu, L0_ffn_bu, L0_ffn_Wd, L0_ffn_bd):
    import jax
    import jax.numpy as jnp

    def _L0_attn_ref(x, Wq, Wk, Wv, Wa, ba, Wb, bb, Wg, Wo, cqw, cqb, ckw, ckb, cvw, cvb, ln_g, ln_b):
        import jax, jax.numpy as jnp
        import numpy as np
        H, DK, DV, D, K = (8, 128, 128, 256, 4)

        def _dconv(x, w, b):
            B, L, C = x.shape
            xp = jnp.pad(x, ((0, 0), (K - 1, 0), (0, 0)))
            acc = xp[:, 0:L, :] * w[:, 0]
            for j in range(1, K):
                acc = acc + xp[:, j:j + L, :] * w[:, j]
            return acc + b

        def _forward(x, Wq, Wk, Wv, Wa, ba, Wb, bb, Wg, Wo, cqw, cqb, ckw, ckb, cvw, cvb, ln_g, ln_b):
            B, L, _ = x.shape
            q = jax.nn.silu(_dconv(x @ Wq, cqw, cqb)).reshape(B, L, H, DK)
            k = jax.nn.silu(_dconv(x @ Wk, ckw, ckb)).reshape(B, L, H, DK) * DK ** (-0.5)
            v = jax.nn.silu(_dconv(x @ Wv, cvw, cvb)).reshape(B, L, H, DV)
            a = jax.nn.sigmoid(x @ Wa + ba).reshape(B, L, H, DV)
            beta = jax.nn.sigmoid(x @ Wb + bb)
            tm = lambda t: jnp.moveaxis(t, 1, 0)

            def step(S, ins):
                qt, kt, vt, at, bt = ins
                err = jnp.einsum('bhvk,bhk->bhv', S, kt) - vt
                Sn = at[..., None] * S - bt[..., None, None] * err[..., None] * kt[:, :, None, :]
                ot = jnp.einsum('bhvk,bhk->bhv', Sn, qt)
                return (Sn, ot)
            S0 = jnp.zeros((B, H, DV, DK), x.dtype)
            _, oT = jax.lax.scan(step, S0, (tm(q), tm(k), tm(v), tm(a), tm(beta)))
            o = jnp.moveaxis(oT, 0, 1)
            mu = o.mean(-1, keepdims=True)
            var = o.var(-1, keepdims=True)
            o = (o - mu) / jnp.sqrt(var + 1e-05) * ln_g + ln_b
            g = jax.nn.sigmoid(x @ Wg).reshape(B, L, H, DV)
            o = (o * g).reshape(B, L, H * DV)
            return o @ Wo
        return _forward(x, Wq, Wk, Wv, Wa, ba, Wb, bb, Wg, Wo, cqw, cqb, ckw, ckb, cvw, cvb, ln_g, ln_b)

    def _L0_xattn_ref(x_query, x_key, x_value, attention_mask, Wq, Wk, Wv, Wo):
        import jax, jax.numpy as jnp
        import numpy as np
        D_MODEL = 256
        N_HEADS = 16
        B, S = (2, 512)
        b, sq, d = x_query.shape
        sk = x_key.shape[1]
        h = N_HEADS
        dk = d // h
        Q = (x_query @ Wq.T).reshape(b, sq, h, dk).transpose(0, 2, 1, 3)
        K = (x_key @ Wk.T).reshape(b, sk, h, dk).transpose(0, 2, 1, 3)
        V = (x_value @ Wv.T).reshape(b, sk, h, dk).transpose(0, 2, 1, 3)
        scores = jnp.einsum('bhqd,bhkd->bhqk', Q, K) / jnp.sqrt(jnp.asarray(dk, (scores_dtype := Q.dtype)))
        causal = jnp.tril(jnp.ones((sq, sk), dtype=bool))
        scores = jnp.where(causal[None, None, :, :], scores, -jnp.inf)
        pad = (attention_mask != 0)[:, None, None, :]
        scores = jnp.where(pad, scores, -jnp.inf)
        probs = jax.nn.softmax(scores, axis=-1)
        out = jnp.einsum('bhqk,bhkd->bhqd', probs, V)
        out = out.transpose(0, 2, 1, 3).reshape(b, sq, d)
        return out @ Wo.T

    def _L0_ffn_ref(x, norm_g, norm_b, slot_g, slot_b, scale, slot_embeds, Wg, bg, Wu, bu, Wd, bd):
        import jax, jax.numpy as jnp
        import numpy as np
        B, N, D = (4, 1024, 256)
        E, S, F = (16, 64, 512)
        DO = 256
        EPS = 1e-05

        def _layernorm(x, g, b):
            mu = jnp.mean(x, axis=-1, keepdims=True)
            var = jnp.mean(jnp.square(x - mu), axis=-1, keepdims=True)
            return (x - mu) * jax.lax.rsqrt(var + EPS) * g + b
        x = _layernorm(x, norm_g, norm_b)
        se = _layernorm(slot_embeds, slot_g, slot_b) * scale
        logits = jnp.einsum('bnd,esd->bnes', x, se)
        dispatch = jax.nn.softmax(logits, axis=1)
        combine = jax.nn.softmax(logits.reshape(x.shape[0], x.shape[1], -1), axis=-1)
        slots = jnp.einsum('bnd,bnes->besd', x, dispatch)
        gate = jax.nn.gelu(jnp.einsum('besd,edf->besf', slots, Wg) + bg[None, :, None, :], approximate=False)
        up = jnp.einsum('besd,edf->besf', slots, Wu) + bu[None, :, None, :]
        eout = jnp.einsum('besf,efo->beso', gate * up, Wd) + bd[None, :, None, :]
        eout = eout.reshape(eout.shape[0], -1, eout.shape[-1])
        return jnp.einsum('bns,bso->bno', combine, eout)
    x = x + _L0_attn_ref(_layernorm(x, axis=-1), L0_attn_Wq, L0_attn_Wk, L0_attn_Wv, L0_attn_Wa, L0_attn_ba, L0_attn_Wb, L0_attn_bb, L0_attn_Wg, L0_attn_Wo, L0_attn_cqw, L0_attn_cqb, L0_attn_ckw, L0_attn_ckb, L0_attn_cvw, L0_attn_cvb, L0_attn_ln_g, L0_attn_ln_b)
    x = x + _L0_xattn_ref(_layernorm(x, axis=-1), ctx_1024, ctx_1024, mask_BxS2_if1, L0_xattn_Wq, L0_xattn_Wk, L0_xattn_Wv, L0_xattn_Wo)
    x = x + _L0_ffn_ref(_layernorm(x, axis=-1), L0_ffn_norm_g, L0_ffn_norm_b, L0_ffn_slot_g, L0_ffn_slot_b, L0_ffn_scale, L0_ffn_slot_embeds, L0_ffn_Wg, L0_ffn_bg, L0_ffn_Wu, L0_ffn_bu, L0_ffn_Wd, L0_ffn_bd)
    return x

_drawn_inputs = setup_inputs


def setup_inputs(seed=0):
    import zlib

    import numpy as np

    out = dict(_drawn_inputs(seed))
    spreads = {'L0_attn_ba': (0.0, 0.8),
     'L0_attn_bb': (0.0, 0.8),
     'L0_attn_cqb': (0.0, 0.385),
     'L0_attn_ckb': (0.0, 0.33),
     'L0_attn_cvb': (0.0, 0.318),
     'L0_attn_ln_g': (1.0, 0.6),
     'L0_attn_ln_b': (0.0, 0.1),
     'L0_ffn_norm_g': (1.0, 0.2),
     'L0_ffn_norm_b': (0.0, 0.1),
     'L0_ffn_slot_g': (1.0, 0.2),
     'L0_ffn_slot_b': (0.0, 0.1),
     'L0_ffn_bg': (0.0, 0.1),
     'L0_ffn_bu': (0.0, 0.1),
     'L0_ffn_bd': (0.0, 0.1)}
    factors = {'L0_attn_Wa': 8.0, 'L0_attn_Wb': 8.0, 'L0_attn_Wg': 7.46}
    for name, (base, spread) in spreads.items():
        noise = np.random.default_rng([zlib.crc32(name.encode()), seed]).standard_normal(out[name].shape)
        drawn = base * np.exp(spread * noise) if base else spread * noise
        out[name] = jnp.asarray(drawn.astype(out[name].dtype))
    for name, factor in factors.items():
        out[name] = (out[name] * factor).astype(out[name].dtype)
    return out
```

```python
from contextlib import ExitStack

import concourse.bass as bass
from concourse import mybir

F32 = mybir.dt.float32
BF16 = mybir.dt.bfloat16
I32 = mybir.dt.int32
ALU = mybir.AluOpType
ACT = mybir.ActivationFunctionType
AX_X = mybir.AxisListType.X

P = 128
B, L, D = 2, 512, 256
H = 8
NP = B * H
NT = B * L // P
KT = D // P
C = 8
NB = 4
CH = C * NB
NCH = L // CH
XH = 16
XD = D // XH
XG = XH // 4
QT_N = L // P
E, SL, F = 16, 64, 512
ES = E * SL
ET = ES // P
FT = F // P
MASKED = -1e30
EPS = 1e-5
S2 = 1.0 / P

OFF = [0]
for _s in range(C):
    OFF.append(OFF[-1] + NP * (C - _s))
TRI = OFF[C]


def wait(eng, sem, value):
    if isinstance(value, int) and value <= 0:
        return
    eng.wait_ge(sem, value)


class Steps:

    def __init__(self, eng, sem):
        self.eng, self.sem, self.start, self.k = eng, sem, 0, 0

    def at(self, start):
        self.start, self.k = start, 0

    def did(self, ins):
        ins.then_inc(self.sem, 1)
        self.k += 1

    def settle(self):
        wait(self.eng, self.sem, self.start + self.k)

    def link(self, ins):
        self.did(ins)
        self.settle()

    def total(self):
        return self.start + self.k


def decoder_layer(nc, x, w_qkva, conv_pack, wb, bb, w_gate, w_o, ln_gb, ctx_keys, mask_rows, mask_cols, rows_k, rows_q,
                  xa_q, xa_k, xa_v, xa_o, slots, slot_gb, norm_gb, scale, w_gate_up, w_down, b_gu, b_down, out):
    ctx = ExitStack()
    with ctx:
        def sb(name, shape, dt=F32):
            return ctx.enter_context(nc.sbuf_tensor(name, shape, dt))

        def sem(name):
            return ctx.enter_context(nc.semaphore(name))

        PS = ctx.enter_context(nc.psum_tensor("PS", [P, 8, 512], F32))
        PSF = PS[:, :, :].rearrange("p b c -> p (b c)")

        ident = sb("ident", [P, P])
        ones = sb("ones", [P, P])
        avg = sb("avg", [P, P])
        eps_col = sb("eps_col", [P, 2])
        xT = sb("xT", [P, KT, B * L])
        stats = sb("stats", [P, NT, 6])
        mv = sb("mv", [P, NT, 2])
        std = sb("std", [P, NT])
        rstd = sb("rstd", [P, NT])
        lngb = sb("lngb", [P, 2])
        bb_sb = sb("bb_sb", [H, 1])
        KQ = sb("KQ", [P, 2, NP, L + 1])
        VO = sb("VO", [P, NP, L])
        A = sb("A", [P, NP, L])
        betaT = sb("betaT", [H, B, L])
        beta_m = sb("beta_m", [H, B, H, CH])
        own = sb("own", [C * NP, NP])

        SCR = 15500
        scratch = sb("scratch", [P, SCR])
        at = [0]

        def cut(n):
            at[0] += n
            assert at[0] <= SCR, at[0]
            return scratch[:, at[0] - n:at[0]]

        xt = cut(NT * D).rearrange("p (n d) -> p n d", n=NT)
        xn = cut(2 * D).rearrange("p (s d) -> p s d", s=2)
        wh = cut(2 * 4 * KT * P).rearrange("p (s q k c) -> p s q k c", s=2, q=4, k=KT)
        cw = cut(2 * 16).rearrange("p (s c) -> p s c", s=2)
        wb_sb = cut(KT * H).rearrange("p (k h) -> p k h", k=KT)
        acc = cut(4 * L).rearrange("p (s t) -> p s t", s=4)
        at[0] = 0
        S = cut(NP * P).rearrange("p (n k) -> p n k", n=NP)
        ST = cut(NP * P).rearrange("p (n k) -> p n k", n=NP)
        KBo = cut(NP * CH).rearrange("p (n s) -> p n s", n=NP)
        KBb = cut(NP * CH).rearrange("p (i n s) -> p i n s", i=NB, n=NP)
        X = [cut(2 * TRI).rearrange("p (y c) -> p y c", y=2) for _ in range(2)]
        N = cut(2 * TRI).rearrange("p (y c) -> p y c", y=2)
        Dt = [cut(TRI) for _ in range(2)]
        Pre = [cut(NP * (C + 1)).rearrange("p (n t) -> p n t", n=NP) for _ in range(2)]
        Suf = [cut(NP * C).rearrange("p (n s) -> p n s", n=NP) for _ in range(2)]
        AB = cut(NB * NP).rearrange("p (i n) -> p i n", i=NB)
        SB = cut((NB + 1) * NP).rearrange("p (i n) -> p i n", i=NB + 1)
        R = [[cut(H * 2 * (C + 1)).rearrange("p (n y t) -> p n y t", n=H, y=2) for _ in range(B)]
             for _ in range(2)]
        Pr = [cut(H * 2 * C) for _ in range(B)]
        Wst = cut(NP * CH).rearrange("p (i n s) -> p i n s", i=NB, n=NP)
        Wsc = cut(NP * CH).rearrange("p (n s) -> p n s", n=NP)
        WTs = cut(P)
        WTo = cut(4 * P).rearrange("p (g v) -> p g v", g=4)
        KBT = cut(4 * P).rearrange("p (g v) -> p g v", g=4)
        GMN = H * 2 * (CH - C + 1)
        GM = cut(GMN)
        Z = [cut(H * 2 * (CH + 1)).rearrange("p (n y t) -> p n y t", n=H, y=2) for _ in range(B)]
        G = KQ[:, 0, :, 0:L]
        at[0] = 0
        xt2 = cut(NT * D).rearrange("p (n d) -> p n d", n=NT)
        wg_sb = cut(2 * KT * P).rearrange("p (s k c) -> p s k c", s=2, k=KT)
        wo_sb = cut(H * D).rearrange("p (h n) -> p h n", h=H)
        oc = cut(2 * L).rearrange("p (s t) -> p s t", s=2)
        sq = cut(2 * L).rearrange("p (s t) -> p s t", s=2)
        sd = cut(2 * L).rearrange("p (s t) -> p s t", s=2)

        identb = sb("identb", [P, P], BF16)
        late = sb("late", [P, P], BF16)
        early = sb("early", [P, P], BF16)
        ones_row = beta_m[0:1, :, :, :].rearrange("r b h s -> r (b h s)")
        mcol_i = sb("mcol_i", [P, NT], I32)
        mcol = sb("mcol", [P, NT])
        xsum = sb("xsum", [P, 2, 16])
        Af, Vf = (t[:, :, :].rearrange("p n t -> p (n t)") for t in (A, VO))
        Kf = KQ[:, :, :, :].rearrange("p y n t -> p (y n t)")
        rowsk = Af[0:2, 7680:7808]
        rowsq = Af[0:1, 7808:7936]
        mrow_i = Kf[0:1, 14464:15488].bitcast(I32)
        ctxt = Af[:, 0:2048].rearrange("p (n d) -> p n d", n=NT)
        xwq = Af[:, 2048:3072].rearrange("p (k c) -> p k c", k=KT)
        xwk = Af[:, 3072:4096].rearrange("p (k c) -> p k c", k=KT)
        xwv = Af[:, 4096:4608].rearrange("p (k c) -> p k c", k=KT)
        ctxT = Af[:, 5120:7168].rearrange("p (k t) -> p k t", k=KT)
        attT = ctxT
        xwo = Af[:, 7168:7680].rearrange("p (k c) -> p k c", k=KT)
        xKT = Kf[:, 0:4096].rearrange("p (g t) -> p g t", g=XG)
        xQT = Kf[:, 4096:8192].rearrange("p (g t) -> p g t", g=XG)
        xQ2 = Kf[:, 8192:12288].rearrange("p (g t) -> p g t", g=XG)
        xV = Kf[:, 12288:12288 + NT * XH * 17].rearrange("p (n h c) -> p n h c", n=NT, h=XH)
        xMx = scratch[:, 7680:11776].rearrange("p (n g c) -> p n g c", n=NT, g=XG)
        att = scratch[:, 11776:13824].rearrange("p (n d) -> p n d", n=NT)
        mrow = scratch[0:2, 13824:14848]
        xn2 = scratch[:, 14848:15360].rearrange("p (s d) -> p s d", s=2)
        POFF = [0, 4 * 512, 4 * (512 + 384), 4 * (512 + 384 + 256), 4 * 1280]
        PT = [Vf[:, 0:POFF[4]], Af[:, 0:POFF[4]]]

        def probs(buf, j):
            return PT[buf][:, POFF[j]:POFF[j + 1]].rearrange("p (h t) -> p h t", h=4)

        se = Af[:, 0:2048].rearrange("p (n d) -> p n d", n=ET)
        xf = scratch[:, 2048:4096].rearrange("p (n d) -> p n d", n=NT)
        seT = scratch[:, 4096:6144].rearrange("p (k s) -> p k s", k=KT)
        we = scratch[:, 6144:12288].rearrange("p (s w) -> p s w", s=2)
        wgu = [we[:, i, 0:2048].rearrange("p (y k f) -> p y k f", y=2, k=KT) for i in range(2)]
        wdn = [we[:, i, 2048:3072].rearrange("p (f d) -> p f d", f=FT) for i in range(2)]
        hT = scratch[:, 12288:13312].rearrange("p (s f c) -> p s f c", s=2, f=FT)
        gel = scratch[:, 13312:14336].rearrange("p (s f c) -> p s f c", s=2, f=FT)
        bdn = scratch[:, 14336:14848].rearrange("p (s d) -> p s d", s=2)
        bgu = sb("bgu", [P, 2, 2 * FT])
        gb = Af[:, 2048:3072].rearrange("p (y d) -> p y d", y=4)
        scl = sb("scl", [P, 1])
        LG = Kf[:, 0:8192].rearrange("p (e t) -> p e t", e=ET)
        FD = Kf[:, 8192:16384].rearrange("p (n s) -> p n s", n=NT)
        FS = Vf.rearrange("p (e t) -> p e t", e=ET)
        EC = Af.rearrange("p (e t) -> p e t", e=ET)
        E1 = we[:, :, 0:1024]
        slT = Kf[:, 0:4096].rearrange("p (k e c) -> p k e c", k=KT, e=E)
        eo = Vf[:, 0:4096].rearrange("p (e b d) -> p e b d", e=ET, b=B)
        mE = sb("mE", [P, ET, B])
        dE = sb("dE", [P, ET, B])
        mN = sb("mN", [P, NT])
        dN = sb("dN", [P, NT])

        s_x = sem("s_x")
        s_small = sem("s_small")
        s_cst = sem("s_cst")
        s_pool = sem("s_pool")
        s_dve = sem("s_dve")
        s_g0, s_g1 = sem("s_g0"), sem("s_g1")
        s_mv = sem("s_mv")
        s_std = sem("s_std")
        s_xn = sem("s_xn")
        s_xtp = sem("s_xtp")
        s_xT = sem("s_xT")
        s_wh = [sem("s_wh0"), sem("s_wh1")]
        s_bp = sem("s_bp")
        s_bs = sem("s_bs")
        s_beta = sem("s_beta")
        s_pa = sem("s_pa")
        s_sa = sem("s_sa")
        s_pq = sem("s_pq")
        s_pre = sem("s_pre")
        s_conv = sem("s_conv")
        s_silu = sem("s_silu")
        s_init = sem("s_init")
        p_bm = sem("p_bm")
        p_x = sem("p_x")
        p_d = sem("p_d")
        p_ab = sem("p_ab")
        e_bb = sem("e_bb")
        e_g = sem("e_g")
        e_gr = sem("e_gr")
        e_kt = sem("e_kt")
        e_wt = sem("e_wt")
        e_ap = sem("e_ap")
        e_wo = sem("e_wo")
        e_dl = sem("e_dl")
        e_st = sem("e_st")
        e_z = sem("e_z")
        v_kb = sem("v_kb")
        v_n = sem("v_n")
        v_gm = sem("v_gm")
        v_r = sem("v_r")
        v_w = sem("v_w")
        v_za = sem("v_za")
        v_wo = sem("v_wo")
        v_s = sem("v_s")
        a_kt = sem("a_kt")
        a_kb = sem("a_kb")
        a_wt = sem("a_wt")
        a_o = sem("a_o")
        a_sa = sem("a_sa")
        a_wo = sem("a_wo")
        a_st = sem("a_st")
        a_z = sem("a_z")
        g_ld = [sem("g_ld0"), sem("g_ld1")]
        g_p = sem("g_p")
        g_s = sem("g_s")
        g_wo = sem("g_wo")
        g_x = sem("g_x")
        o_m = sem("o_m")
        o_c = sem("o_c")
        o_q = sem("o_q")
        o_v = sem("o_v")
        o_d = sem("o_d")
        o_y = sem("o_y")
        o_a = sem("o_a")
        o_g = sem("o_g")
        o_p = sem("o_p")
        o_x = sem("o_x")
        s_out = sem("s_out")
        x_ld = sem("x_ld")
        x_cst = sem("x_cst")
        x_mv = sem("x_mv")
        x_sd = sem("x_sd")
        x_xn = sem("x_xn")
        x_tp = sem("x_tp")
        x_xT = sem("x_xT")
        x_mk = sem("x_mk")
        x_ct = sem("x_ct")
        x_cT = sem("x_cT")
        x_kp = sem("x_kp")
        x_k = sem("x_k")
        x_vp = sem("x_vp")
        x_v = sem("x_v")
        x_qp = sem("x_qp")
        x_q = sem("x_q")
        x_s = sem("x_s")
        x_mx = sem("x_mx")
        x_mt = sem("x_mt")
        x_q2 = sem("x_q2")
        x_st = sem("x_st")
        x_e = sem("x_e")
        x_pv = sem("x_pv")
        x_at = sem("x_at")
        x_tt = sem("x_tt")
        x_aT = sem("x_aT")
        x_op = sem("x_op")
        x_x = sem("x_x")
        f_ld = sem("f_ld")
        f_y = sem("f_y")
        f_se = sem("f_se")
        f_st = sem("f_st")
        f_sT = sem("f_sT")
        f_lg = sem("f_lg")
        f_lk = sem("f_lk")
        f_mE = sem("f_mE")
        f_fs = sem("f_fs")
        f_fn = sem("f_fn")
        f_ft = sem("f_ft")
        f_fk = sem("f_fk")
        f_lt = sem("f_lt")
        f_mN = sem("f_mN")
        f_e1 = sem("f_e1")
        f_eh = sem("f_eh")
        f_dn = sem("f_dn")
        f_ek = sem("f_ek")
        f_sp = sem("f_sp")
        f_sk = sem("f_sk")
        w_ld = [sem("w_ld0"), sem("w_ld1")]
        w_gu = sem("w_gu")
        w_ge = sem("w_ge")
        w_h = sem("w_h")
        w_dn = sem("w_dn")
        w_eo = sem("w_eo")
        w_cb = sem("w_cb")
        w_x = sem("w_x")

        x_tiles = x.rearrange("b (i p) d -> p (b i) d", p=P)
        out_tiles = out.rearrange("b (i p) d -> p (b i) d", p=P)
        GRAMS = 2 * (NB - 1)

        block = ctx.enter_context(nc.Block())

        @block.sync
        def _(sp):
            sp.dma_start(xt, x_tiles).then_inc(s_x, 16)
            sp.dma_start(wb_sb, wb).then_inc(s_small, 16)
            sp.dma_start(bb_sb[:, :], bb).then_inc(s_small, 16)
            sp.dma_start(lngb[:, :], ln_gb).then_inc(s_small, 16)

            def head_weights(h, slot):
                wait(sp, s_silu, (h - 1) * 6)
                sp.dma_start(wh[:, slot], w_qkva[h]).then_inc(s_wh[slot], 16)
                sp.dma_start(cw[:, slot], conv_pack[h]).then_inc(s_wh[slot], 16)

            head_weights(0, 0)
            head_weights(1, 1)
            with sp.Fori(1, H // 2) as i:
                for slot in range(2):
                    sp.wait_ge(s_silu, 12 * i + (slot - 1) * 6)
                    sp.dma_start(wh[:, slot], w_qkva[bass.ds(2 * i + slot, 1)].rearrange("a p q k c -> p (a q) k c")
                                 ).then_inc(s_wh[slot], 16)
                    sp.dma_start(cw[:, slot], conv_pack[bass.ds(2 * i + slot, 1)].rearrange("a p c -> p (a c)")
                                 ).then_inc(s_wh[slot], 16)
            sp.wait_ge(a_o, 2 * NCH * NB)
            sp.wait_ge(v_w, 2 * NCH * NB)
            sp.dma_start(xt2, x_tiles).then_inc(g_x, 16)
            sp.dma_start(wo_sb, w_o).then_inc(g_wo, 16)
            for h in range(H):
                wait(sp, g_p, 2 * (h - 1))
                sp.dma_start(wg_sb[:, h % 2], w_gate[h]).then_inc(g_ld[h % 2], 16)
            for dst, src in ((ctxt, ctx_keys), (xwk, xa_k), (xwv, xa_v), (xwq, xa_q), (xwo, xa_o), (rowsk, rows_k),
                             (rowsq, rows_q), (mrow_i, mask_rows), (mcol_i[:, :], mask_cols)):
                sp.dma_start(dst, src).then_inc(x_ld, 16)
            sp.wait_ge(x_pv, 2 * XG)
            sp.dma_start(se, slots).then_inc(f_ld, 16)
            sp.dma_start(gb[:, 0:2], norm_gb.partition_broadcast(P)).then_inc(f_ld, 16)
            sp.dma_start(gb[:, 2:4], slot_gb.partition_broadcast(P)).then_inc(f_ld, 16)
            sp.dma_start(scl[:, :], scale.partition_broadcast(P)).then_inc(f_ld, 16)

            def expert(e, slot):
                sp.dma_start(wgu[slot], w_gate_up[bass.ds(e, 1)].rearrange("a p y k f -> p (a y) k f")).then_inc(w_ld[slot], 16)
                sp.dma_start(wdn[slot], w_down[bass.ds(e, 1)].rearrange("a p f d -> p (a f) d")).then_inc(w_ld[slot], 16)
                sp.dma_start(bgu[:, slot], b_gu[bass.ds(e, 1)].rearrange("a p c -> p (a c)")).then_inc(w_ld[slot], 16)
                sp.dma_start(bdn[:, slot], b_down[bass.ds(e, 1), :].rearrange("a d -> (a d)").partition_broadcast(P)
                             ).then_inc(w_ld[slot], 16)

            sp.wait_ge(f_eh, 2 * NT)
            sp.wait_ge(x_x, NT)
            expert(0, 0)
            expert(1, 1)
            with sp.Fori(1, E // 2) as i:
                for slot in range(2):
                    sp.wait_ge(w_eo, 4 * i + 2 * (slot - 1))
                    expert(2 * i + slot, slot)
            sp.wait_ge(w_x, NT)
            sp.dma_start(out_tiles, xt2).then_inc(s_out, 16)
            sp.wait_ge(s_out, 16)

        @block.gpsimd
        def _(pool):
            me = Steps(pool, s_pool)
            nc.gpsimd.memset(ones[:, :], 1.0).then_inc(s_cst, 1)
            nc.gpsimd.memset(avg[:, :], 1.0 / P).then_inc(s_cst, 1)
            nc.gpsimd.memset(eps_col[:, 0:1], EPS).then_inc(s_cst, 1)
            nc.gpsimd.memset(eps_col[:, 1:2], EPS * S2).then_inc(s_cst, 1)
            me.did(nc.gpsimd.memset(ident[:, :], 0.0))
            me.did(nc.gpsimd.memset(own[:, :], -1.0))
            me.settle()
            nc.gpsimd.affine_select(out=ident[:, :], in_=ident[:, :], compare_op=ALU.not_equal, fill=1.0,
                                    base=0, pattern=[[-1, P]], channel_multiplier=1).then_inc(s_cst, 1)
            me.link(nc.gpsimd.affine_select(out=own[:, :], in_=own[:, :], compare_op=ALU.is_ge, fill=0.0,
                                            base=0, pattern=[[-C, NP]], channel_multiplier=1))
            nc.gpsimd.affine_select(out=own[:, :], in_=own[:, :], compare_op=ALU.is_ge, fill=0.0,
                                    base=C - 1, pattern=[[C, NP]], channel_multiplier=-1).then_inc(s_cst, 1)
            nc.gpsimd.memset(KQ[:, 0, :, L:L + 1], 0.0).then_inc(s_cst, 1)
            nc.gpsimd.memset(KQ[:, 1, :, 0:1], 0.0).then_inc(s_cst, 1)
            me.did(nc.gpsimd.memset(late[:, :], 0.0))
            me.did(nc.gpsimd.memset(early[:, :], 0.0))
            pool.wait_ge(s_cst, 5)
            nc.gpsimd.tensor_copy(identb[:, :], ident[:, :]).then_inc(x_cst, 1)
            me.settle()
            nc.gpsimd.affine_select(out=late[:, :], in_=late[:, :], compare_op=ALU.is_ge, fill=MASKED,
                                    base=0, pattern=[[-1, P]], channel_multiplier=1).then_inc(x_cst, 1)
            nc.gpsimd.affine_select(out=early[:, :], in_=early[:, :], compare_op=ALU.is_ge, fill=MASKED,
                                    base=0, pattern=[[1, P]], channel_multiplier=-1).then_inc(x_cst, 1)
            pool.wait_ge(s_silu, 6 * H)
            pool.wait_ge(s_sa, 2 * H)
            pool.wait_ge(s_bp, 1)
            nc.gpsimd.memset(S, 0.0).then_inc(s_init, 1)
            nc.gpsimd.memset(ST, 0.0).then_inc(s_init, 1)
            me.did(nc.gpsimd.memset(SB, 1.0))
            for y in range(2):
                me.did(nc.gpsimd.memset(Dt[y], 1.0))
                me.did(nc.gpsimd.memset(Pre[y], 1.0))
                me.did(nc.gpsimd.memset(Suf[y], 1.0))
            me.settle()
            pool.wait_ge(s_beta, 1)

            def spread_beta(o):
                wait(pool, e_bb, o)
                for b in range(B):
                    ins = nc.gpsimd.tensor_tensor(
                        out=beta_m[:, b], in0=betaT[:, b:b + 1, bass.ds(o * CH, CH)].to_broadcast([H, H, CH]),
                        in1=ident[0:H, 0:H].unsqueeze(2).to_broadcast([H, H, CH]), op=ALU.mult)
                ins.then_inc(p_bm, 1)

            def prep(o, i):
                m, t0, y = o * NB + i, o * CH + i * C, i % 2

                def col(s):
                    return Dt[y][:, OFF[s]:OFF[s + 1]].rearrange("p (n t) -> p n t", n=NP)

                def a(s, n):
                    return A[:, :, bass.ds(t0 + s, 1)].to_broadcast([P, NP, n])

                wait(pool, v_kb, o + 1)
                wait(pool, e_g, m - 1)
                wait(pool, v_n, m - 1)
                wait(pool, v_w, 2 * (m - 1))
                wait(pool, v_r, 2 * (m - 1))
                if i >= 2:
                    wait(pool, v_za, o * GRAMS + 2 * (i - 1))
                else:
                    wait(pool, v_za, o * GRAMS)
                for s in range(C - 1, -1, -1):
                    if s < C - 1:
                        me.did(nc.gpsimd.tensor_tensor(out=col(s)[:, :, 1:C - s], in0=col(s + 1),
                                                       in1=a(s + 1, C - 1 - s), op=ALU.mult))
                        me.did(nc.gpsimd.tensor_tensor(out=Suf[y][:, :, s:s + 1], in0=Suf[y][:, :, s + 1:s + 2],
                                                       in1=a(s + 1, 1), op=ALU.mult))
                    n = C - s
                    for q in range(2):
                        ins = nc.gpsimd.tensor_tensor(
                            out=X[y][:, q, OFF[s]:OFF[s + 1]].rearrange("p (n t) -> p n t", n=NP),
                            in0=KQ[:, q, :, bass.ds(t0 + 1 + s, n)],
                            in1=KBo[:, :, i * C + s:i * C + s + 1].to_broadcast([P, NP, n]), op=ALU.mult)
                    me.settle()
                ins.then_inc(p_x, 1)
                me.did(nc.gpsimd.tensor_tensor(out=AB[:, i, :].unsqueeze(2), in0=col(0)[:, :, C - 1:C], in1=a(0, 1),
                                               op=ALU.mult))
                nc.gpsimd.tensor_tensor(out=Pre[y][:, :, 1:C + 1], in0=col(0), in1=a(0, C),
                                        op=ALU.mult).then_inc(p_d, 1)
                if i == NB - 1:
                    me.settle()
                    wait(pool, v_wo, o)
                    wait(pool, a_sa, o)
                    for j in range(NB - 1, 0, -1):
                        me.link(nc.gpsimd.tensor_tensor(out=SB[:, j], in0=AB[:, j], in1=SB[:, j + 1] if j < NB - 1
                                                        else SB[:, NB], op=ALU.mult))
                    nc.gpsimd.tensor_tensor(out=SB[:, 0], in0=AB[:, 0], in1=SB[:, 1], op=ALU.mult).then_inc(p_ab, 1)

            def chunk(o, last=False):
                for i in range(1, NB):
                    prep(o, i)
                if not last:
                    spread_beta(o + 1)
                    prep(o + 1, 0)

            spread_beta(0)
            prep(0, 0)
            first = me.total()
            me.at(first)
            chunk(0)
            per = me.k
            second = me.total()
            with pool.Fori(1, NCH - 1) as o:
                me.at(second + (o - 1) * per)
                chunk(o)
                assert me.k == per
            me.at(second + (NCH - 2) * per)
            chunk(NCH - 1, last=True)
            pool.wait_ge(p_ab, NCH)
            pool.wait_ge(a_o, 2 * NCH * NB)
            pool.wait_ge(v_w, 2 * NCH * NB)
            nc.gpsimd.memset(xMx, 0.0).then_inc(x_cst, 1)
            nc.gpsimd.memset(mrow, 1.0).then_inc(x_cst, 1)
            nc.gpsimd.memset(ones_row, 1.0).then_inc(x_cst, 1)

        @block.scalar
        def _(act):
            act.wait_ge(s_cst, 8)
            act.wait_ge(s_mv, NT)
            nc.scalar.activation(std[:, :], mv[:, :, 1], ACT.Sqrt, bias=eps_col[:, 0:1]).then_inc(s_std, 1)
            act.wait_ge(s_small, 48)
            act.wait_ge(s_bp, 1)
            nc.scalar.activation(betaT[:, :, :], PS[0:H, 0:B, :], ACT.Sigmoid, bias=bb_sb[:, 0:1]).then_inc(s_bs, 1)
            act.wait_ge(s_bs, 1)
            nc.scalar.mul(betaT[:, :, :], betaT[:, :, :], S2).then_inc(s_beta, 1)

            def activate(i, u):
                hh, b, q = u // 6, u // 3 % 2, u % 3
                n = b * H + 2 * i + hh
                dst = (KQ[:, 1, bass.ds(n, 1), 1:L + 1], KQ[:, 0, bass.ds(n, 1), 0:L], VO[:, bass.ds(n, 1), :])[q]
                wait(act, s_conv, i * 12 + u + 1)
                nc.scalar.activation(dst, acc[:, u % 4:u % 4 + 1, :], ACT.Silu).then_inc(s_silu, 1)

            def heads(i, load):
                for hh in range(2):
                    wait(act, s_wh[hh], 32 * (i + 1))
                    for b in range(B):
                        wait(act, s_pa, 4 * i + 2 * hh + b + 1)
                        nc.scalar.activation(A[:, bass.ds(b * H + 2 * i + hh, 1), :], PS[:, 6 + b:7 + b, :], ACT.Sigmoid,
                                             bias=cw[:, hh, 15:16]).then_inc(s_sa, 1)
                for u in range(12 + 2):
                    if u < 12:
                        q = u % 3
                        wait(act, s_pq, 12 * i + u + 1)
                        wait(act, s_silu, 12 * i + u - 3)
                        nc.scalar.activation(acc[:, u % 4, :], PS[:, u % 6, :], ACT.Identity,
                                             scale=cw[:, u // 6, 5 * q + 3:5 * q + 4],
                                             bias=cw[:, u // 6, 5 * q + 4:5 * q + 5]).then_inc(s_pre, 1)
                    if u >= 2:
                        activate(i, u - 2)

            heads(0, False)
            with act.Fori(1, H // 2) as i:
                heads(i, True)

            def keep_z(o):
                for u in range(4):
                    b = u // 2
                    wait(act, e_z, 4 * o + u + 1)
                    wait(act, v_r, 2 * (o * NB - 1) + b + 1)
                    nc.scalar.activation(Z[b][:, 4 * (u % 2):4 * (u % 2) + 4],
                                         PS[:, 6 + u % 2, 0:4 * 2 * (CH + 1)].rearrange("p (n y t) -> p n y t", n=4, y=2),
                                         ACT.Copy).then_inc(a_z, 1)

            def keys_by_block(o):
                wait(act, v_kb, o + 1)
                wait(act, e_gr, o * GRAMS)
                nc.scalar.activation(KBb.rearrange("p i n s -> p n i s"), KBo.rearrange("p n (i s) -> p n i s", i=NB),
                                     ACT.Copy).then_inc(a_kb, 1)

            def chunk(o, last=False):
                keep_z(o)
                for i in range(NB):
                    m, t0, y = o * NB + i, o * CH + i * C, i % 2
                    if i < NB - 1:
                        wait(act, e_wt, o * (NB - 1) + i + 1)
                        wait(act, e_ap, o * GRAMS + 2 * i)
                        nc.scalar.activation(WTs, PS[:, 4, 0:P], ACT.Copy).then_inc(a_wt, 1)
                    for b in range(B):
                        wait(act, v_r, 2 * m + b + 1)
                        nc.scalar.activation(VO[:, b * H:(b + 1) * H, bass.ds(t0, C)], R[y][b][:, :, 1, 1:C + 1],
                                             ACT.Copy).then_inc(a_o, 1)
                    if i == 2:
                        wait(act, e_kt, o + 1)
                        wait(act, e_dl, 4 * o)
                        nc.scalar.activation(KBT, PS[:, 3, :].rearrange("p (g k) -> p g k", g=4), ACT.Copy,
                                             scale=-1.0).then_inc(a_kt, 1)
                    if i == 2 and not last:
                        wait(act, p_ab, o + 1)
                        wait(act, e_st, 4 * o)
                        wait(act, v_s, 4 * o)
                        act.wait_ge(s_init, 2)
                        for n in range(NP):
                            ins = nc.scalar.activation(S[:, n], S[:, n], ACT.Copy, scale=SB[:, 0, n:n + 1])
                        ins.then_inc(a_sa, 1)
                    if i == NB - 2 and not last:
                        keys_by_block(o + 1)
                if last:
                    return
                wait(act, e_wo, o + 1)
                wait(act, e_dl, 4 * o)
                nc.scalar.activation(WTo, PS[:, 3, :].rearrange("p (g k) -> p g k", g=4), ACT.Copy).then_inc(a_wo, 1)
                for u in range(4):
                    wait(act, e_st, 4 * o + u + 1)
                    wait(act, e_z, 4 * o + 4)
                    nc.scalar.activation(ST[:, u:NP:4], PS[:, 6 + u % 2, :].rearrange("p (n k) -> p n k", n=4),
                                         ACT.Copy).then_inc(a_st, 1)

            keys_by_block(0)
            chunk(0)
            with act.Fori(1, NCH - 1) as o:
                chunk(o)
            chunk(NCH - 1, last=True)

            for h in range(H):
                for b in range(B):
                    act.wait_ge(g_p, 2 * h + b + 1)
                    nc.scalar.activation(G[:, b * H + h], PS[:, 2 * (h % 2) + b, :], ACT.Sigmoid).then_inc(g_s, 1)
            for n in range(NP):
                act.wait_ge(o_c, n + 1)
                wait(act, o_v, n - 1)
                nc.scalar.activation(sq[:, n % 2], oc[:, n % 2], ACT.Square).then_inc(o_q, 1)
                act.wait_ge(o_v, n + 1)
                wait(act, o_y, n - 1)
                nc.scalar.activation(sd[:, n % 2], PS[:, 6 + n % 2, :], ACT.Sqrt, bias=eps_col[:, 1:2]).then_inc(o_d, 1)
                act.wait_ge(o_y, n + 1)
                nc.scalar.activation(oc[:, n % 2], oc[:, n % 2], ACT.Identity, scale=lngb[:, 0:1],
                                     bias=lngb[:, 1:2]).then_inc(o_a, 1)

            def norm_std(r):
                act.wait_ge(x_mv, NT * (r + 1))
                nc.scalar.activation(std[:, :], mv[:, :, 1], ACT.Sqrt, bias=eps_col[:, 0:1]).then_inc(x_sd, 1)

            act.wait_ge(o_g, NP)
            for u in range(B * XG):
                g, b = u % XG, u // XG
                act.wait_ge(x_kp, u + 1)
                nc.scalar.activation(xKT[:, g, b * L:(b + 1) * L], PS[:, 4 + u % 2, :], ACT.Copy).then_inc(x_k, 1)
            norm_std(0)
            for u in range(B * XG):
                g, b = u % XG, u // XG
                act.wait_ge(x_qp, u + 1)
                nc.scalar.activation(xQT[:, g, b * L:(b + 1) * L], PS[:, 4 + u % 2, :], ACT.Copy,
                                     scale=XD ** -0.5).then_inc(x_q, 1)
            u = 0
            for b in range(B):
                for g in range(XG):
                    if b * XG + g >= 2:
                        act.wait_ge(x_pv, b * XG + g - 1)
                    for j in range(QT_N):
                        for half in range(2):
                            act.wait_ge(x_st, u + 1)
                            n = L - j * P
                            nc.scalar.activation(probs(g % 2, j)[:, 2 * half:2 * half + 2], PS[:, 2 * (u % 3):2 * (u % 3) + 2, 0:n],
                                                 ACT.Exp).then_inc(x_e, 1)
                            u += 1
            norm_std(1)
            norm_std(2)
            norm_std(3)
            for u in range(ET * B):
                e, b = u // B, u % B
                act.wait_ge(f_lg, u + 1)
                nc.scalar.activation(LG[:, e, b * L:(b + 1) * L], PS[:, u % 4, :], ACT.Copy).then_inc(f_lk, 1)
                act.wait_ge(f_mE, u + 1)
                nc.scalar.activation(FS[:, e, b * L:(b + 1) * L], PS[:, u % 4, :], ACT.Exp, bias=mE[:, e, b:b + 1],
                                     accum_out=dE[:, e, b:b + 1]).then_inc(f_fs, 1)
            for n in range(NT):
                act.wait_ge(f_mN, n + 1)
                wait(act, f_eh, 2 * (n - 1))
                nc.scalar.activation(E1[:, n % 2], PS[:, 4 + 2 * (n % 2):6 + 2 * (n % 2), :].rearrange("p b c -> p (b c)"),
                                     ACT.Exp, bias=mN[:, n:n + 1], accum_out=dN[:, n:n + 1]).then_inc(f_e1, 1)
            act.wait_ge(f_lt, NT)
            for u in range(2 * B * KT):
                b, k, half = u // 4, u // 2 % 2, u % 2
                act.wait_ge(f_sp, u + 1)
                nc.scalar.activation(slT[:, k, half * 8:(half + 1) * 8, b * SL:(b + 1) * SL],
                                     PS[:, u % 2, :].rearrange("p (e s) -> p e s", e=8), ACT.Copy).then_inc(f_sk, 1)

            def experts(i):
                for slot in range(2):
                    act.wait_ge(w_ld[slot], 64 * (i + 1))
                    act.wait_ge(w_gu, 2 * i + slot + 1)
                    wait(act, w_h, 2 * i + slot - 1)
                    for f in range(FT):
                        ins = nc.scalar.activation(gel[:, slot, f], PS[:, 2 * slot, f * P:(f + 1) * P], ACT.Gelu,
                                                   bias=bgu[:, slot, f:f + 1])
                    ins.then_inc(w_ge, 1)

            experts(0)
            with act.Fori(1, E // 2) as i:
                experts(i)

        @block.tensor
        def _(pe):
            pe.wait_ge(s_cst, 8)
            for n in range(NT):
                pe.wait_ge(s_xn, n + 1)
                wait(pe, s_xT, n - 1)
                for k in range(KT):
                    ins = nc.tensor.transpose(PS[:, 6 + n % 2, k * P:(k + 1) * P], xn[:, n % 2, k * P:(k + 1) * P],
                                              ident[:, :])
                ins.then_inc(s_xtp, 1)
            pe.wait_ge(s_xT, NT)
            pe.wait_ge(s_small, 48)
            for b in range(B):
                for k in range(KT):
                    ins = nc.tensor.matmul(PS[0:H, b, :], wb_sb[:, k, :], xT[:, k, b * L:(b + 1) * L],
                                           start=(k == 0), stop=(k == KT - 1))
            ins.then_inc(s_bp, 1)

            def heads(i, first):
                for hh in range(2):
                    wait(pe, s_wh[hh], 32 * (i + 1))
                    for b in range(B):
                        if not (first and hh == 0):
                            wait(pe, s_sa, 4 * i + 2 * hh + b - 1)
                        for k in range(KT):
                            ins = nc.tensor.matmul(PS[:, 6 + b, :], wh[:, hh, 3, k, :], xT[:, k, b * L:(b + 1) * L],
                                                   start=(k == 0), stop=(k == KT - 1))
                        ins.then_inc(s_pa, 1)
                if first:
                    pe.wait_ge(s_bs, 1)
                for u in range(12):
                    hh, b, q = u // 6, u // 3 % 2, u % 3
                    wait(pe, s_conv, 12 * i + u - 5)
                    for k in range(KT):
                        ins = nc.tensor.matmul(PS[:, u % 6, :], wh[:, hh, q, k, :], xT[:, k, b * L:(b + 1) * L],
                                               start=(k == 0), stop=(k == KT - 1))
                    ins.then_inc(s_pq, 1)

            heads(0, True)
            with pe.Fori(1, H // 2) as i:
                heads(i, False)

            def beta_all(o):
                wait(pe, p_bm, o + 1)
                wait(pe, a_kt, o)
                wait(pe, a_wo, o - 1)
                nc.tensor.matmul(PS[:, 3, :], ones[0:H, :], beta_m[:, :, :, :].rearrange("r b h s -> r (b h s)"),
                                 start=True, stop=True).then_inc(e_bb, 1)

            def prep(o, i):
                m, y = o * NB + i, i % 2
                wait(pe, p_x, m + 1)
                wait(pe, v_n, m)
                xf = X[y].rearrange("p y c -> p (y c)")
                for c0 in range(0, 2 * TRI, 512):
                    c1 = min(c0 + 512, 2 * TRI)
                    ins = nc.tensor.matmul(PSF[:, c0:c1], ones[:, :], xf[:, c0:c1], start=True, stop=True)
                ins.then_inc(e_g, 1)

            def grams(o, i):
                if i < NB - 1:
                    n = CH - (i + 1) * C + 1
                    for b in range(B):
                        wait(pe, v_gm, o * GRAMS + 2 * i + b)
                        if i == 0 and b == 0:
                            wait(pe, a_kb, o + 1)
                            wait(pe, a_wo, o)
                        for q in range(2):
                            ins = nc.tensor.matmul(
                                PS[:, 3, q * H * n:(q + 1) * H * n].rearrange("p (h t) -> p h t", h=H),
                                KBb[:, i].rearrange("p n s -> p (n s)"),
                                KQ[:, q, b * H:(b + 1) * H, bass.ds(o * CH + (i + 1) * C, n)],
                                start=(q == 0), stop=(q == 1), skip_group_check=True)
                        ins.then_inc(e_gr, 1)

            def chunk(o, last=False):
                for u in range(4):
                    wait(pe, a_st, 4 * o)
                    wait(pe, a_z, 4 * o + u - 1)
                    for j in range(4):
                        n = 4 * u + j
                        ins = nc.tensor.matmul(
                            PS[:, 6 + u % 2, j * 2 * (CH + 1):(j + 1) * 2 * (CH + 1)].rearrange("p (y t) -> p y t", y=2),
                            ST[:, n], KQ[:, :, n, bass.ds(o * CH, CH + 1)], start=True, stop=True)
                    ins.then_inc(e_z, 1)
                for i in range(NB):
                    if i < NB - 1:
                        prep(o, i + 1)
                    elif not last:
                        beta_all(o + 1)
                        prep(o + 1, 0)
                    if i == 2:
                        wait(pe, v_gm, o * GRAMS + GRAMS)
                        for g in range(4):
                            ins = nc.tensor.transpose(PS[:, 3, g * P:(g + 1) * P],
                                                      KBo[:, 4 * g:4 * g + 4, :].rearrange("p n s -> p (n s)"), ident[:, :])
                        ins.then_inc(e_kt, 1)
                    if i == NB - 1:
                        break
                    wait(pe, v_w, 2 * (o * NB + i) + 2)
                    wait(pe, v_za, o * GRAMS + 2 * i)
                    nc.tensor.transpose(PS[:, 4, 0:P], Wst[:, i].rearrange("p n s -> p (n s)"),
                                        ident[:, :]).then_inc(e_wt, 1)
                    n = CH - (i + 1) * C + 1
                    for b in range(B):
                        k = o * GRAMS + 2 * i + b + 1
                        rows = slice(C * H * b, C * H * (b + 1))
                        wait(pe, a_wt, o * (NB - 1) + i + 1)
                        wait(pe, v_gm, k)
                        nc.tensor.matmul(PS[:, 4 + b, 0:2 * H * n], WTs[rows, :], GM[rows, 0:2 * H * n], start=True,
                                         stop=True, tile_position=(C * H * b, 0)).then_inc(e_ap, 1)
                    grams(o, i + 1)
                if last:
                    return
                wait(pe, v_wo, o + 1)
                wait(pe, v_kb, o + 2)
                wait(pe, a_kt, o + 1)
                for g in range(4):
                    ins = nc.tensor.transpose(PS[:, 3, g * P:(g + 1) * P],
                                              Wsc[:, 4 * g:4 * g + 4, :].rearrange("p n s -> p (n s)"), ident[:, :])
                ins.then_inc(e_wo, 1)
                wait(pe, a_wo, o + 1)
                for u in range(4):
                    wait(pe, a_z, 4 * o + 4)
                    wait(pe, v_s, 4 * o + u - 1)
                    for j in range(4):
                        ins = nc.tensor.matmul(PS[:, 6 + u % 2, j * P:(j + 1) * P], WTo[CH * u:CH * (u + 1), j, :],
                                               KBT[CH * u:CH * (u + 1), j, :], start=True, stop=True,
                                               tile_position=(CH * u, 0))
                    ins.then_inc(e_dl, 1)
                grams(o + 1, 0)
                for u in range(4):
                    wait(pe, v_s, 4 * o + max(u + 1, min(u + 3, 4)))
                    wait(pe, a_st, 4 * o + u - 1)
                    for j in range(4):
                        ins = nc.tensor.transpose(PS[:, 6 + u % 2, j * P:(j + 1) * P], S[:, 4 * j + u, :], ident[:, :])
                    ins.then_inc(e_st, 1)

            pe.wait_ge(s_beta, 1)
            pe.wait_ge(s_conv, 6 * H)
            pe.wait_ge(s_silu, 6 * H)
            pe.wait_ge(s_sa, 2 * H)
            pe.wait_ge(s_init, 2)
            beta_all(0)
            prep(0, 0)
            grams(0, 0)
            chunk(0)
            with pe.Fori(1, NCH - 1) as o:
                chunk(o)
            chunk(NCH - 1, last=True)

            pe.wait_ge(a_o, 2 * NCH * NB)
            for h in range(H):
                pe.wait_ge(g_ld[h % 2], 16 * (h // 2 + 1))
                for b in range(B):
                    wait(pe, g_s, 2 * h + b - 3)
                    for k in range(KT):
                        ins = nc.tensor.matmul(PS[:, 2 * (h % 2) + b, :], wg_sb[:, h % 2, k, :], xT[:, k, b * L:(b + 1) * L],
                                               start=(k == 0), stop=(k == KT - 1))
                    ins.then_inc(g_p, 1)
            for n in range(NP):
                wait(pe, o_c, n - 1)
                nc.tensor.matmul(PS[:, 4 + n % 2, :], avg[:, :], VO[:, n], start=True, stop=True).then_inc(o_m, 1)
                pe.wait_ge(o_q, n + 1)
                wait(pe, o_d, n - 1)
                nc.tensor.matmul(PS[:, 6 + n % 2, :], avg[:, :], sq[:, n % 2], start=True, stop=True).then_inc(o_v, 1)
            pe.wait_ge(g_wo, 16)
            pe.wait_ge(o_g, NP)
            for n in range(NT):
                b, i = n // (NT // B), n % (NT // B)
                wait(pe, o_x, n - 3)
                for h in range(H):
                    ins = nc.tensor.matmul(PS[:, n % 4, 0:D], VO[:, b * H + h, i * P:(i + 1) * P], wo_sb[:, h, :],
                                           start=(h == 0), stop=(h == H - 1))
                ins.then_inc(o_p, 1)

            pe.wait_ge(x_cst, 6)
            pe.wait_ge(x_ld, 16 * 9)
            for n in range(NT):
                wait(pe, x_cT, n - 1)
                for k in range(KT):
                    ins = nc.tensor.transpose(PS[:, 6 + n % 2, k * P:(k + 1) * P], ctxt[:, n, k * P:(k + 1) * P],
                                              ident[:, :])
                ins.then_inc(x_ct, 1)
            pe.wait_ge(x_cT, NT)
            pe.wait_ge(x_mk, 3)
            for u in range(B * XG):
                g, b = u % XG, u // XG
                wait(pe, x_k, u - 1)
                for k in range(KT):
                    nc.tensor.matmul(PS[:, 4 + u % 2, :], xwk[:, k, g * P:(g + 1) * P], ctxT[:, k, b * L:(b + 1) * L],
                                     start=(k == 0), stop=False)
                nc.tensor.matmul(PS[:, 4 + u % 2, :], rowsk, mrow[:, b * L:(b + 1) * L], start=False,
                                 stop=True).then_inc(x_kp, 1)
            for n in range(NT):
                wait(pe, x_v, n - 1)
                for k in range(KT):
                    ins = nc.tensor.matmul(PS[:, 6 + n % 2, 0:D], ctxT[:, k, n * P:(n + 1) * P], xwv[:, k, :],
                                           start=(k == 0), stop=(k == KT - 1))
                ins.then_inc(x_vp, 1)

            def transpose_x(r, bank):
                for n in range(NT):
                    pe.wait_ge(x_xn, NT * r + n + 1)
                    wait(pe, x_xT, NT * r + n - 1)
                    for k in range(KT):
                        ins = nc.tensor.transpose(PS[:, bank + n % 2, k * P:(k + 1) * P],
                                                  (xn2[:, n % 2] if r == 0 else xf[:, n])[:, k * P:(k + 1) * P], ident[:, :])
                    ins.then_inc(x_tp, 1)
                pe.wait_ge(x_xT, NT * (r + 1))

            pe.wait_ge(x_v, NT)
            transpose_x(0, 6)
            pe.wait_ge(x_k, B * XG)
            for u in range(B * XG):
                g, b = u % XG, u // XG
                wait(pe, x_q, u - 1)
                for k in range(KT):
                    nc.tensor.matmul(PS[:, 4 + u % 2, :], xwq[:, k, g * P:(g + 1) * P], xT[:, k, b * L:(b + 1) * L],
                                     start=(k == 0), stop=False)
                nc.tensor.matmul(PS[:, 4 + u % 2, :], rowsq, ones_row, start=False, stop=True).then_inc(x_qp, 1)
            pe.wait_ge(x_q, B * XG)
            u = 0
            for n in range(NT):
                b, i = n // QT_N, n % QT_N
                w = (i + 1) * P
                for g in range(XG):
                    for half in range(2):
                        wait(pe, x_mx, u - 2)
                        for j in range(2):
                            h, bank = 2 * half + j, 2 * (u % 3) + j
                            nc.tensor.matmul(PS[:, bank, i * P:w], identb[:, :], late[:, :], start=True, stop=True)
                            if i:
                                nc.tensor.matmul(PS[:, bank, 0:i * P], xQT[32 * h:32 * h + 32, g, n * P:(n + 1) * P],
                                                 xKT[32 * h:32 * h + 32, g, b * L:b * L + i * P], start=False, stop=True,
                                                 tile_position=(32 * h, 0), skip_group_check=True)
                            ins = nc.tensor.matmul(PS[:, bank, i * P:w], xQT[32 * h:32 * h + 32, g, n * P:(n + 1) * P],
                                                   xKT[32 * h:32 * h + 32, g, b * L + i * P:b * L + w], start=False,
                                                   stop=True, tile_position=(32 * h, 0), skip_group_check=True)
                        ins.then_inc(x_s, 1)
                        u += 1
            for n in range(NT):
                pe.wait_ge(x_mx, 8 * (n + 1))
                wait(pe, x_q2, n - 1)
                for g in range(XG):
                    ins = nc.tensor.transpose(PS[:, 6 + n % 2, g * P:(g + 1) * P], xMx[:, n, g, :], ident[:, :])
                ins.then_inc(x_mt, 1)
            pe.wait_ge(x_q2, NT)
            u = 0
            for b in range(B):
                for g in range(XG):
                    for j in range(QT_N):
                        w = L - j * P
                        for half in range(2):
                            wait(pe, x_e, u - 2)
                            for hh in range(2):
                                h, bank = 2 * half + hh, 2 * (u % 3) + hh
                                nc.tensor.matmul(PS[:, bank, 0:P], identb[:, :], early[:, :], start=True, stop=True)
                                ins = nc.tensor.matmul(PS[:, bank, 0:w],
                                                       xKT[32 * h:32 * h + 32, g, b * L + j * P:b * L + (j + 1) * P],
                                                       xQ2[32 * h:32 * h + 32, g, b * L + j * P:(b + 1) * L], start=False,
                                                       stop=True, tile_position=(32 * h, 0), skip_group_check=True)
                            ins.then_inc(x_st, 1)
                            u += 1
                    pe.wait_ge(x_e, u)
                    wait(pe, x_at, b * XG + g - 1)
                    for i in range(QT_N):
                        for h in range(4):
                            c0 = (i * 4 + h) * 17
                            for j in range(i + 1):
                                ins = nc.tensor.matmul(PS[:, 6 + g % 2, c0:c0 + 17],
                                                       probs(g % 2, j)[:, h, (i - j) * P:(i - j + 1) * P],
                                                       xV[:, b * QT_N + j, 4 * g + h, :], start=(j == 0), stop=(j == i))
                    ins.then_inc(x_pv, 1)
            pe.wait_ge(x_at, 2 * XG)
            for n in range(NT):
                wait(pe, x_aT, n - 1)
                for k in range(KT):
                    ins = nc.tensor.transpose(PS[:, 6 + n % 2, k * P:(k + 1) * P], att[:, n, k * P:(k + 1) * P], ident[:, :])
                ins.then_inc(x_tt, 1)
            for n in range(NT):
                pe.wait_ge(x_aT, n + 1)
                wait(pe, x_x, n - 1)
                for k in range(KT):
                    ins = nc.tensor.matmul(PS[:, 4 + n % 2, 0:D], attT[:, k, n * P:(n + 1) * P], xwo[:, k, :],
                                           start=(k == 0), stop=(k == KT - 1))
                ins.then_inc(x_op, 1)

            for n in range(ET):
                pe.wait_ge(f_se, n + 1)
                wait(pe, f_sT, n - 1)
                for k in range(KT):
                    ins = nc.tensor.transpose(PS[:, 6 + n % 2, k * P:(k + 1) * P], se[:, n, k * P:(k + 1) * P], ident[:, :])
                ins.then_inc(f_st, 1)
            pe.wait_ge(f_sT, ET)
            transpose_x(1, 6)
            for u in range(ET * B):
                e, b = u // B, u % B
                wait(pe, f_fs, u - 3)
                wait(pe, f_mE, u - 3)
                for k in range(KT):
                    ins = nc.tensor.matmul(PS[:, u % 4, :], seT[:, k, e * P:(e + 1) * P], xT[:, k, b * L:(b + 1) * L],
                                           start=(k == 0), stop=(k == KT - 1))
                ins.then_inc(f_lg, 1)
            pe.wait_ge(f_lk, ET * B)

            def logits_turned(n):
                wait(pe, f_e1, n - 1)
                wait(pe, f_mN, n - 1)
                for e in range(ET):
                    ins = nc.tensor.transpose(PS[:, 4 + 2 * (n % 2) + e // 4, (e % 4) * P:(e % 4 + 1) * P],
                                              LG[:, e, n * P:(n + 1) * P], ident[:, :])
                ins.then_inc(f_lt, 1)

            logits_turned(0)
            pe.wait_ge(f_fs, ET * B)
            for n in range(NT):
                if n + 1 < NT:
                    logits_turned(n + 1)
                for half in range(2):
                    v = 2 * n + half
                    wait(pe, f_fk, v - 1)
                    pe.wait_ge(f_fn, 8 * half + 8)
                    for e in range(4):
                        ins = nc.tensor.transpose(PS[:, v % 2, e * P:(e + 1) * P], FS[:, 4 * half + e, n * P:(n + 1) * P],
                                                  ident[:, :])
                    ins.then_inc(f_ft, 1)
                pe.wait_ge(f_e1, n + 1)
                for half in range(2):
                    v = 2 * n + half
                    wait(pe, f_ek, v - 1)
                    for e in range(4):
                        c0 = (4 * half + e) * P
                        ins = nc.tensor.transpose(PS[:, 2 + v % 2, e * P:(e + 1) * P], E1[:, n % 2, c0:c0 + P], ident[:, :])
                    ins.then_inc(f_eh, 1)
            pe.wait_ge(f_fk, 2 * NT)
            for u in range(2 * B * KT):
                b, k, half = u // 4, u // 2 % 2, u % 2
                wait(pe, f_sk, u - 1)
                for j in range(QT_N):
                    n = b * QT_N + j
                    ins = nc.tensor.matmul(PS[:, u % 2, :], xf[:, n, k * P:(k + 1) * P], FD[:, n, half * L:(half + 1) * L],
                                           start=(j == 0), stop=(j == QT_N - 1))
                ins.then_inc(f_sp, 1)
            pe.wait_ge(f_sk, 2 * B * KT)
            pe.wait_ge(f_ek, 2 * NT)

            def gate_up(i, slot):
                e = 2 * i + slot
                wait(pe, w_ld[slot], 64 * (i + 1))
                wait(pe, w_ge, e - 1)
                wait(pe, w_h, e - 1)
                for y in range(2):
                    for f in range(FT):
                        for k in range(KT):
                            ins = nc.tensor.matmul(PS[:, 2 * slot + y, f * P:(f + 1) * P],
                                                   wgu[slot][:, y, k, f * P:(f + 1) * P],
                                                   slT[:, k, bass.ds(e, 1), :].rearrange("p e c -> p (e c)"),
                                                   start=(k == 0), stop=(k == KT - 1))
                ins.then_inc(w_gu, 1)

            def down(i, slot):
                e = 2 * i + slot
                wait(pe, w_h, e + 1)
                wait(pe, w_eo, 2 * (e - 1))
                for f in range(FT):
                    ins = nc.tensor.matmul(PS[:, 4 + slot, 0:D], hT[:, slot, f], wdn[slot][:, f, :], start=(f == 0),
                                           stop=(f == FT - 1))
                ins.then_inc(w_dn, 1)

            def experts(i):
                gate_up(i, 0)
                gate_up(i, 1)
                down(i, 0)
                down(i, 1)

            experts(0)
            with pe.Fori(1, E // 2) as i:
                experts(i)
            for n in range(NT):
                b = n // QT_N
                pe.wait_ge(w_eo, 2 * E)
                wait(pe, w_x, n - 1)
                for e in range(ET):
                    ins = nc.tensor.matmul(PS[:, 6 + n % 2, 0:D], EC[:, e, n * P:(n + 1) * P], eo[:, e, b, :],
                                           start=(e == 0), stop=(e == ET - 1))
                ins.then_inc(w_cb, 1)

        @block.vector
        def _(dve):
            me = Steps(dve, s_dve)
            dve.wait_ge(s_x, 16)
            for n in range(NT):
                me.did(nc.vector.bn_stats(stats[:, n, :], xt[:, n, :]))
            me.settle()
            for n in range(NT):
                nc.vector.bn_aggr(mv[:, n, :], stats[:, n, :]).then_inc(s_mv, 1)
            dve.wait_ge(s_std, 1)
            me.link(nc.vector.reciprocal(rstd[:, :], std[:, :]))
            dve.wait_ge(s_mv, NT)
            for n in range(NT):
                wait(dve, s_xtp, n - 1)
                nc.vector.tensor_scalar(xn[:, n % 2], xt[:, n, :], mv[:, n, 0:1], rstd[:, n:n + 1], ALU.subtract,
                                        ALU.mult).then_inc(s_xn, 1)
                if n > 0:
                    dve.wait_ge(s_xtp, n)
                    nc.vector.tensor_copy(xT[:, :, (n - 1) * P:n * P],
                                          PS[:, 6 + (n - 1) % 2, 0:KT * P].rearrange("p (k c) -> p k c", k=KT)
                                          ).then_inc(s_xT, 1)
            dve.wait_ge(s_xtp, NT)
            nc.vector.tensor_copy(xT[:, :, (NT - 1) * P:NT * P],
                                  PS[:, 6 + (NT - 1) % 2, 0:KT * P].rearrange("p (k c) -> p k c", k=KT)).then_inc(s_xT, 1)

            def heads(i):
                for u in range(12):
                    hh, q = u // 6, u % 3
                    wait(dve, s_pre, 12 * i + u + 1)
                    for j in range(1, 4):
                        ins = nc.vector.scalar_tensor_tensor(
                            out=acc[:, u % 4, j:L], in0=PS[:, u % 6, 0:L - j], scalar=cw[:, hh, 5 * q + 3 - j:5 * q + 4 - j],
                            in1=acc[:, u % 4, j:L], op0=ALU.mult, op1=ALU.add)
                        if j < 3:
                            me.link(ins)
                    ins.then_inc(s_conv, 1)

            base = me.total()
            me.at(base)
            heads(0)
            per = me.k
            second = me.total()
            with dve.Fori(1, H // 2) as i:
                me.at(second + (i - 1) * per)
                heads(i)
            me.at(second + (H // 2 - 1) * per)

            own_steps = [Steps(dve, s_g0), Steps(dve, s_g1)]

            def beta_keys(o):
                wait(dve, e_bb, o + 1)
                wait(dve, e_kt, o)
                wait(dve, p_x, o * NB)
                wait(dve, a_kb, o)
                nc.vector.tensor_tensor(out=KBo, in0=KQ[:, 0, :, bass.ds(o * CH, CH)],
                                        in1=PS[:, 3, :].rearrange("p (n s) -> p n s", n=NP), op=ALU.mult).then_inc(v_kb, 1)

            def prep(o, i):
                m, y = o * NB + i, i % 2
                wait(dve, e_g, m + 1)
                wait(dve, p_d, m + 1)
                nc.vector.tensor_tensor(out=N, in0=PSF[:, 0:2 * TRI].rearrange("p (y c) -> p y c", y=2),
                                        in1=Dt[y].unsqueeze(1).to_broadcast([P, 2, TRI]), op=ALU.mult).then_inc(v_n, 1)

            def masks(o, i):
                if i < NB - 1:
                    n = CH - (i + 1) * C + 1
                    for b in range(B):
                        wait(dve, e_gr, o * GRAMS + 2 * i + b + 1)
                        wait(dve, e_ap, o * GRAMS + 2 * (i - 1) + b + 1)
                        rows = slice(C * H * b, C * H * (b + 1))
                        nc.vector.tensor_tensor(
                            out=GM[rows, 0:2 * H * n].rearrange("p (y h t) -> p y h t", y=2, h=H),
                            in0=PS[rows, 3, 0:2 * H * n].rearrange("p (y h t) -> p y h t", y=2, h=H),
                            in1=own[rows, b * H:(b + 1) * H].unsqueeze(1).unsqueeze(3).to_broadcast([C * H, 2, H, n]),
                            op=ALU.mult).then_inc(v_gm, 1)

            def solve(o, i):
                m, t0, y = o * NB + i, o * CH + i * C, i % 2
                r = R[y]
                wait(dve, p_d, m + 1)
                wait(dve, a_o, 2 * (m - 1))
                for b, st in enumerate(own_steps):
                    if i == 0:
                        wait(dve, a_z, 4 * o + 2 * b + 2)
                    st.settle()
                    st.did(nc.vector.tensor_tensor(
                        out=r[b], in0=Z[b][:, :, :, i * C:(i + 1) * C + 1],
                        in1=Pre[y][:, b * H:(b + 1) * H].unsqueeze(2).to_broadcast([P, H, 2, C + 1]), op=ALU.mult))
                for b, st in enumerate(own_steps):
                    st.settle()
                    st.did(nc.vector.tensor_tensor(out=r[b][:, :, 0, 0:C], in0=r[b][:, :, 0, 0:C],
                                                   in1=VO[:, b * H:(b + 1) * H, bass.ds(t0, C)], op=ALU.subtract))
                dve.wait_ge(v_n, m + 1)
                for s in range(C):
                    n = C - s
                    for b, st in enumerate(own_steps):
                        st.settle()
                        cols = N[:, :, OFF[s] + b * H * n:OFF[s] + (b + 1) * H * n]
                        st.did(nc.vector.tensor_tensor(
                            out=Pr[b][:, 0:2 * H * n].rearrange("p (y h t) -> p y h t", y=2, h=H),
                            in0=cols.rearrange("p y (h t) -> p y h t", h=H),
                            in1=r[b][:, :, 0, s:s + 1].unsqueeze(1).to_broadcast([P, 2, H, n]), op=ALU.mult))
                    for b, st in enumerate(own_steps):
                        st.settle()
                        dst = r[b][:, :, :, s + 1:C + 1].rearrange("p h y t -> p y h t")
                        ins = nc.vector.tensor_tensor(
                            out=dst, in0=dst, in1=Pr[b][:, 0:2 * H * n].rearrange("p (y h t) -> p y h t", y=2, h=H),
                            op=ALU.subtract)
                        if s < C - 1:
                            st.did(ins)
                        else:
                            ins.then_inc(v_r, 1)
                for b in range(B):
                    dve.wait_ge(v_r, 2 * m + b + 1)
                    nc.vector.tensor_tensor(out=Wst[:, i, b * H:(b + 1) * H], in0=r[b][:, :, 0, 0:C],
                                            in1=Suf[y][:, b * H:(b + 1) * H], op=ALU.mult).then_inc(v_w, 1)

            def move_on(o, i):
                y, n = i % 2, CH - (i + 1) * C + 1
                for b, st in enumerate(own_steps):
                    z = Z[b][:, :, :, (i + 1) * C:CH + 1]
                    st.did(nc.vector.tensor_tensor(
                        out=z, in0=z, in1=Pre[y][:, b * H:(b + 1) * H, C:C + 1].unsqueeze(2).to_broadcast([P, H, 2, n]),
                        op=ALU.mult))
                for b, st in enumerate(own_steps):
                    st.settle()
                    wait(dve, e_ap, o * GRAMS + 2 * i + b + 1)
                    z = Z[b][:, :, :, (i + 1) * C:CH + 1].rearrange("p h y t -> p y h t")
                    nc.vector.tensor_tensor(
                        out=z, in0=z, in1=PS[:, 4 + b, 0:2 * H * n].rearrange("p (y h t) -> p y h t", y=2, h=H),
                        op=ALU.add).then_inc(v_za, 1)

            def chunk(o, last=False):
                for i in range(NB):
                    if i > 0:
                        dve.wait_ge(v_za, o * GRAMS + 2 * i)
                    solve(o, i)
                    if i < NB - 1:
                        prep(o, i + 1)
                        move_on(o, i)
                        masks(o, i + 1)
                        if i == NB - 2 and not last:
                            beta_keys(o + 1)
                if last:
                    return
                wait(dve, p_ab, o + 1)
                dve.wait_ge(v_w, 2 * (o + 1) * NB)
                for b in range(B):
                    ins = nc.vector.tensor_tensor(
                        out=Wsc[:, b * H:(b + 1) * H].rearrange("p n (i s) -> p n i s", i=NB),
                        in0=Wst[:, :, b * H:(b + 1) * H].rearrange("p i n s -> p n i s"),
                        in1=SB[:, 1:NB + 1, b * H:(b + 1) * H].rearrange("p i n -> p n i").unsqueeze(3)
                        .to_broadcast([P, H, NB, C]), op=ALU.mult)
                ins.then_inc(v_wo, 1)
                prep(o + 1, 0)
                wait(dve, a_sa, o + 1)
                for u in range(4):
                    wait(dve, e_dl, 4 * o + u + 1)
                    nc.vector.tensor_tensor(out=S[:, u:NP:4], in0=S[:, u:NP:4],
                                            in1=PS[:, 6 + u % 2, :].rearrange("p (n k) -> p n k", n=4),
                                            op=ALU.add).then_inc(v_s, 1)
                masks(o + 1, 0)

            dve.wait_ge(s_silu, 6 * H)
            dve.wait_ge(s_cst, 8)
            beta_keys(0)
            prep(0, 0)
            masks(0, 0)
            chunk(0)
            per = [st.k for st in own_steps]
            with dve.Fori(1, NCH - 1) as o:
                for st, k in zip(own_steps, per):
                    st.at(o * k)
                chunk(o)
            for st, k in zip(own_steps, per):
                st.at((NCH - 1) * k)
            chunk(NCH - 1, last=True)

            for n in range(NP):
                dve.wait_ge(o_m, n + 1)
                wait(dve, o_g, n - 1)
                nc.vector.tensor_tensor(out=oc[:, n % 2], in0=VO[:, n], in1=PS[:, 4 + n % 2, :],
                                        op=ALU.subtract).then_inc(o_c, 1)
                dve.wait_ge(o_d, n + 1)
                me.link(nc.vector.reciprocal(sd[:, n % 2], sd[:, n % 2]))
                nc.vector.tensor_tensor(out=oc[:, n % 2], in0=oc[:, n % 2], in1=sd[:, n % 2],
                                        op=ALU.mult).then_inc(o_y, 1)
                dve.wait_ge(o_a, n + 1)
                dve.wait_ge(g_s, 2 * (n % H) + n // H + 1)
                nc.vector.tensor_tensor(out=VO[:, n], in0=oc[:, n % 2], in1=G[:, n], op=ALU.mult).then_inc(o_g, 1)
            dve.wait_ge(g_x, 16)
            for n in range(NT):
                dve.wait_ge(o_p, n + 1)
                nc.vector.tensor_tensor(out=xt2[:, n, :], in0=xt2[:, n, :], in1=PS[:, n % 4, 0:D],
                                        op=ALU.add).then_inc(o_x, 1)

            def norm_stats(r, src):
                for n in range(NT):
                    me.did(nc.vector.bn_stats(stats[:, n, :], src[:, n, :]))
                me.settle()
                for n in range(NT):
                    nc.vector.bn_aggr(mv[:, n, :], stats[:, n, :]).then_inc(x_mv, 1)
                dve.wait_ge(x_sd, r + 1)
                me.link(nc.vector.reciprocal(rstd[:, :], std[:, :]))
                dve.wait_ge(x_mv, NT * (r + 1))

            def keep_xT(r, n, bank):
                dve.wait_ge(x_tp, NT * r + n + 1)
                nc.vector.tensor_copy(xT[:, :, n * P:(n + 1) * P],
                                      PS[:, bank + n % 2, 0:KT * P].rearrange("p (k c) -> p k c", k=KT)).then_inc(x_xT, 1)

            dve.wait_ge(x_ld, 16 * 9)
            dve.wait_ge(x_cst, 6)
            me.link(nc.vector.tensor_scalar(mrow[0:1, :], mrow_i, 0, -MASKED, ALU.not_equal, ALU.mult))
            nc.vector.tensor_scalar(mrow[0:1, :], mrow[0:1, :], MASKED, None, ALU.add).then_inc(x_mk, 1)
            nc.vector.tensor_scalar(mcol[:, :], mcol_i[:, :], 0, None, ALU.not_equal).then_inc(x_mk, 1)
            dve.wait_ge(x_mk, 2)
            dve.wait_ge(o_g, NP)
            nc.vector.tensor_copy(xV[:, :, :, 16:17], mcol[:, :].unsqueeze(2).unsqueeze(3).to_broadcast([P, NT, XH, 1])
                                  ).then_inc(x_mk, 1)
            for n in range(NT):
                dve.wait_ge(x_ct, n + 1)
                nc.vector.tensor_copy(ctxT[:, :, n * P:(n + 1) * P],
                                      PS[:, 6 + n % 2, 0:KT * P].rearrange("p (k c) -> p k c", k=KT)).then_inc(x_cT, 1)
            for n in range(NT):
                dve.wait_ge(x_vp, n + 1)
                nc.vector.tensor_scalar(xV[:, n, :, 0:16], PS[:, 6 + n % 2, 0:D].rearrange("p (h c) -> p h c", h=XH),
                                        mcol[:, n:n + 1], None, ALU.mult).then_inc(x_v, 1)
            dve.wait_ge(o_x, NT)
            norm_stats(0, xt2)
            for n in range(NT):
                wait(dve, x_tp, n - 1)
                nc.vector.tensor_scalar(xn2[:, n % 2], xt2[:, n, :], mv[:, n, 0:1], rstd[:, n:n + 1], ALU.subtract,
                                        ALU.mult).then_inc(x_xn, 1)
                if n > 0:
                    keep_xT(0, n - 1, 6)
            keep_xT(0, NT - 1, 6)
            u = 0
            for n in range(NT):
                w = (n % QT_N + 1) * P
                for g in range(XG):
                    for half in range(2):
                        dve.wait_ge(x_s, u + 1)
                        c0 = 64 * half + 17
                        nc.vector.tensor_reduce(xMx[:, n, g, c0:c0 + 33:32], PS[:, 2 * (u % 3):2 * (u % 3) + 2, 0:w], AX_X,
                                                ALU.max, negate=True).then_inc(x_mx, 1)
                        u += 1
            dve.wait_ge(x_q, B * XG)
            for n in range(NT):
                dve.wait_ge(x_mt, n + 1)
                nc.vector.tensor_tensor(out=xQ2[:, :, n * P:(n + 1) * P], in0=xQT[:, :, n * P:(n + 1) * P],
                                        in1=PS[:, 6 + n % 2, :].rearrange("p (g c) -> p g c", g=XG),
                                        op=ALU.add).then_inc(x_q2, 1)
            for b in range(B):
                for g in range(XG):
                    k = b * XG + g
                    dve.wait_ge(x_pv, k + 1)
                    o4 = PS[:, 6 + g % 2, 0:16 * 17].rearrange("p (i h c) -> p i h c", i=QT_N, h=4)
                    me.link(nc.vector.reciprocal(xsum[:, g % 2].rearrange("p (i h) -> p i h", i=QT_N), o4[:, :, :, 16]))
                    nc.vector.tensor_tensor(
                        out=att[:, b * QT_N:(b + 1) * QT_N, g * 64:(g + 1) * 64].rearrange("p i (h c) -> p i h c", h=4),
                        in0=o4[:, :, :, 0:16], in1=xsum[:, g % 2].rearrange("p (i h) -> p i h", i=QT_N).unsqueeze(3)
                        .to_broadcast([P, QT_N, 4, 16]), op=ALU.mult).then_inc(x_at, 1)
            for n in range(NT):
                dve.wait_ge(x_tt, n + 1)
                nc.vector.tensor_copy(attT[:, :, n * P:(n + 1) * P],
                                      PS[:, 6 + n % 2, 0:KT * P].rearrange("p (k c) -> p k c", k=KT)).then_inc(x_aT, 1)
            for n in range(NT):
                dve.wait_ge(x_op, n + 1)
                nc.vector.tensor_tensor(out=xt2[:, n, :], in0=xt2[:, n, :], in1=PS[:, 4 + n % 2, 0:D],
                                        op=ALU.add).then_inc(x_x, 1)

            dve.wait_ge(f_ld, 64)

            def affine(t, n, y):
                me.link(nc.vector.tensor_tensor(out=t[:, n, :], in0=t[:, n, :], in1=gb[:, y], op=ALU.mult))
                me.link(nc.vector.tensor_tensor(out=t[:, n, :], in0=t[:, n, :], in1=gb[:, y + 1], op=ALU.add))

            norm_stats(1, se)
            for n in range(ET):
                me.link(nc.vector.tensor_scalar(se[:, n, :], se[:, n, :], mv[:, n, 0:1], rstd[:, n:n + 1], ALU.subtract,
                                                ALU.mult))
                affine(se, n, 2)
                nc.vector.tensor_scalar(se[:, n, :], se[:, n, :], scl[:, 0:1], None, ALU.mult).then_inc(f_se, 1)
                if n > 0:
                    dve.wait_ge(f_st, n)
                    nc.vector.tensor_copy(seT[:, :, (n - 1) * P:n * P],
                                          PS[:, 6 + (n - 1) % 2, 0:KT * P].rearrange("p (k c) -> p k c", k=KT)
                                          ).then_inc(f_sT, 1)
            dve.wait_ge(f_st, ET)
            nc.vector.tensor_copy(seT[:, :, (ET - 1) * P:ET * P],
                                  PS[:, 6 + (ET - 1) % 2, 0:KT * P].rearrange("p (k c) -> p k c", k=KT)).then_inc(f_sT, 1)
            dve.wait_ge(x_x, NT)
            norm_stats(2, xt2)
            for n in range(NT):
                me.did(nc.vector.tensor_scalar(xf[:, n, :], xt2[:, n, :], mv[:, n, 0:1], rstd[:, n:n + 1], ALU.subtract,
                                               ALU.mult))
            me.settle()
            norm_stats(3, xf)
            for n in range(NT):
                me.link(nc.vector.tensor_scalar(xf[:, n, :], xf[:, n, :], mv[:, n, 0:1], rstd[:, n:n + 1], ALU.subtract,
                                                ALU.mult))
                me.link(nc.vector.tensor_tensor(out=xf[:, n, :], in0=xf[:, n, :], in1=gb[:, 0], op=ALU.mult))
                nc.vector.tensor_tensor(out=xf[:, n, :], in0=xf[:, n, :], in1=gb[:, 1], op=ALU.add).then_inc(x_xn, 1)
                if n > 0:
                    keep_xT(1, n - 1, 6)
            keep_xT(1, NT - 1, 6)
            for u in range(ET * B):
                e, b = u // B, u % B
                dve.wait_ge(f_lk, u + 1)
                nc.vector.tensor_reduce(mE[:, e, b:b + 1], PS[:, u % 4, :], AX_X, ALU.max, negate=True).then_inc(f_mE, 1)
            for u in range(ET * B):
                e, b = u // B, u % B
                dve.wait_ge(f_fs, u + 1)
                me.link(nc.vector.reciprocal(dE[:, e, b:b + 1], dE[:, e, b:b + 1]))
                nc.vector.tensor_scalar(FS[:, e, b * L:(b + 1) * L], FS[:, e, b * L:(b + 1) * L], dE[:, e, b:b + 1], None,
                                        ALU.mult).then_inc(f_fn, 1)
            for n in range(NT + 1):
                if n < NT:
                    dve.wait_ge(f_lt, n + 1)
                    nc.vector.tensor_reduce(mN[:, n:n + 1], PS[:, 4 + 2 * (n % 2):6 + 2 * (n % 2), :]
                                            .rearrange("p b c -> p (b c)"), AX_X, ALU.max, negate=True).then_inc(f_mN, 1)
                if n == 0:
                    continue
                for half in range(2):
                    v = 2 * (n - 1) + half
                    dve.wait_ge(f_ft, v + 1)
                    nc.vector.tensor_copy(FD[:, n - 1, half * L:(half + 1) * L], PS[:, v % 2, :]).then_inc(f_fk, 1)
                for half in range(2):
                    v = 2 * (n - 1) + half
                    dve.wait_ge(f_eh, v + 1)
                    nc.vector.tensor_copy(EC[:, 4 * half:4 * half + 4, (n - 1) * P:n * P],
                                          PS[:, 2 + v % 2, :].rearrange("p (e c) -> p e c", e=4)).then_inc(f_ek, 1)
            dve.wait_ge(f_e1, NT)
            nc.vector.reciprocal(dN[:, :], dN[:, :]).then_inc(f_dn, 1)

            def experts(i):
                for slot in range(2):
                    wait(dve, w_ld[slot], 64 * (i + 1))
                    dve.wait_ge(w_ge, 2 * i + slot + 1)
                    wait(dve, w_dn, 2 * i + slot - 1)
                    for f in range(FT):
                        ins = nc.vector.scalar_tensor_tensor(
                            out=hT[:, slot, f], in0=PS[:, 2 * slot + 1, f * P:(f + 1) * P],
                            scalar=bgu[:, slot, FT + f:FT + f + 1], in1=gel[:, slot, f], op0=ALU.add, op1=ALU.mult)
                    ins.then_inc(w_h, 1)
                for slot in range(2):
                    dve.wait_ge(w_dn, 2 * i + slot + 1)
                    for b in range(B):
                        nc.vector.tensor_tensor(out=eo[SL * slot:SL * (slot + 1), bass.ds(i, 1), b, :],
                                                in0=PS[SL * b:SL * (b + 1), 4 + slot:5 + slot, 0:D],
                                                in1=bdn[SL * b:SL * (b + 1), slot:slot + 1, :],
                                                op=ALU.add).then_inc(w_eo, 1)

            dve.wait_ge(f_ft, 2 * NT)
            experts(0)
            with dve.Fori(1, E // 2) as i:
                experts(i)
            dve.wait_ge(f_dn, 1)
            for n in range(NT):
                dve.wait_ge(w_cb, n + 1)
                nc.vector.scalar_tensor_tensor(out=xt2[:, n, :], in0=PS[:, 6 + n % 2, 0:D], scalar=dN[:, n:n + 1],
                                               in1=xt2[:, n, :], op0=ALU.mult, op1=ALU.add).then_inc(w_x, 1)


def kernel(**inputs):
    import numpy as np
    import concourse.bacc as bacc
    from concourse.bass_utils import run_bass_kernel_spmd as run

    a = {k: np.ascontiguousarray(v) for k, v in inputs.items()}

    def by_head(w):
        return w.reshape(KT, P, H, P).transpose(2, 1, 0, 3)

    def by_width(w):
        return w.T.reshape(KT, P, D).transpose(1, 0, 2)

    def by_group(w):
        cols = np.zeros((D, XH, 32), w.dtype)
        cols[:, :, :XD] = w.T.reshape(D, XH, XD)
        return cols.reshape(KT, P, XH * 32).transpose(1, 0, 2)

    rows_k = np.zeros((2, 4, 32), np.float32)
    rows_k[0, :, XD] = 1
    rows_k[1, :, XD + 1] = 1
    rows_q = np.zeros((1, 4, 32), np.float32)
    rows_q[0, :, XD] = XD ** 0.5
    rows_k, rows_q = rows_k.reshape(2, P), rows_q.reshape(1, P)

    conv = [np.concatenate([a[f"L0_attn_c{q}w"].reshape(H, P, 4), a[f"L0_attn_c{q}b"].reshape(H, P, 1)], axis=2)
            for q in "qkv"]
    given = {
        "x": a["x"],
        "w_qkva": np.stack([by_head(a[f"L0_attn_W{q}"]) for q in "qkva"], axis=2),
        "conv_pack": np.concatenate(conv + [a["L0_attn_ba"].reshape(H, P, 1)], axis=2),
        "wb": a["L0_attn_Wb"].reshape(KT, P, H).transpose(1, 0, 2),
        "bb": a["L0_attn_bb"].reshape(H, 1),
        "w_gate": by_head(a["L0_attn_Wg"]),
        "w_o": a["L0_attn_Wo"].reshape(H, P, D).transpose(1, 0, 2),
        "ln_gb": np.stack([a["L0_attn_ln_g"], a["L0_attn_ln_b"]], axis=1),
        "ctx_keys": a["ctx_1024"][:, :L].reshape(NT, P, D).transpose(1, 0, 2),
        "mask_rows": a["mask_BxS2_if1"][:, :L].reshape(1, B * L),
        "mask_cols": a["mask_BxS2_if1"][:, :L].reshape(NT, P).T,
        "rows_k": rows_k, "rows_q": rows_q,
        "xa_q": by_group(a["L0_xattn_Wq"]), "xa_k": by_group(a["L0_xattn_Wk"]),
        "xa_v": by_width(a["L0_xattn_Wv"]), "xa_o": by_width(a["L0_xattn_Wo"]),
        "slots": a["L0_ffn_slot_embeds"].reshape(ET, P, D).transpose(1, 0, 2),
        "slot_gb": np.stack([a["L0_ffn_slot_g"], a["L0_ffn_slot_b"]]),
        "norm_gb": np.stack([a["L0_ffn_norm_g"], a["L0_ffn_norm_b"]]),
        "scale": a["L0_ffn_scale"],
        "w_gate_up": np.stack([a[f"L0_ffn_W{q}"].reshape(E, KT, P, F).transpose(0, 2, 1, 3) for q in "gu"], axis=2),
        "w_down": a["L0_ffn_Wd"].reshape(E, FT, P, D).transpose(0, 2, 1, 3),
        "b_gu": np.concatenate([a[f"L0_ffn_b{q}"].reshape(E, FT, P).transpose(0, 2, 1) for q in "gu"], axis=2),
        "b_down": a["L0_ffn_bd"],
    }
    nc = bacc.Bacc("TRN2", target_bir_lowering=False, num_devices=1)
    arrays, args = {}, []
    for name, v in given.items():
        v = np.ascontiguousarray(v)
        arrays[name] = v
        args.append(nc.dram_tensor(name, v.shape, mybir.dt.from_np(v.dtype), kind="ExternalInput").ap())
    out = nc.dram_tensor("out", (B, L, D), F32, kind="ExternalOutput").ap()
    decoder_layer(nc, *args, out)
    return run(nc, [arrays], core_ids=[0]).results[0]["out"]
```

```python
from contextlib import ExitStack

import concourse.bass as bass
from concourse import mybir

F32 = mybir.dt.float32
BF16 = mybir.dt.bfloat16
I32 = mybir.dt.int32
ALU = mybir.AluOpType
ACT = mybir.ActivationFunctionType
AX_X = mybir.AxisListType.X

P = 128
B, L, D = 2, 512, 256
H = 8
NP = B * H
NT = B * L // P
KT = D // P
C = 8
NB = 4
CH = C * NB
NCH = L // CH
XH = 16
XD = D // XH
XG = XH // 4
QT_N = L // P
E, SL, F = 16, 64, 512
ES = E * SL
ET = ES // P
FT = F // P
MASKED = -1e30
EPS = 1e-5
S2 = 1.0 / P

OFF = [0]
for _s in range(C):
    OFF.append(OFF[-1] + NP * (C - _s))
TRI = OFF[C]
BANKS = [(0, 2), (2, 5), (5, 8)]


def wait(eng, sem, value):
    if isinstance(value, int) and value <= 0:
        return
    eng.wait_ge(sem, value)


class Steps:

    def __init__(self, eng, sem):
        self.eng, self.sem, self.start, self.k = eng, sem, 0, 0

    def at(self, start):
        self.start, self.k = start, 0

    def did(self, ins):
        ins.then_inc(self.sem, 1)
        self.k += 1

    def settle(self):
        wait(self.eng, self.sem, self.start + self.k)

    def link(self, ins):
        self.did(ins)
        self.settle()

    def total(self):
        return self.start + self.k


def decoder_layer(nc, x, w_qkva, conv_pack, wb, bb, w_gate, w_o, ln_gb, ctx_keys, mask_rows, mask_cols, rows_k, rows_q,
                  xa_q, xa_k, xa_v, xa_o, slots, slot_gb, norm_gb, scale, w_gate_up, w_down, b_gu, b_down, out):
    ctx = ExitStack()
    with ctx:
        def sb(name, shape, dt=F32):
            return ctx.enter_context(nc.sbuf_tensor(name, shape, dt))

        def sem(name):
            return ctx.enter_context(nc.semaphore(name))

        PS = ctx.enter_context(nc.psum_tensor("PS", [P, 8, 512], F32))
        PSF = PS[:, :, :].rearrange("p b c -> p (b c)")

        ident = sb("ident", [P, P])
        ones = sb("ones", [P, P])
        avg = sb("avg", [P, P])
        eps_col = sb("eps_col", [P, 2])
        xT = sb("xT", [P, KT, B * L])
        stats = sb("stats", [P, NT, 6])
        mv = sb("mv", [P, NT, 2])
        std = sb("std", [P, NT])
        rstd = sb("rstd", [P, NT])
        lngb = sb("lngb", [P, 2])
        bb_sb = sb("bb_sb", [H, 1])
        KQ = sb("KQ", [P, 2, NP, L + 1])
        VO = sb("VO", [P, NP, L])
        A = sb("A", [P, NP, L])
        betaT = sb("betaT", [H, B, L])
        beta_m = sb("beta_m", [H, B, H, CH])
        own = sb("own", [C * NP, NP])
        own_h = sb("own_h", [C * NP, H])
        own_s = sb("own_s", [C * NP, C])

        SCR = 16160
        scratch = sb("scratch", [P, SCR])
        at = [0]

        def cut(n):
            at[0] += n
            assert at[0] <= SCR, at[0]
            return scratch[:, at[0] - n:at[0]]

        xt = cut(NT * D).rearrange("p (n d) -> p n d", n=NT)
        xn = cut(2 * D).rearrange("p (s d) -> p s d", s=2)
        wh = cut(2 * 4 * KT * P).rearrange("p (s q k c) -> p s q k c", s=2, q=4, k=KT)
        cw = cut(2 * 16).rearrange("p (s c) -> p s c", s=2)
        wb_sb = cut(KT * H).rearrange("p (k h) -> p k h", k=KT)
        acc = cut(4 * L).rearrange("p (s t) -> p s t", s=4)
        at[0] = 0
        S = cut(NP * P).rearrange("p (n k) -> p n k", n=NP)
        ST = cut(NP * P).rearrange("p (n k) -> p n k", n=NP)
        KBb = cut(NP * CH).rearrange("p (i n s) -> p i n s", i=NB, n=NP)
        KBz = cut(2 * NB * NP * C).rearrange("p (b i n s) -> p b i n s", b=2, i=NB, n=NP)
        pick = cut(C * P).rearrange("p (s c) -> p s c", s=C)
        GS = [cut(2 * NP * C).rearrange("p (y n t) -> p y n t", y=2, n=NP) for _ in range(2)]
        N = cut(2 * TRI)
        Dt = [cut(TRI) for _ in range(2)]
        Pre = [cut(NP * (C + 1)).rearrange("p (n t) -> p n t", n=NP) for _ in range(2)]
        Suf = [cut(NP * C).rearrange("p (n s) -> p n s", n=NP) for _ in range(2)]
        Far = [cut(NP * (C + 1)).rearrange("p (n t) -> p n t", n=NP) for _ in range(2)]
        R = [cut(NP * 2 * (C + 1)).rearrange("p (n y t) -> p n y t", n=NP, y=2) for _ in range(2)]
        Pr = [cut(H * 2 * (C + 1)) for _ in range(B)]
        Ef = [p.rearrange("p (y h t) -> p y h t", y=2, h=H) for p in Pr]
        Wst = cut(NP * CH).rearrange("p (i n s) -> p i n s", i=NB, n=NP)
        turn = cut(NP * CH).rearrange("p (n s) -> p n s", n=NP)
        WTs = cut(NB * P).rearrange("p (j v) -> p j v", j=NB)
        WTo = cut(4 * P).rearrange("p (g v) -> p g v", g=4)
        KBT = cut(4 * P).rearrange("p (g v) -> p g v", g=4)
        REACH = [(NB - i) * C + 1 for i in range(NB)]
        GM = [cut(H * 2 * n) for n in REACH]
        Z = cut(NP * 2 * (CH + 1)).rearrange("p (n y t) -> p n y t", n=NP, y=2)

        def decays(y, s):
            return Dt[y][:, OFF[s]:OFF[s + 1]].rearrange("p (n t) -> p n t", n=NP)

        def bank_cols(t, g):
            lo, hi = (OFF[c] for c in BANKS[g])
            return t[:, 2 * lo:2 * hi].rearrange("p (y c) -> p y c", y=2)

        G = KQ[:, 0, :, 0:L]
        at[0] = 0
        xt2 = cut(NT * D).rearrange("p (n d) -> p n d", n=NT)
        wg_sb = cut(2 * KT * P).rearrange("p (s k c) -> p s k c", s=2, k=KT)
        wo_sb = cut(H * D).rearrange("p (h n) -> p h n", h=H)
        oc = cut(2 * L).rearrange("p (s t) -> p s t", s=2)
        sq = cut(2 * L).rearrange("p (s t) -> p s t", s=2)
        sd = cut(2 * L).rearrange("p (s t) -> p s t", s=2)

        consts = scratch[:, 15360:15360 + 3 * P // 2].bitcast(BF16)
        identb = consts[:, 0:P]
        late = consts[:, P:2 * P]
        early = consts[:, 2 * P:3 * P]
        ones_row = beta_m[0:1, :, :, :].rearrange("r b h s -> r (b h s)")
        mcol_i = sb("mcol_i", [P, NT], I32)
        mcol = sb("mcol", [P, NT])
        xsum = sb("xsum", [P, 2, 16])
        Af, Vf = (t[:, :, :].rearrange("p n t -> p (n t)") for t in (A, VO))
        Kf = KQ[:, :, :, :].rearrange("p y n t -> p (y n t)")
        rowsk = Af[0:2, 7680:7808]
        rowsq = Af[0:1, 7808:7936]
        mrow_i = Kf[0:1, 14464:15488].bitcast(I32)
        ctxt = Af[:, 0:2048].rearrange("p (n d) -> p n d", n=NT)
        xwq = Af[:, 2048:3072].rearrange("p (k c) -> p k c", k=KT)
        xwk = Af[:, 3072:4096].rearrange("p (k c) -> p k c", k=KT)
        xwv = Af[:, 4096:4608].rearrange("p (k c) -> p k c", k=KT)
        ctxT = Af[:, 5120:7168].rearrange("p (k t) -> p k t", k=KT)
        attT = ctxT
        xwo = Af[:, 7168:7680].rearrange("p (k c) -> p k c", k=KT)
        xKT = Kf[:, 0:4096].rearrange("p (g t) -> p g t", g=XG)
        xQT = Kf[:, 4096:8192].rearrange("p (g t) -> p g t", g=XG)
        xQ2 = Kf[:, 8192:12288].rearrange("p (g t) -> p g t", g=XG)
        xV = Kf[:, 12288:12288 + NT * XH * 17].rearrange("p (n h c) -> p n h c", n=NT, h=XH)
        xMx = scratch[:, 7680:11776].rearrange("p (n g c) -> p n g c", n=NT, g=XG)
        att = scratch[:, 11776:13824].rearrange("p (n d) -> p n d", n=NT)
        mrow = scratch[0:2, 13824:14848]
        xn2 = scratch[:, 14848:15360].rearrange("p (s d) -> p s d", s=2)
        POFF = [0, 4 * 512, 4 * (512 + 384), 4 * (512 + 384 + 256), 4 * 1280]
        PT = [Vf[:, 0:POFF[4]], Af[:, 0:POFF[4]]]

        def probs(buf, j):
            return PT[buf][:, POFF[j]:POFF[j + 1]].rearrange("p (h t) -> p h t", h=4)

        se = Af[:, 0:2048].rearrange("p (n d) -> p n d", n=ET)
        xf = scratch[:, 2048:4096].rearrange("p (n d) -> p n d", n=NT)
        seT = scratch[:, 4096:6144].rearrange("p (k s) -> p k s", k=KT)
        we = scratch[:, 6144:12288].rearrange("p (s w) -> p s w", s=2)
        wgu = [we[:, i, 0:2048].rearrange("p (y k f) -> p y k f", y=2, k=KT) for i in range(2)]
        wdn = [we[:, i, 2048:3072].rearrange("p (f d) -> p f d", f=FT) for i in range(2)]
        hT = scratch[:, 12288:13312].rearrange("p (s f c) -> p s f c", s=2, f=FT)
        gel = scratch[:, 13312:14336].rearrange("p (s f c) -> p s f c", s=2, f=FT)
        bdn = scratch[:, 14336:14848].rearrange("p (s d) -> p s d", s=2)
        bgu = sb("bgu", [P, 2, 2 * FT])
        gb = Af[:, 2048:3072].rearrange("p (y d) -> p y d", y=4)
        scl = sb("scl", [P, 1])
        LG = Kf[:, 0:8192].rearrange("p (e t) -> p e t", e=ET)
        FD = Kf[:, 8192:16384].rearrange("p (n s) -> p n s", n=NT)
        FS = Vf.rearrange("p (e t) -> p e t", e=ET)
        EC = Af.rearrange("p (e t) -> p e t", e=ET)
        E1 = we[:, :, 0:1024]
        slT = Kf[:, 0:4096].rearrange("p (k e c) -> p k e c", k=KT, e=E)
        eo = Vf[:, 0:4096].rearrange("p (e b d) -> p e b d", e=ET, b=B)
        mE = sb("mE", [P, ET, B])
        dE = sb("dE", [P, ET, B])
        mN = sb("mN", [P, NT])
        dN = sb("dN", [P, NT])

        s_x = sem("s_x")
        s_small = sem("s_small")
        s_cst = sem("s_cst")
        s_pool = sem("s_pool")
        s_dve = sem("s_dve")
        s_g0, s_g1 = sem("s_g0"), sem("s_g1")
        s_mv = sem("s_mv")
        s_std = sem("s_std")
        s_xn = sem("s_xn")
        s_xtp = sem("s_xtp")
        s_xT = sem("s_xT")
        s_wh = [sem("s_wh0"), sem("s_wh1")]
        s_bp = sem("s_bp")
        s_bs = sem("s_bs")
        s_beta = sem("s_beta")
        s_pa = sem("s_pa")
        s_sa = sem("s_sa")
        s_pq = sem("s_pq")
        s_pre = sem("s_pre")
        s_conv = sem("s_conv")
        s_silu = sem("s_silu")
        s_init = sem("s_init")
        p_bm = sem("p_bm")
        p_kb = sem("p_kb")
        p_gs = sem("p_gs")
        p_gm = sem("p_gm")
        p_d = sem("p_d")
        p_r = sem("p_r")
        p_ws = sem("p_ws")
        e_bb = sem("e_bb")
        e_g = sem("e_g")
        e_gs = sem("e_gs")
        e_gr = sem("e_gr")
        e_kt = sem("e_kt")
        e_wt = sem("e_wt")
        e_we = sem("e_we")
        e_ap = sem("e_ap")
        e_wo = sem("e_wo")
        e_dl = sem("e_dl")
        e_st = sem("e_st")
        e_z = sem("e_z")
        v_pk = sem("v_pk")
        v_n = sem("v_n")
        v_r = sem("v_r")
        v_w = sem("v_w")
        v_ef = sem("v_ef")
        v_s = sem("v_s")
        a_kt = sem("a_kt")
        a_bb = sem("a_bb")
        a_gs = sem("a_gs")
        a_gm = sem("a_gm")
        a_kz = sem("a_kz")
        a_ks = sem("a_ks")
        a_ws = sem("a_ws")
        a_wt = sem("a_wt")
        a_we = sem("a_we")
        a_o = sem("a_o")
        a_sa = sem("a_sa")
        a_wo = sem("a_wo")
        a_st = sem("a_st")
        a_z = sem("a_z")
        g_ld = [sem("g_ld0"), sem("g_ld1")]
        g_p = sem("g_p")
        g_s = sem("g_s")
        g_wo = sem("g_wo")
        g_x = sem("g_x")
        o_m = sem("o_m")
        o_c = sem("o_c")
        o_q = sem("o_q")
        o_v = sem("o_v")
        o_d = sem("o_d")
        o_y = sem("o_y")
        o_a = sem("o_a")
        o_g = sem("o_g")
        o_p = sem("o_p")
        o_x = sem("o_x")
        s_out = sem("s_out")
        x_ld = sem("x_ld")
        x_cst = sem("x_cst")
        x_mv = sem("x_mv")
        x_sd = sem("x_sd")
        x_xn = sem("x_xn")
        x_tp = sem("x_tp")
        x_xT = sem("x_xT")
        x_mk = sem("x_mk")
        x_ct = sem("x_ct")
        x_cT = sem("x_cT")
        x_kp = sem("x_kp")
        x_k = sem("x_k")
        x_vp = sem("x_vp")
        x_v = sem("x_v")
        x_qp = sem("x_qp")
        x_q = sem("x_q")
        x_s = sem("x_s")
        x_mx = sem("x_mx")
        x_mt = sem("x_mt")
        x_q2 = sem("x_q2")
        x_st = sem("x_st")
        x_e = sem("x_e")
        x_pv = sem("x_pv")
        x_at = sem("x_at")
        x_tt = sem("x_tt")
        x_aT = sem("x_aT")
        x_op = sem("x_op")
        x_x = sem("x_x")
        f_ld = sem("f_ld")
        f_y = sem("f_y")
        f_se = sem("f_se")
        f_st = sem("f_st")
        f_sT = sem("f_sT")
        f_lg = sem("f_lg")
        f_lk = sem("f_lk")
        f_mE = sem("f_mE")
        f_fs = sem("f_fs")
        f_fn = sem("f_fn")
        f_ft = sem("f_ft")
        f_fk = sem("f_fk")
        f_lt = sem("f_lt")
        f_mN = sem("f_mN")
        f_e1 = sem("f_e1")
        f_eh = sem("f_eh")
        f_dn = sem("f_dn")
        f_ek = sem("f_ek")
        f_sp = sem("f_sp")
        f_sk = sem("f_sk")
        w_ld = [sem("w_ld0"), sem("w_ld1")]
        w_gu = sem("w_gu")
        w_ge = sem("w_ge")
        w_h = sem("w_h")
        w_dn = sem("w_dn")
        w_eo = sem("w_eo")
        w_cb = sem("w_cb")
        w_x = sem("w_x")

        x_tiles = x.rearrange("b (i p) d -> p (b i) d", p=P)
        out_tiles = out.rearrange("b (i p) d -> p (b i) d", p=P)
        LB = NB - 1
        STATE_BANKS = (6, 7, 4, 5)

        block = ctx.enter_context(nc.Block())

        @block.sync
        def _(sp):
            sp.dma_start(xt, x_tiles).then_inc(s_x, 16)
            sp.dma_start(wb_sb, wb).then_inc(s_small, 16)
            sp.dma_start(bb_sb[:, :], bb).then_inc(s_small, 16)
            sp.dma_start(lngb[:, :], ln_gb).then_inc(s_small, 16)

            def head_weights(h, slot):
                wait(sp, s_silu, (h - 1) * 6)
                sp.dma_start(wh[:, slot], w_qkva[h]).then_inc(s_wh[slot], 16)
                sp.dma_start(cw[:, slot], conv_pack[h]).then_inc(s_wh[slot], 16)

            head_weights(0, 0)
            head_weights(1, 1)
            with sp.Fori(1, H // 2) as i:
                for slot in range(2):
                    sp.wait_ge(s_silu, 12 * i + (slot - 1) * 6)
                    sp.dma_start(wh[:, slot], w_qkva[bass.ds(2 * i + slot, 1)].rearrange("a p q k c -> p (a q) k c")
                                 ).then_inc(s_wh[slot], 16)
                    sp.dma_start(cw[:, slot], conv_pack[bass.ds(2 * i + slot, 1)].rearrange("a p c -> p (a c)")
                                 ).then_inc(s_wh[slot], 16)
            sp.wait_ge(a_o, 2 * NCH * NB)
            sp.wait_ge(v_w, 2 * NCH * NB)
            sp.dma_start(xt2, x_tiles).then_inc(g_x, 16)
            sp.dma_start(wo_sb, w_o).then_inc(g_wo, 16)
            for h in range(H):
                wait(sp, g_p, 2 * (h - 1))
                sp.dma_start(wg_sb[:, h % 2], w_gate[h]).then_inc(g_ld[h % 2], 16)
            for dst, src in ((ctxt, ctx_keys), (xwk, xa_k), (xwv, xa_v), (xwq, xa_q), (xwo, xa_o), (rowsk, rows_k),
                             (rowsq, rows_q), (mrow_i, mask_rows), (mcol_i[:, :], mask_cols)):
                sp.dma_start(dst, src).then_inc(x_ld, 16)
            sp.wait_ge(x_pv, 2 * XG)
            sp.dma_start(se, slots).then_inc(f_ld, 16)
            sp.dma_start(gb[:, 0:2], norm_gb.partition_broadcast(P)).then_inc(f_ld, 16)
            sp.dma_start(gb[:, 2:4], slot_gb.partition_broadcast(P)).then_inc(f_ld, 16)
            sp.dma_start(scl[:, :], scale.partition_broadcast(P)).then_inc(f_ld, 16)

            def expert(e, slot):
                sp.dma_start(wgu[slot], w_gate_up[bass.ds(e, 1)].rearrange("a p y k f -> p (a y) k f")).then_inc(w_ld[slot], 16)
                sp.dma_start(wdn[slot], w_down[bass.ds(e, 1)].rearrange("a p f d -> p (a f) d")).then_inc(w_ld[slot], 16)
                sp.dma_start(bgu[:, slot], b_gu[bass.ds(e, 1)].rearrange("a p c -> p (a c)")).then_inc(w_ld[slot], 16)
                sp.dma_start(bdn[:, slot], b_down[bass.ds(e, 1), :].rearrange("a d -> (a d)").partition_broadcast(P)
                             ).then_inc(w_ld[slot], 16)

            sp.wait_ge(f_eh, 2 * NT)
            sp.wait_ge(x_x, NT)
            expert(0, 0)
            expert(1, 1)
            with sp.Fori(1, E // 2) as i:
                for slot in range(2):
                    sp.wait_ge(w_eo, 4 * i + 2 * (slot - 1))
                    expert(2 * i + slot, slot)
            sp.wait_ge(w_x, NT)
            sp.dma_start(out_tiles, xt2).then_inc(s_out, 16)
            sp.wait_ge(s_out, 16)

        @block.gpsimd
        def _(pool):
            me = Steps(pool, s_pool)
            nc.gpsimd.memset(ones[:, :], 1.0).then_inc(s_cst, 1)
            nc.gpsimd.memset(avg[:, :], 1.0 / P).then_inc(s_cst, 1)
            nc.gpsimd.memset(eps_col[:, 0:1], EPS).then_inc(s_cst, 1)
            nc.gpsimd.memset(eps_col[:, 1:2], EPS * S2).then_inc(s_cst, 1)
            me.did(nc.gpsimd.memset(ident[:, :], 0.0))
            me.did(nc.gpsimd.memset(own[:, :], -1.0))
            me.settle()
            nc.gpsimd.affine_select(out=ident[:, :], in_=ident[:, :], compare_op=ALU.not_equal, fill=1.0,
                                    base=0, pattern=[[-1, P]], channel_multiplier=1).then_inc(s_cst, 1)
            me.link(nc.gpsimd.affine_select(out=own[:, :], in_=own[:, :], compare_op=ALU.is_ge, fill=0.0,
                                            base=0, pattern=[[-C, NP]], channel_multiplier=1))
            nc.gpsimd.affine_select(out=own[:, :], in_=own[:, :], compare_op=ALU.is_ge, fill=0.0,
                                    base=C - 1, pattern=[[C, NP]], channel_multiplier=-1).then_inc(s_cst, 1)
            pool.wait_ge(s_cst, 6)
            nc.gpsimd.tensor_tensor(out=own_h[:, :], in0=own[:, 0:H], in1=own[:, H:NP], op=ALU.add).then_inc(s_cst, 1)
            nc.gpsimd.memset(KQ[:, 0, :, L:L + 1], 0.0).then_inc(s_cst, 1)
            nc.gpsimd.memset(KQ[:, 1, :, 0:1], 0.0).then_inc(s_cst, 1)
            pool.wait_ge(s_silu, 6 * H)
            pool.wait_ge(s_sa, 2 * H)
            pool.wait_ge(s_bp, 1)
            me.did(nc.gpsimd.memset(KBz, 0.0))
            me.did(nc.gpsimd.memset(GM[0], 0.0))
            me.did(nc.gpsimd.memset(R[0], 0.0))
            for y in range(2):
                me.did(nc.gpsimd.memset(Dt[y], 1.0))
                me.did(nc.gpsimd.memset(Suf[y], 1.0))
                me.did(nc.gpsimd.memset(Pre[y], 1.0))
            me.settle()
            nc.gpsimd.memset(S, 0.0).then_inc(s_init, 1)
            nc.gpsimd.memset(ST, 0.0).then_inc(s_init, 1)
            pool.wait_ge(s_beta, 1)

            def spread_beta(o):
                wait(pool, e_bb, o)
                for b in range(B):
                    ins = nc.gpsimd.tensor_tensor(
                        out=beta_m[:, b], in0=betaT[:, b:b + 1, bass.ds(o * CH, CH)].to_broadcast([H, H, CH]),
                        in1=ident[0:H, 0:H].unsqueeze(2).to_broadcast([H, H, CH]), op=ALU.mult)
                ins.then_inc(p_bm, 1)

            def beta_keys(o):
                wait(pool, a_bb, o + 1)
                by_pair = KBb.rearrange("p i n s -> p n i s")
                nc.gpsimd.tensor_tensor(out=by_pair, in1=by_pair,
                                        in0=KQ[:, 0, :, bass.ds(o * CH, CH)].rearrange("p n (i s) -> p n i s", i=NB),
                                        op=ALU.mult).then_inc(p_kb, 1)

            def decays_of(o, i, first=False):
                m, t0, y = o * NB + i, o * CH + i * C, i % 2

                def a(s, n):
                    return A[:, :, bass.ds(t0 + s, 1)].to_broadcast([P, NP, n])

                wait(pool, p_d, m)
                wait(pool, v_n, m - 1)
                wait(pool, v_w, 2 * (m - 1))
                if i == 1:
                    wait(pool, a_sa, o)
                for s in range(C - 2, -1, -1):
                    me.did(nc.gpsimd.tensor_tensor(out=decays(y, s)[:, :, 1:C - s], in0=decays(y, s + 1),
                                                   in1=a(s + 1, C - 1 - s), op=ALU.mult))
                    me.did(nc.gpsimd.tensor_tensor(out=Suf[y][:, :, s:s + 1], in0=Suf[y][:, :, s + 1:s + 2],
                                                   in1=a(s + 1, 1), op=ALU.mult))
                    me.settle()
                ins = nc.gpsimd.tensor_tensor(out=Pre[y][:, :, 1:C + 1], in0=decays(y, 0), in1=a(0, C), op=ALU.mult)
                if not first:
                    me.link(ins)
                    before = Pre[1 - y] if i == 1 else Far[1 - y]
                    ins = nc.gpsimd.tensor_tensor(out=Far[y], in0=Pre[y],
                                                  in1=before[:, :, C:C + 1].to_broadcast([P, NP, C + 1]), op=ALU.mult)
                ins.then_inc(p_d, 1)

            def own_gram(o, i):
                m, y = o * NB + i, i % 2
                wait(pool, a_gs, m + 1)
                nc.gpsimd.tensor_tensor(out=GS[y], in0=GS[y],
                                        in1=own[:, :].unsqueeze(1).unsqueeze(3).to_broadcast([P, 2, NP, C]),
                                        op=ALU.mult).then_inc(p_gs, 1)

            def later_gram(o, i, last):
                n = REACH[i] - C * last
                wait(pool, a_gm, o * NB + i + 1)
                gm = GM[i][:, 0:2 * H * n].rearrange("p (y h t) -> p y h t", y=2, h=H)
                nc.gpsimd.tensor_tensor(out=gm, in0=gm,
                                        in1=own_h[:, :].unsqueeze(1).unsqueeze(3).to_broadcast([P, 2, H, n]),
                                        op=ALU.mult).then_inc(p_gm, 1)

            def from_state(o, i):
                m, t0, y = o * NB + i, o * CH + i * C, i % 2
                wait(pool, a_z, 4 * o + 4)
                wait(pool, v_w, 2 * (m - 1))
                wait(pool, a_o, 2 * (m - 1))
                wait(pool, p_d, m + 1)
                me.link(nc.gpsimd.tensor_tensor(out=R[y], in0=Z[:, :, :, (i - 1) * C:i * C + 1],
                                                in1=Far[y].unsqueeze(2).to_broadcast([P, NP, 2, C + 1]), op=ALU.mult))
                nc.gpsimd.tensor_tensor(out=R[y][:, :, 0, 0:C], in0=R[y][:, :, 0, 0:C],
                                        in1=VO[:, :, bass.ds(t0, C)], op=ALU.subtract).then_inc(p_r, 1)

            def decay_errors(o, i):
                wait(pool, v_w, 2 * (o * NB + i))
                wait(pool, e_wt, o * NB + i)
                wait(pool, e_we, LB * o + i - 1)
                wait(pool, p_d, o * NB + i + 1)
                me.settle()
                nc.gpsimd.tensor_tensor(
                    out=Wst[:, 0:i], in0=Wst[:, 0:i],
                    in1=Pre[i % 2][:, :, C].unsqueeze(1).unsqueeze(3).to_broadcast([P, i, NP, C]),
                    op=ALU.mult).then_inc(p_ws, 1)

            def chunk(o, last=False):
                if not last:
                    spread_beta(o + 1)
                decays_of(o, 1)
                later_gram(o, 0, last)
                from_state(o, 1)
                own_gram(o, 2)
                later_gram(o, 1, last)

                decay_errors(o, 1)
                decays_of(o, 2)
                from_state(o, 2)
                own_gram(o, 3)
                later_gram(o, 2, last)
                if not last:
                    beta_keys(o + 1)

                decay_errors(o, 2)
                decays_of(o, 3)
                from_state(o, 3)
                if last:
                    return
                own_gram(o + 1, 0)
                later_gram(o, 3, last)

                decay_errors(o, 3)
                decays_of(o + 1, 0)
                from_state(o, 4)
                own_gram(o + 1, 1)

            spread_beta(0)
            beta_keys(0)
            own_gram(0, 0)
            decays_of(0, 0, first=True)
            own_gram(0, 1)
            first = me.total()
            me.at(first)
            chunk(0)
            per = me.k
            second = me.total()
            with pool.Fori(1, NCH - 1) as o:
                me.at(second + (o - 1) * per)
                chunk(o)
                assert me.k == per
            me.at(second + (NCH - 2) * per)
            chunk(NCH - 1, last=True)
            me.at(me.total())
            pool.wait_ge(a_o, 2 * NCH * NB)
            pool.wait_ge(v_w, 2 * NCH * NB)
            me.did(nc.gpsimd.memset(late[:, :], 0.0))
            me.did(nc.gpsimd.memset(early[:, :], 0.0))
            nc.gpsimd.tensor_copy(identb[:, :], ident[:, :]).then_inc(x_cst, 1)
            me.settle()
            nc.gpsimd.affine_select(out=late[:, :], in_=late[:, :], compare_op=ALU.is_ge, fill=MASKED,
                                    base=0, pattern=[[-1, P]], channel_multiplier=1).then_inc(x_cst, 1)
            nc.gpsimd.affine_select(out=early[:, :], in_=early[:, :], compare_op=ALU.is_ge, fill=MASKED,
                                    base=0, pattern=[[1, P]], channel_multiplier=-1).then_inc(x_cst, 1)
            nc.gpsimd.memset(xMx, 0.0).then_inc(x_cst, 1)
            nc.gpsimd.memset(mrow, 1.0).then_inc(x_cst, 1)
            nc.gpsimd.memset(ones_row, 1.0).then_inc(x_cst, 1)

        @block.scalar
        def _(act):
            act.wait_ge(s_cst, 9)
            act.wait_ge(s_mv, NT)
            nc.scalar.activation(std[:, :], mv[:, :, 1], ACT.Sqrt, bias=eps_col[:, 0:1]).then_inc(s_std, 1)
            act.wait_ge(s_small, 48)
            act.wait_ge(s_bp, 1)
            nc.scalar.activation(betaT[:, :, :], PS[0:H, 0:B, :], ACT.Sigmoid, bias=bb_sb[:, 0:1]).then_inc(s_bs, 1)
            act.wait_ge(s_bs, 1)
            nc.scalar.mul(betaT[:, :, :], betaT[:, :, :], S2).then_inc(s_beta, 1)

            def activate(i, u):
                hh, b, q = u // 6, u // 3 % 2, u % 3
                n = b * H + 2 * i + hh
                dst = (KQ[:, 1, bass.ds(n, 1), 1:L + 1], KQ[:, 0, bass.ds(n, 1), 0:L], VO[:, bass.ds(n, 1), :])[q]
                wait(act, s_conv, i * 12 + u + 1)
                nc.scalar.activation(dst, acc[:, u % 4:u % 4 + 1, :], ACT.Silu).then_inc(s_silu, 1)

            def heads(i, load):
                for hh in range(2):
                    wait(act, s_wh[hh], 32 * (i + 1))
                    for b in range(B):
                        wait(act, s_pa, 4 * i + 2 * hh + b + 1)
                        nc.scalar.activation(A[:, bass.ds(b * H + 2 * i + hh, 1), :], PS[:, 6 + b:7 + b, :], ACT.Sigmoid,
                                             bias=cw[:, hh, 15:16]).then_inc(s_sa, 1)
                for u in range(12 + 2):
                    if u < 12:
                        q = u % 3
                        wait(act, s_pq, 12 * i + u + 1)
                        wait(act, s_silu, 12 * i + u - 3)
                        nc.scalar.activation(acc[:, u % 4, :], PS[:, u % 6, :], ACT.Identity,
                                             scale=cw[:, u // 6, 5 * q + 3:5 * q + 4],
                                             bias=cw[:, u // 6, 5 * q + 4:5 * q + 5]).then_inc(s_pre, 1)
                    if u >= 2:
                        activate(i, u - 2)

            heads(0, False)
            with act.Fori(1, H // 2) as i:
                heads(i, True)

            def keys_by_batch(o):
                wait(act, p_kb, o + 1)
                wait(act, e_gr, o * NB)
                for b in range(B):
                    pairs = slice(b * H, (b + 1) * H)
                    ins = nc.scalar.activation(KBz[:, b, :, pairs], KBb[:, :, pairs], ACT.Copy)
                ins.then_inc(a_kz, 1)

            def beta(o):
                wait(act, e_bb, o + 1)
                wait(act, e_gs, o * NB)
                wait(act, a_kz, o)
                wait(act, a_ks, o)
                nc.scalar.activation(KBb.rearrange("p i n s -> p n i s"),
                                     PS[:, 3, :].rearrange("p (n i s) -> p n i s", n=NP, i=NB), ACT.Copy).then_inc(a_bb, 1)

            def own_gram(o, i):
                m, y = o * NB + i, i % 2
                wait(act, e_gs, m + 1)
                wait(act, e_g, m - 1)
                nc.scalar.activation(GS[y], PS[:, 7, 0:2 * NP * C].rearrange("p (y n t) -> p y n t", y=2, n=NP),
                                     ACT.Copy).then_inc(a_gs, 1)

            def later_gram(o, i, last):
                n = REACH[i] - C * last
                wait(act, e_gr, o * NB + i + 1)
                wait(act, e_ap, o * 2 * NB)
                if 2 * H * n <= 512:
                    nc.scalar.activation(GM[i][:, 0:2 * H * n], PS[:, 3, 0:2 * H * n], ACT.Copy).then_inc(a_gm, 1)
                else:
                    for q in range(2):
                        ins = nc.scalar.activation(
                            GM[i].rearrange("p (y h t) -> p y h t", y=2, h=H)[:, q:q + 1, :, q:q + n - 1],
                            PS[:, 3, q * 256:(q + 1) * 256].rearrange("p (y h t) -> p y h t", y=1, h=H), ACT.Copy)
                    ins.then_inc(a_gm, 1)

            def by_pair(dst, src):
                return nc.scalar.activation(dst.rearrange("p n (i s) -> p n i s", i=NB), src.rearrange("p i n s -> p n i s"),
                                            ACT.Copy)

            def errors_turned(o, i):
                m, t0, y = o * NB + i, o * CH + i * C, i % 2
                wait(act, e_wt, m + 1)
                wait(act, e_ap, o * 2 * NB)
                nc.scalar.activation(WTs[:, i], PS[:, 6, 3 * P:4 * P], ACT.Copy).then_inc(a_wt, 1)

            def outputs(o, i):
                m, t0, y = o * NB + i, o * CH + i * C, i % 2
                for b in range(B):
                    wait(act, v_r, 2 * m + b + 1)
                    nc.scalar.activation(VO[:, b * H:(b + 1) * H, bass.ds(t0, C)], R[y][:, b * H:(b + 1) * H, 1, 1:C + 1],
                                         ACT.Copy).then_inc(a_o, 1)

            def earlier_turned(o, i):
                wait(act, e_we, LB * o + i)
                wait(act, e_ap, 2 * (o * NB + i))
                nc.scalar.activation(WTs[:, 0:i], PS[:, 6, 0:i * P].rearrange("p (j v) -> p j v", j=i),
                                     ACT.Copy).then_inc(a_we, 1)

            def chunk(o, first=False, last=False):
                if not first:
                    wait(act, v_w, 2 * NB * o)
                    wait(act, p_ws, LB * o)
                    wait(act, e_kt, o)
                    by_pair(turn, Wst).then_inc(a_ws, 1)
                    wait(act, e_wo, o)
                    nc.scalar.activation(WTo, PS[:, 3, :].rearrange("p (g k) -> p g k", g=4), ACT.Copy).then_inc(a_wo, 1)
                if not last:
                    wait(act, p_kb, o + 1)
                    by_pair(turn, KBb).then_inc(a_ks, 1)
                    wait(act, e_kt, o + 1)
                    wait(act, e_dl, 4 * o)
                    nc.scalar.activation(KBT, PS[:, 3, :].rearrange("p (g k) -> p g k", g=4), ACT.Copy,
                                         scale=-1.0).then_inc(a_kt, 1)
                if not first:
                    for u in range(4):
                        wait(act, e_st, 4 * (o - 1) + u + 1)
                        wait(act, e_z, 4 * o)
                        nc.scalar.activation(ST[:, u:NP:4], PS[:, STATE_BANKS[u], :].rearrange("p (n k) -> p n k", n=4),
                                             ACT.Copy).then_inc(a_st, 1)
                later_gram(o, 0, last)
                n = CH + 1 - C * last
                for u in range(4):
                    wait(act, e_z, 4 * o + u + 1)
                    wait(act, p_r, NB * o)
                    nc.scalar.activation(Z[:, 4 * u:4 * u + 4, :, 0:n],
                                         PS[:, STATE_BANKS[u], 0:8 * n].rearrange("p (n y t) -> p n y t", n=4, y=2),
                                         ACT.Copy).then_inc(a_z, 1)
                own_gram(o, 2)
                later_gram(o, 1, last)
                errors_turned(o, 0)
                outputs(o, 0)

                own_gram(o, 3)
                later_gram(o, 2, last)
                if not last:
                    beta(o + 1)
                earlier_turned(o, 1)
                errors_turned(o, 1)
                outputs(o, 1)

                if not last:
                    own_gram(o + 1, 0)
                    later_gram(o, 3, last)
                earlier_turned(o, 2)
                errors_turned(o, 2)
                outputs(o, 2)
                if last:
                    outputs(o, NB - 1)
                    return
                wait(act, p_d, NB * (o + 1))
                wait(act, e_st, 4 * o)
                wait(act, v_s, 4 * o)
                act.wait_ge(s_init, 2)
                for n in range(NP):
                    ins = nc.scalar.activation(S[:, n], S[:, n], ACT.Copy, scale=Far[1][:, n, C:C + 1])
                ins.then_inc(a_sa, 1)
                own_gram(o + 1, 1)
                earlier_turned(o, 3)
                keys_by_batch(o + 1)
                errors_turned(o, 3)
                outputs(o, 3)

            act.wait_ge(s_init, 2)
            beta(0)
            own_gram(0, 0)
            own_gram(0, 1)
            keys_by_batch(0)
            chunk(0, first=True)
            with act.Fori(1, NCH - 1) as o:
                chunk(o)
            chunk(NCH - 1, last=True)

            for h in range(H):
                for b in range(B):
                    act.wait_ge(g_p, 2 * h + b + 1)
                    nc.scalar.activation(G[:, b * H + h], PS[:, 2 * (h % 2) + b, :], ACT.Sigmoid).then_inc(g_s, 1)
            for n in range(NP):
                act.wait_ge(o_c, n + 1)
                wait(act, o_v, n - 1)
                nc.scalar.activation(sq[:, n % 2], oc[:, n % 2], ACT.Square).then_inc(o_q, 1)
                act.wait_ge(o_v, n + 1)
                wait(act, o_y, n - 1)
                nc.scalar.activation(sd[:, n % 2], PS[:, 6 + n % 2, :], ACT.Sqrt, bias=eps_col[:, 1:2]).then_inc(o_d, 1)
                act.wait_ge(o_y, n + 1)
                nc.scalar.activation(oc[:, n % 2], oc[:, n % 2], ACT.Identity, scale=lngb[:, 0:1],
                                     bias=lngb[:, 1:2]).then_inc(o_a, 1)

            def norm_std(r):
                act.wait_ge(x_mv, NT * (r + 1))
                nc.scalar.activation(std[:, :], mv[:, :, 1], ACT.Sqrt, bias=eps_col[:, 0:1]).then_inc(x_sd, 1)

            act.wait_ge(o_g, NP)
            for u in range(B * XG):
                g, b = u % XG, u // XG
                act.wait_ge(x_kp, u + 1)
                nc.scalar.activation(xKT[:, g, b * L:(b + 1) * L], PS[:, 4 + u % 2, :], ACT.Copy).then_inc(x_k, 1)
            norm_std(0)
            for u in range(B * XG):
                g, b = u % XG, u // XG
                act.wait_ge(x_qp, u + 1)
                nc.scalar.activation(xQT[:, g, b * L:(b + 1) * L], PS[:, 4 + u % 2, :], ACT.Copy,
                                     scale=XD ** -0.5).then_inc(x_q, 1)
            u = 0
            for b in range(B):
                for g in range(XG):
                    if b * XG + g >= 2:
                        act.wait_ge(x_pv, b * XG + g - 1)
                    for j in range(QT_N):
                        for half in range(2):
                            act.wait_ge(x_st, u + 1)
                            n = L - j * P
                            nc.scalar.activation(probs(g % 2, j)[:, 2 * half:2 * half + 2], PS[:, 2 * (u % 3):2 * (u % 3) + 2, 0:n],
                                                 ACT.Exp).then_inc(x_e, 1)
                            u += 1
            norm_std(1)
            norm_std(2)
            norm_std(3)
            for u in range(ET * B):
                e, b = u // B, u % B
                act.wait_ge(f_lg, u + 1)
                nc.scalar.activation(LG[:, e, b * L:(b + 1) * L], PS[:, u % 4, :], ACT.Copy).then_inc(f_lk, 1)
                act.wait_ge(f_mE, u + 1)
                nc.scalar.activation(FS[:, e, b * L:(b + 1) * L], PS[:, u % 4, :], ACT.Exp, bias=mE[:, e, b:b + 1],
                                     accum_out=dE[:, e, b:b + 1]).then_inc(f_fs, 1)
            for n in range(NT):
                act.wait_ge(f_mN, n + 1)
                wait(act, f_eh, 2 * (n - 1))
                nc.scalar.activation(E1[:, n % 2], PS[:, 4 + 2 * (n % 2):6 + 2 * (n % 2), :].rearrange("p b c -> p (b c)"),
                                     ACT.Exp, bias=mN[:, n:n + 1], accum_out=dN[:, n:n + 1]).then_inc(f_e1, 1)
            act.wait_ge(f_lt, NT)
            for u in range(2 * B * KT):
                b, k, half = u // 4, u // 2 % 2, u % 2
                act.wait_ge(f_sp, u + 1)
                nc.scalar.activation(slT[:, k, half * 8:(half + 1) * 8, b * SL:(b + 1) * SL],
                                     PS[:, u % 2, :].rearrange("p (e s) -> p e s", e=8), ACT.Copy).then_inc(f_sk, 1)

            def experts(i):
                for slot in range(2):
                    act.wait_ge(w_ld[slot], 64 * (i + 1))
                    act.wait_ge(w_gu, 2 * i + slot + 1)
                    wait(act, w_h, 2 * i + slot - 1)
                    for f in range(FT):
                        ins = nc.scalar.activation(gel[:, slot, f], PS[:, 2 * slot, f * P:(f + 1) * P], ACT.Gelu,
                                                   bias=bgu[:, slot, f:f + 1])
                    ins.then_inc(w_ge, 1)

            experts(0)
            with act.Fori(1, E // 2) as i:
                experts(i)

        @block.tensor
        def _(pe):
            pe.wait_ge(s_cst, 9)
            for n in range(NT):
                pe.wait_ge(s_xn, n + 1)
                wait(pe, s_xT, n - 1)
                for k in range(KT):
                    ins = nc.tensor.transpose(PS[:, 6 + n % 2, k * P:(k + 1) * P], xn[:, n % 2, k * P:(k + 1) * P],
                                              ident[:, :])
                ins.then_inc(s_xtp, 1)
            pe.wait_ge(s_xT, NT)
            pe.wait_ge(s_small, 48)
            for b in range(B):
                for k in range(KT):
                    ins = nc.tensor.matmul(PS[0:H, b, :], wb_sb[:, k, :], xT[:, k, b * L:(b + 1) * L],
                                           start=(k == 0), stop=(k == KT - 1))
            ins.then_inc(s_bp, 1)

            def heads(i, first):
                for hh in range(2):
                    wait(pe, s_wh[hh], 32 * (i + 1))
                    for b in range(B):
                        if not (first and hh == 0):
                            wait(pe, s_sa, 4 * i + 2 * hh + b - 1)
                        for k in range(KT):
                            ins = nc.tensor.matmul(PS[:, 6 + b, :], wh[:, hh, 3, k, :], xT[:, k, b * L:(b + 1) * L],
                                                   start=(k == 0), stop=(k == KT - 1))
                        ins.then_inc(s_pa, 1)
                if first:
                    pe.wait_ge(s_bs, 1)
                for u in range(12):
                    hh, b, q = u // 6, u // 3 % 2, u % 3
                    wait(pe, s_conv, 12 * i + u - 5)
                    for k in range(KT):
                        ins = nc.tensor.matmul(PS[:, u % 6, :], wh[:, hh, q, k, :], xT[:, k, b * L:(b + 1) * L],
                                               start=(k == 0), stop=(k == KT - 1))
                    ins.then_inc(s_pq, 1)

            heads(0, True)
            with pe.Fori(1, H // 2) as i:
                heads(i, False)

            def beta_all(o):
                wait(pe, p_bm, o + 1)
                if not isinstance(o, int) or o > 0:
                    wait(pe, a_gm, (o - 1) * NB + 3)
                nc.tensor.matmul(PS[:, 3, :], ones[0:H, :], beta_m[:, :, :, :].rearrange("r b h s -> r (b h s)"),
                                 start=True, stop=True).then_inc(e_bb, 1)

            def own_gram(o, i):
                m = o * NB + i
                wait(pe, p_kb, o + 1)
                wait(pe, a_gs, m)
                if i == 2:
                    wait(pe, a_z, 4 * o + 4)
                nc.tensor.matmul(PS[:, 7, 0:2 * NP * C].rearrange("p (y n t) -> p y n t", y=2, n=NP),
                                 KBb[:, i].rearrange("p n s -> p (n s)"), KQ[:, :, :, bass.ds(o * CH + i * C + 1, C)],
                                 start=True, stop=True).then_inc(e_gs, 1)

            def later_gram(o, i, last):
                n = REACH[i] - C * last
                t0 = o * CH + (i + 1) * C
                wait(pe, a_kz, o + 1)
                wait(pe, a_gm, o * NB + i)
                if i == 0:
                    if last:
                        wait(pe, a_wo, o)
                    else:
                        wait(pe, a_kt, o + 1)
                if i == 3:
                    wait(pe, a_bb, o + 2)
                if 2 * H * n <= 512:
                    for b in range(B):
                        ins = nc.tensor.matmul(
                            PS[:, 3, 0:2 * H * n].rearrange("p (y h t) -> p y h t", y=2, h=H),
                            KBz[:, b, i].rearrange("p n s -> p (n s)"),
                            KQ[:, :, b * H:(b + 1) * H, bass.ds(t0, n)], start=(b == 0), stop=(b == B - 1))
                else:
                    for q in range(2):
                        for b in range(B):
                            ins = nc.tensor.matmul(
                                PS[:, 3, q * 256:(q + 1) * 256].rearrange("p (h t) -> p h t", h=H),
                                KBz[:, b, i].rearrange("p n s -> p (n s)"),
                                KQ[:, q, b * H:(b + 1) * H, bass.ds(t0 + q, n - 1)], start=(b == 0), stop=(b == B - 1),
                                skip_group_check=True)
                ins.then_inc(e_gr, 1)

            def dots(o, i):
                m, y = o * NB + i, i % 2
                wait(pe, p_gs, m + 1)
                wait(pe, v_n, m)
                for g, (s0, s1) in enumerate(BANKS):
                    width = OFF[s1] - OFF[s0]
                    for s in range(s0, s1):
                        ins = nc.tensor.matmul(
                            PS[:, g, 0:2 * width].rearrange("p (y c) -> p y c", y=2)[:, :, OFF[s] - OFF[s0]:OFF[s + 1] - OFF[s0]]
                            .rearrange("p y (n t) -> p y n t", n=NP),
                            pick[:, s, :], GS[y][:, :, :, s:C], start=True, stop=True)
                ins.then_inc(e_g, 1)

            def effects(o, i, last):
                m = o * NB + i
                if i > 0:
                    wait(pe, p_ws, LB * o + i)
                    wait(pe, a_wt, m)
                    for j in range(i):
                        ins = nc.tensor.transpose(PS[:, 6, j * P:(j + 1) * P],
                                                  Wst[:, j].rearrange("p n s -> p (n s)"), ident[:, :])
                    ins.then_inc(e_we, 1)
                for j in range(i + 1):
                    if j == 0:
                        wait(pe, v_ef, 2 * m)
                        wait(pe, a_z, 4 * o + 4)
                    if j == i:
                        wait(pe, v_w, 2 * m + 2)
                        if i > 0:
                            wait(pe, a_we, LB * o + i)
                        nc.tensor.transpose(PS[:, 6, 3 * P:4 * P], Wst[:, i].rearrange("p n s -> p (n s)"),
                                            ident[:, :]).then_inc(e_wt, 1)
                        wait(pe, a_wt, m + 1)
                        wait(pe, p_gm, m + 1)
                    else:
                        wait(pe, a_we, LB * o + i)
                    n = REACH[j] - C * last
                    for b in range(B):
                        rows = slice(C * H * b, C * H * (b + 1))
                        later = GM[j][rows, 0:2 * H * n].rearrange("p (y h t) -> p y h t", y=2, h=H)
                        ins = nc.tensor.matmul(
                            PS[:, 4 + b, 0:2 * H * (C + 1)].rearrange("p (y h t) -> p y h t", y=2, h=H), WTs[rows, j, :],
                            later[:, :, :, (i - j) * C:(i - j + 1) * C + 1], start=(j == 0), stop=(j == i),
                            tile_position=(C * H * b, 0), skip_group_check=True)
                        if j == i:
                            ins.then_inc(e_ap, 1)

            def chunk(o, first=False, last=False):
                if not first:
                    wait(pe, a_ws, o)
                    wait(pe, a_gm, NB * o)
                    for g in range(4):
                        ins = nc.tensor.transpose(PS[:, 3, g * P:(g + 1) * P],
                                                  turn[:, 4 * g:4 * g + 4, :].rearrange("p n s -> p (n s)"), ident[:, :])
                    ins.then_inc(e_wo, 1)
                dots(o, 1)
                wait(pe, a_gs, NB * o + 2)
                wait(pe, a_wt, NB * o)
                wait(pe, v_ef, 2 * NB * o)
                if not first:
                    wait(pe, a_wo, o)
                    wait(pe, a_kt, o)
                    for u in range(4):
                        for j in range(4):
                            ins = nc.tensor.matmul(PS[:, STATE_BANKS[u], j * P:(j + 1) * P],
                                                   WTo[CH * u:CH * (u + 1), j, :], KBT[CH * u:CH * (u + 1), j, :],
                                                   start=True, stop=True, tile_position=(CH * u, 0))
                        ins.then_inc(e_dl, 1)
                if not last:
                    wait(pe, a_ks, o + 1)
                    wait(pe, a_wo, o)
                    for g in range(4):
                        ins = nc.tensor.transpose(PS[:, 3, g * P:(g + 1) * P],
                                                  turn[:, 4 * g:4 * g + 4, :].rearrange("p n s -> p (n s)"), ident[:, :])
                    ins.then_inc(e_kt, 1)
                if not first:
                    for u in range(4):
                        wait(pe, v_s, 4 * (o - 1) + u + 1)
                        for j in range(4):
                            ins = nc.tensor.transpose(PS[:, STATE_BANKS[u], j * P:(j + 1) * P], S[:, 4 * j + u, :],
                                                      ident[:, :])
                        ins.then_inc(e_st, 1)
                later_gram(o, 0, last)
                n = CH + 1 - C * last
                wait(pe, a_st, 4 * o)
                for u in range(4):
                    for j in range(4):
                        pair = 4 * u + j
                        ins = nc.tensor.matmul(
                            PS[:, STATE_BANKS[u], j * 2 * n:(j + 1) * 2 * n].rearrange("p (y t) -> p y t", y=2),
                            ST[:, pair], KQ[:, :, pair, bass.ds(o * CH + C, n)], start=True, stop=True)
                    ins.then_inc(e_z, 1)
                own_gram(o, 2)
                later_gram(o, 1, last)
                effects(o, 0, last)

                dots(o, 2)
                own_gram(o, 3)
                later_gram(o, 2, last)
                if not last:
                    beta_all(o + 1)
                effects(o, 1, last)

                dots(o, 3)
                if not last:
                    own_gram(o + 1, 0)
                    later_gram(o, 3, last)
                effects(o, 2, last)
                if last:
                    return
                dots(o + 1, 0)
                own_gram(o + 1, 1)
                effects(o, 3, last)

            pe.wait_ge(s_beta, 1)
            pe.wait_ge(s_conv, 6 * H)
            pe.wait_ge(s_silu, 6 * H)
            pe.wait_ge(s_sa, 2 * H)
            pe.wait_ge(s_init, 2)
            beta_all(0)
            own_gram(0, 0)
            pe.wait_ge(v_pk, 1)
            dots(0, 0)
            own_gram(0, 1)
            chunk(0, first=True)
            with pe.Fori(1, NCH - 1) as o:
                chunk(o)
            chunk(NCH - 1, last=True)

            pe.wait_ge(a_o, 2 * NCH * NB)
            for h in range(H):
                pe.wait_ge(g_ld[h % 2], 16 * (h // 2 + 1))
                for b in range(B):
                    wait(pe, g_s, 2 * h + b - 3)
                    for k in range(KT):
                        ins = nc.tensor.matmul(PS[:, 2 * (h % 2) + b, :], wg_sb[:, h % 2, k, :], xT[:, k, b * L:(b + 1) * L],
                                               start=(k == 0), stop=(k == KT - 1))
                    ins.then_inc(g_p, 1)
            for n in range(NP):
                wait(pe, o_c, n - 1)
                nc.tensor.matmul(PS[:, 4 + n % 2, :], avg[:, :], VO[:, n], start=True, stop=True).then_inc(o_m, 1)
                pe.wait_ge(o_q, n + 1)
                wait(pe, o_d, n - 1)
                nc.tensor.matmul(PS[:, 6 + n % 2, :], avg[:, :], sq[:, n % 2], start=True, stop=True).then_inc(o_v, 1)
            pe.wait_ge(g_wo, 16)
            pe.wait_ge(o_g, NP)
            for n in range(NT):
                b, i = n // (NT // B), n % (NT // B)
                wait(pe, o_x, n - 3)
                for h in range(H):
                    ins = nc.tensor.matmul(PS[:, n % 4, 0:D], VO[:, b * H + h, i * P:(i + 1) * P], wo_sb[:, h, :],
                                           start=(h == 0), stop=(h == H - 1))
                ins.then_inc(o_p, 1)

            pe.wait_ge(x_cst, 6)
            pe.wait_ge(x_ld, 16 * 9)
            for n in range(NT):
                wait(pe, x_cT, n - 1)
                for k in range(KT):
                    ins = nc.tensor.transpose(PS[:, 6 + n % 2, k * P:(k + 1) * P], ctxt[:, n, k * P:(k + 1) * P],
                                              ident[:, :])
                ins.then_inc(x_ct, 1)
            pe.wait_ge(x_cT, NT)
            pe.wait_ge(x_mk, 3)
            for u in range(B * XG):
                g, b = u % XG, u // XG
                wait(pe, x_k, u - 1)
                for k in range(KT):
                    nc.tensor.matmul(PS[:, 4 + u % 2, :], xwk[:, k, g * P:(g + 1) * P], ctxT[:, k, b * L:(b + 1) * L],
                                     start=(k == 0), stop=False)
                nc.tensor.matmul(PS[:, 4 + u % 2, :], rowsk, mrow[:, b * L:(b + 1) * L], start=False,
                                 stop=True).then_inc(x_kp, 1)
            for n in range(NT):
                wait(pe, x_v, n - 1)
                for k in range(KT):
                    ins = nc.tensor.matmul(PS[:, 6 + n % 2, 0:D], ctxT[:, k, n * P:(n + 1) * P], xwv[:, k, :],
                                           start=(k == 0), stop=(k == KT - 1))
                ins.then_inc(x_vp, 1)

            def transpose_x(r, bank):
                for n in range(NT):
                    pe.wait_ge(x_xn, NT * r + n + 1)
                    wait(pe, x_xT, NT * r + n - 1)
                    for k in range(KT):
                        ins = nc.tensor.transpose(PS[:, bank + n % 2, k * P:(k + 1) * P],
                                                  (xn2[:, n % 2] if r == 0 else xf[:, n])[:, k * P:(k + 1) * P], ident[:, :])
                    ins.then_inc(x_tp, 1)
                pe.wait_ge(x_xT, NT * (r + 1))

            pe.wait_ge(x_v, NT)
            transpose_x(0, 6)
            pe.wait_ge(x_k, B * XG)
            for u in range(B * XG):
                g, b = u % XG, u // XG
                wait(pe, x_q, u - 1)
                for k in range(KT):
                    nc.tensor.matmul(PS[:, 4 + u % 2, :], xwq[:, k, g * P:(g + 1) * P], xT[:, k, b * L:(b + 1) * L],
                                     start=(k == 0), stop=False)
                nc.tensor.matmul(PS[:, 4 + u % 2, :], rowsq, ones_row, start=False, stop=True).then_inc(x_qp, 1)
            pe.wait_ge(x_q, B * XG)
            u = 0
            for n in range(NT):
                b, i = n // QT_N, n % QT_N
                w = (i + 1) * P
                for g in range(XG):
                    for half in range(2):
                        wait(pe, x_mx, u - 2)
                        for j in range(2):
                            h, bank = 2 * half + j, 2 * (u % 3) + j
                            nc.tensor.matmul(PS[:, bank, i * P:w], identb[:, :], late[:, :], start=True, stop=True)
                            if i:
                                nc.tensor.matmul(PS[:, bank, 0:i * P], xQT[32 * h:32 * h + 32, g, n * P:(n + 1) * P],
                                                 xKT[32 * h:32 * h + 32, g, b * L:b * L + i * P], start=False, stop=True,
                                                 tile_position=(32 * h, 0), skip_group_check=True)
                            ins = nc.tensor.matmul(PS[:, bank, i * P:w], xQT[32 * h:32 * h + 32, g, n * P:(n + 1) * P],
                                                   xKT[32 * h:32 * h + 32, g, b * L + i * P:b * L + w], start=False,
                                                   stop=True, tile_position=(32 * h, 0), skip_group_check=True)
                        ins.then_inc(x_s, 1)
                        u += 1
            for n in range(NT):
                pe.wait_ge(x_mx, 8 * (n + 1))
                wait(pe, x_q2, n - 1)
                for g in range(XG):
                    ins = nc.tensor.transpose(PS[:, 6 + n % 2, g * P:(g + 1) * P], xMx[:, n, g, :], ident[:, :])
                ins.then_inc(x_mt, 1)
            pe.wait_ge(x_q2, NT)
            u = 0
            for b in range(B):
                for g in range(XG):
                    for j in range(QT_N):
                        w = L - j * P
                        for half in range(2):
                            wait(pe, x_e, u - 2)
                            for hh in range(2):
                                h, bank = 2 * half + hh, 2 * (u % 3) + hh
                                nc.tensor.matmul(PS[:, bank, 0:P], identb[:, :], early[:, :], start=True, stop=True)
                                ins = nc.tensor.matmul(PS[:, bank, 0:w],
                                                       xKT[32 * h:32 * h + 32, g, b * L + j * P:b * L + (j + 1) * P],
                                                       xQ2[32 * h:32 * h + 32, g, b * L + j * P:(b + 1) * L], start=False,
                                                       stop=True, tile_position=(32 * h, 0), skip_group_check=True)
                            ins.then_inc(x_st, 1)
                            u += 1
                    pe.wait_ge(x_e, u)
                    wait(pe, x_at, b * XG + g - 1)
                    for i in range(QT_N):
                        for h in range(4):
                            c0 = (i * 4 + h) * 17
                            for j in range(i + 1):
                                ins = nc.tensor.matmul(PS[:, 6 + g % 2, c0:c0 + 17],
                                                       probs(g % 2, j)[:, h, (i - j) * P:(i - j + 1) * P],
                                                       xV[:, b * QT_N + j, 4 * g + h, :], start=(j == 0), stop=(j == i))
                    ins.then_inc(x_pv, 1)
            pe.wait_ge(x_at, 2 * XG)
            for n in range(NT):
                wait(pe, x_aT, n - 1)
                for k in range(KT):
                    ins = nc.tensor.transpose(PS[:, 6 + n % 2, k * P:(k + 1) * P], att[:, n, k * P:(k + 1) * P], ident[:, :])
                ins.then_inc(x_tt, 1)
            for n in range(NT):
                pe.wait_ge(x_aT, n + 1)
                wait(pe, x_x, n - 1)
                for k in range(KT):
                    ins = nc.tensor.matmul(PS[:, 4 + n % 2, 0:D], attT[:, k, n * P:(n + 1) * P], xwo[:, k, :],
                                           start=(k == 0), stop=(k == KT - 1))
                ins.then_inc(x_op, 1)

            for n in range(ET):
                pe.wait_ge(f_se, n + 1)
                wait(pe, f_sT, n - 1)
                for k in range(KT):
                    ins = nc.tensor.transpose(PS[:, 6 + n % 2, k * P:(k + 1) * P], se[:, n, k * P:(k + 1) * P], ident[:, :])
                ins.then_inc(f_st, 1)
            pe.wait_ge(f_sT, ET)
            transpose_x(1, 6)
            for u in range(ET * B):
                e, b = u // B, u % B
                wait(pe, f_fs, u - 3)
                wait(pe, f_mE, u - 3)
                for k in range(KT):
                    ins = nc.tensor.matmul(PS[:, u % 4, :], seT[:, k, e * P:(e + 1) * P], xT[:, k, b * L:(b + 1) * L],
                                           start=(k == 0), stop=(k == KT - 1))
                ins.then_inc(f_lg, 1)
            pe.wait_ge(f_lk, ET * B)

            def logits_turned(n):
                wait(pe, f_e1, n - 1)
                wait(pe, f_mN, n - 1)
                for e in range(ET):
                    ins = nc.tensor.transpose(PS[:, 4 + 2 * (n % 2) + e // 4, (e % 4) * P:(e % 4 + 1) * P],
                                              LG[:, e, n * P:(n + 1) * P], ident[:, :])
                ins.then_inc(f_lt, 1)

            logits_turned(0)
            pe.wait_ge(f_fs, ET * B)
            for n in range(NT):
                if n + 1 < NT:
                    logits_turned(n + 1)
                for half in range(2):
                    v = 2 * n + half
                    wait(pe, f_fk, v - 1)
                    pe.wait_ge(f_fn, 8 * half + 8)
                    for e in range(4):
                        ins = nc.tensor.transpose(PS[:, v % 2, e * P:(e + 1) * P], FS[:, 4 * half + e, n * P:(n + 1) * P],
                                                  ident[:, :])
                    ins.then_inc(f_ft, 1)
                pe.wait_ge(f_e1, n + 1)
                for half in range(2):
                    v = 2 * n + half
                    wait(pe, f_ek, v - 1)
                    for e in range(4):
                        c0 = (4 * half + e) * P
                        ins = nc.tensor.transpose(PS[:, 2 + v % 2, e * P:(e + 1) * P], E1[:, n % 2, c0:c0 + P], ident[:, :])
                    ins.then_inc(f_eh, 1)
            pe.wait_ge(f_fk, 2 * NT)
            for u in range(2 * B * KT):
                b, k, half = u // 4, u // 2 % 2, u % 2
                wait(pe, f_sk, u - 1)
                for j in range(QT_N):
                    n = b * QT_N + j
                    ins = nc.tensor.matmul(PS[:, u % 2, :], xf[:, n, k * P:(k + 1) * P], FD[:, n, half * L:(half + 1) * L],
                                           start=(j == 0), stop=(j == QT_N - 1))
                ins.then_inc(f_sp, 1)
            pe.wait_ge(f_sk, 2 * B * KT)
            pe.wait_ge(f_ek, 2 * NT)

            def gate_up(i, slot):
                e = 2 * i + slot
                wait(pe, w_ld[slot], 64 * (i + 1))
                wait(pe, w_ge, e - 1)
                wait(pe, w_h, e - 1)
                for y in range(2):
                    for f in range(FT):
                        for k in range(KT):
                            ins = nc.tensor.matmul(PS[:, 2 * slot + y, f * P:(f + 1) * P],
                                                   wgu[slot][:, y, k, f * P:(f + 1) * P],
                                                   slT[:, k, bass.ds(e, 1), :].rearrange("p e c -> p (e c)"),
                                                   start=(k == 0), stop=(k == KT - 1))
                ins.then_inc(w_gu, 1)

            def down(i, slot):
                e = 2 * i + slot
                wait(pe, w_h, e + 1)
                wait(pe, w_eo, 2 * (e - 1))
                for f in range(FT):
                    ins = nc.tensor.matmul(PS[:, 4 + slot, 0:D], hT[:, slot, f], wdn[slot][:, f, :], start=(f == 0),
                                           stop=(f == FT - 1))
                ins.then_inc(w_dn, 1)

            def experts(i):
                gate_up(i, 0)
                gate_up(i, 1)
                down(i, 0)
                down(i, 1)

            experts(0)
            with pe.Fori(1, E // 2) as i:
                experts(i)
            for n in range(NT):
                b = n // QT_N
                pe.wait_ge(w_eo, 2 * E)
                wait(pe, w_x, n - 1)
                for e in range(ET):
                    ins = nc.tensor.matmul(PS[:, 6 + n % 2, 0:D], EC[:, e, n * P:(n + 1) * P], eo[:, e, b, :],
                                           start=(e == 0), stop=(e == ET - 1))
                ins.then_inc(w_cb, 1)

        @block.vector
        def _(dve):
            me = Steps(dve, s_dve)
            dve.wait_ge(s_x, 16)
            for n in range(NT):
                me.did(nc.vector.bn_stats(stats[:, n, :], xt[:, n, :]))
            me.settle()
            for n in range(NT):
                nc.vector.bn_aggr(mv[:, n, :], stats[:, n, :]).then_inc(s_mv, 1)
            dve.wait_ge(s_std, 1)
            me.link(nc.vector.reciprocal(rstd[:, :], std[:, :]))
            dve.wait_ge(s_mv, NT)
            for n in range(NT):
                wait(dve, s_xtp, n - 1)
                nc.vector.tensor_scalar(xn[:, n % 2], xt[:, n, :], mv[:, n, 0:1], rstd[:, n:n + 1], ALU.subtract,
                                        ALU.mult).then_inc(s_xn, 1)
                if n > 0:
                    dve.wait_ge(s_xtp, n)
                    nc.vector.tensor_copy(xT[:, :, (n - 1) * P:n * P],
                                          PS[:, 6 + (n - 1) % 2, 0:KT * P].rearrange("p (k c) -> p k c", k=KT)
                                          ).then_inc(s_xT, 1)
            dve.wait_ge(s_xtp, NT)
            nc.vector.tensor_copy(xT[:, :, (NT - 1) * P:NT * P],
                                  PS[:, 6 + (NT - 1) % 2, 0:KT * P].rearrange("p (k c) -> p k c", k=KT)).then_inc(s_xT, 1)

            def heads(i):
                for u in range(12):
                    hh, q = u // 6, u % 3
                    wait(dve, s_pre, 12 * i + u + 1)
                    for j in range(1, 4):
                        ins = nc.vector.scalar_tensor_tensor(
                            out=acc[:, u % 4, j:L], in0=PS[:, u % 6, 0:L - j], scalar=cw[:, hh, 5 * q + 3 - j:5 * q + 4 - j],
                            in1=acc[:, u % 4, j:L], op0=ALU.mult, op1=ALU.add)
                        if j < 3:
                            me.link(ins)
                    ins.then_inc(s_conv, 1)

            base = me.total()
            me.at(base)
            heads(0)
            per = me.k
            second = me.total()
            with dve.Fori(1, H // 2) as i:
                me.at(second + (i - 1) * per)
                heads(i)
            me.at(second + (H // 2 - 1) * per)

            own_steps = [Steps(dve, s_g0), Steps(dve, s_g1)]
            STATE_AFTER = (2, 4, 5, 6)

            def decayed_dots(o, i):
                m, y = o * NB + i, i % 2
                wait(dve, e_g, m + 1)
                wait(dve, p_d, m + 1)
                for g, (s0, s1) in enumerate(BANKS):
                    width = OFF[s1] - OFF[s0]
                    ins = nc.vector.tensor_tensor(
                        out=bank_cols(N, g), in0=PS[:, g, 0:2 * width].rearrange("p (y c) -> p y c", y=2),
                        in1=Dt[y][:, OFF[s0]:OFF[s1]].unsqueeze(1).to_broadcast([P, 2, width]), op=ALU.mult)
                ins.then_inc(v_n, 1)

            def state_step(o, u):
                wait(dve, a_sa, o + 1)
                wait(dve, e_dl, 4 * o + u + 1)
                nc.vector.tensor_tensor(out=S[:, u:NP:4], in0=S[:, u:NP:4],
                                        in1=PS[:, STATE_BANKS[u], :].rearrange("p (n k) -> p n k", n=4),
                                        op=ALU.add).then_inc(v_s, 1)

            def solve(o, i, first=False):
                m, t0, y = o * NB + i, o * CH + i * C, i % 2
                r = [R[y][:, b * H:(b + 1) * H] for b in range(B)]
                wait(dve, p_d, m + 1)
                if first:
                    for b, st in enumerate(own_steps):
                        st.did(nc.vector.tensor_scalar(r[b][:, :, 0, 0:C], VO[:, b * H:(b + 1) * H, bass.ds(t0, C)], -1.0,
                                                       None, ALU.mult))
                else:
                    wait(dve, p_r, m)
                    for b, st in enumerate(own_steps):
                        wait(dve, e_ap, 2 * (m - 1) + b + 1)
                        nc.vector.tensor_tensor(
                            out=Ef[b], in0=PS[:, 4 + b, 0:2 * H * (C + 1)].rearrange("p (y h t) -> p y h t", y=2, h=H),
                            in1=Pre[y][:, b * H:(b + 1) * H].unsqueeze(1).to_broadcast([P, 2, H, C + 1]),
                            op=ALU.mult).then_inc(v_ef, 1)
                    for b, st in enumerate(own_steps):
                        wait(dve, v_ef, 2 * (m - 1) + b + 1)
                        st.did(nc.vector.tensor_tensor(out=r[b], in0=r[b], in1=Ef[b].rearrange("p y h t -> p h y t"),
                                                       op=ALU.add))
                dve.wait_ge(v_n, m + 1)
                for s in range(C):
                    n = C - s
                    g = [s0 <= s < s1 for s0, s1 in BANKS].index(True)
                    c0 = OFF[s] - OFF[BANKS[g][0]]
                    for b, st in enumerate(own_steps):
                        st.settle()
                        cols = bank_cols(N, g)[:, :, c0 + b * H * n:c0 + (b + 1) * H * n]
                        st.did(nc.vector.tensor_tensor(
                            out=Pr[b][:, 0:2 * H * n].rearrange("p (y h t) -> p y h t", y=2, h=H),
                            in0=cols.rearrange("p y (h t) -> p y h t", h=H),
                            in1=r[b][:, :, 0, s:s + 1].unsqueeze(1).to_broadcast([P, 2, H, n]), op=ALU.mult))
                    for b, st in enumerate(own_steps):
                        st.settle()
                        dst = r[b][:, :, :, s + 1:C + 1].rearrange("p h y t -> p y h t")
                        ins = nc.vector.tensor_tensor(
                            out=dst, in0=dst, in1=Pr[b][:, 0:2 * H * n].rearrange("p (y h t) -> p y h t", y=2, h=H),
                            op=ALU.subtract)
                        if s < C - 1:
                            st.did(ins)
                        else:
                            ins.then_inc(v_r, 1)
                    if i == 0 and not first and s in STATE_AFTER:
                        state_step(o - 1, STATE_AFTER.index(s))
                if i == 0:
                    wait(dve, a_ws, o)
                    wait(dve, e_we, LB * o)
                    wait(dve, e_wt, NB * o)
                for b in range(B):
                    dve.wait_ge(v_r, 2 * m + b + 1)
                    nc.vector.tensor_tensor(out=Wst[:, i, b * H:(b + 1) * H], in0=r[b][:, :, 0, 0:C],
                                            in1=Suf[y][:, b * H:(b + 1) * H], op=ALU.mult).then_inc(v_w, 1)

            def chunk(o, first=False, last=False):
                for i in range(NB):
                    solve(o, i, first and i == 0)
                    if i < NB - 1:
                        decayed_dots(o, i + 1)
                if not last:
                    decayed_dots(o + 1, 0)

            dve.wait_ge(s_silu, 6 * H)
            dve.wait_ge(s_cst, 9)
            dve.wait_ge(s_init, 2)
            me.link(nc.vector.tensor_reduce(own_s[:, :], ident[:, :].rearrange("p (n s) -> p s n", n=NP), AX_X, ALU.add,
                                            negate=True))
            nc.vector.tensor_copy(pick, own_s[:, :].unsqueeze(2).to_broadcast([P, C, P])).then_inc(v_pk, 1)
            decayed_dots(0, 0)
            chunk(0, first=True)
            first_steps = [st.total() for st in own_steps]
            per = [2 * C * NB] * B
            with dve.Fori(1, NCH - 1) as o:
                for st, k, k0 in zip(own_steps, per, first_steps):
                    st.at(k0 + (o - 1) * k)
                chunk(o)
                assert [st.k for st in own_steps] == per
            for st, k, k0 in zip(own_steps, per, first_steps):
                st.at(k0 + (NCH - 2) * k)
            chunk(NCH - 1, last=True)

            for n in range(NP):
                dve.wait_ge(o_m, n + 1)
                wait(dve, o_g, n - 1)
                nc.vector.tensor_tensor(out=oc[:, n % 2], in0=VO[:, n], in1=PS[:, 4 + n % 2, :],
                                        op=ALU.subtract).then_inc(o_c, 1)
                dve.wait_ge(o_d, n + 1)
                me.link(nc.vector.reciprocal(sd[:, n % 2], sd[:, n % 2]))
                nc.vector.tensor_tensor(out=oc[:, n % 2], in0=oc[:, n % 2], in1=sd[:, n % 2],
                                        op=ALU.mult).then_inc(o_y, 1)
                dve.wait_ge(o_a, n + 1)
                dve.wait_ge(g_s, 2 * (n % H) + n // H + 1)
                nc.vector.tensor_tensor(out=VO[:, n], in0=oc[:, n % 2], in1=G[:, n], op=ALU.mult).then_inc(o_g, 1)
            dve.wait_ge(g_x, 16)
            for n in range(NT):
                dve.wait_ge(o_p, n + 1)
                nc.vector.tensor_tensor(out=xt2[:, n, :], in0=xt2[:, n, :], in1=PS[:, n % 4, 0:D],
                                        op=ALU.add).then_inc(o_x, 1)

            def norm_stats(r, src):
                for n in range(NT):
                    me.did(nc.vector.bn_stats(stats[:, n, :], src[:, n, :]))
                me.settle()
                for n in range(NT):
                    nc.vector.bn_aggr(mv[:, n, :], stats[:, n, :]).then_inc(x_mv, 1)
                dve.wait_ge(x_sd, r + 1)
                me.link(nc.vector.reciprocal(rstd[:, :], std[:, :]))
                dve.wait_ge(x_mv, NT * (r + 1))

            def keep_xT(r, n, bank):
                dve.wait_ge(x_tp, NT * r + n + 1)
                nc.vector.tensor_copy(xT[:, :, n * P:(n + 1) * P],
                                      PS[:, bank + n % 2, 0:KT * P].rearrange("p (k c) -> p k c", k=KT)).then_inc(x_xT, 1)

            dve.wait_ge(x_ld, 16 * 9)
            dve.wait_ge(x_cst, 6)
            me.link(nc.vector.tensor_scalar(mrow[0:1, :], mrow_i, 0, -MASKED, ALU.not_equal, ALU.mult))
            nc.vector.tensor_scalar(mrow[0:1, :], mrow[0:1, :], MASKED, None, ALU.add).then_inc(x_mk, 1)
            nc.vector.tensor_scalar(mcol[:, :], mcol_i[:, :], 0, None, ALU.not_equal).then_inc(x_mk, 1)
            dve.wait_ge(x_mk, 2)
            dve.wait_ge(o_g, NP)
            nc.vector.tensor_copy(xV[:, :, :, 16:17], mcol[:, :].unsqueeze(2).unsqueeze(3).to_broadcast([P, NT, XH, 1])
                                  ).then_inc(x_mk, 1)
            for n in range(NT):
                dve.wait_ge(x_ct, n + 1)
                nc.vector.tensor_copy(ctxT[:, :, n * P:(n + 1) * P],
                                      PS[:, 6 + n % 2, 0:KT * P].rearrange("p (k c) -> p k c", k=KT)).then_inc(x_cT, 1)
            for n in range(NT):
                dve.wait_ge(x_vp, n + 1)
                nc.vector.tensor_scalar(xV[:, n, :, 0:16], PS[:, 6 + n % 2, 0:D].rearrange("p (h c) -> p h c", h=XH),
                                        mcol[:, n:n + 1], None, ALU.mult).then_inc(x_v, 1)
            dve.wait_ge(o_x, NT)
            norm_stats(0, xt2)
            for n in range(NT):
                wait(dve, x_tp, n - 1)
                nc.vector.tensor_scalar(xn2[:, n % 2], xt2[:, n, :], mv[:, n, 0:1], rstd[:, n:n + 1], ALU.subtract,
                                        ALU.mult).then_inc(x_xn, 1)
                if n > 0:
                    keep_xT(0, n - 1, 6)
            keep_xT(0, NT - 1, 6)
            u = 0
            for n in range(NT):
                w = (n % QT_N + 1) * P
                for g in range(XG):
                    for half in range(2):
                        dve.wait_ge(x_s, u + 1)
                        c0 = 64 * half + 17
                        nc.vector.tensor_reduce(xMx[:, n, g, c0:c0 + 33:32], PS[:, 2 * (u % 3):2 * (u % 3) + 2, 0:w], AX_X,
                                                ALU.max, negate=True).then_inc(x_mx, 1)
                        u += 1
            dve.wait_ge(x_q, B * XG)
            for n in range(NT):
                dve.wait_ge(x_mt, n + 1)
                nc.vector.tensor_tensor(out=xQ2[:, :, n * P:(n + 1) * P], in0=xQT[:, :, n * P:(n + 1) * P],
                                        in1=PS[:, 6 + n % 2, :].rearrange("p (g c) -> p g c", g=XG),
                                        op=ALU.add).then_inc(x_q2, 1)
            for b in range(B):
                for g in range(XG):
                    k = b * XG + g
                    dve.wait_ge(x_pv, k + 1)
                    o4 = PS[:, 6 + g % 2, 0:16 * 17].rearrange("p (i h c) -> p i h c", i=QT_N, h=4)
                    me.link(nc.vector.reciprocal(xsum[:, g % 2].rearrange("p (i h) -> p i h", i=QT_N), o4[:, :, :, 16]))
                    nc.vector.tensor_tensor(
                        out=att[:, b * QT_N:(b + 1) * QT_N, g * 64:(g + 1) * 64].rearrange("p i (h c) -> p i h c", h=4),
                        in0=o4[:, :, :, 0:16], in1=xsum[:, g % 2].rearrange("p (i h) -> p i h", i=QT_N).unsqueeze(3)
                        .to_broadcast([P, QT_N, 4, 16]), op=ALU.mult).then_inc(x_at, 1)
            for n in range(NT):
                dve.wait_ge(x_tt, n + 1)
                nc.vector.tensor_copy(attT[:, :, n * P:(n + 1) * P],
                                      PS[:, 6 + n % 2, 0:KT * P].rearrange("p (k c) -> p k c", k=KT)).then_inc(x_aT, 1)
            for n in range(NT):
                dve.wait_ge(x_op, n + 1)
                nc.vector.tensor_tensor(out=xt2[:, n, :], in0=xt2[:, n, :], in1=PS[:, 4 + n % 2, 0:D],
                                        op=ALU.add).then_inc(x_x, 1)

            dve.wait_ge(f_ld, 64)

            def affine(t, n, y):
                me.link(nc.vector.tensor_tensor(out=t[:, n, :], in0=t[:, n, :], in1=gb[:, y], op=ALU.mult))
                me.link(nc.vector.tensor_tensor(out=t[:, n, :], in0=t[:, n, :], in1=gb[:, y + 1], op=ALU.add))

            norm_stats(1, se)
            for n in range(ET):
                me.link(nc.vector.tensor_scalar(se[:, n, :], se[:, n, :], mv[:, n, 0:1], rstd[:, n:n + 1], ALU.subtract,
                                                ALU.mult))
                affine(se, n, 2)
                nc.vector.tensor_scalar(se[:, n, :], se[:, n, :], scl[:, 0:1], None, ALU.mult).then_inc(f_se, 1)
                if n > 0:
                    dve.wait_ge(f_st, n)
                    nc.vector.tensor_copy(seT[:, :, (n - 1) * P:n * P],
                                          PS[:, 6 + (n - 1) % 2, 0:KT * P].rearrange("p (k c) -> p k c", k=KT)
                                          ).then_inc(f_sT, 1)
            dve.wait_ge(f_st, ET)
            nc.vector.tensor_copy(seT[:, :, (ET - 1) * P:ET * P],
                                  PS[:, 6 + (ET - 1) % 2, 0:KT * P].rearrange("p (k c) -> p k c", k=KT)).then_inc(f_sT, 1)
            dve.wait_ge(x_x, NT)
            norm_stats(2, xt2)
            for n in range(NT):
                me.did(nc.vector.tensor_scalar(xf[:, n, :], xt2[:, n, :], mv[:, n, 0:1], rstd[:, n:n + 1], ALU.subtract,
                                               ALU.mult))
            me.settle()
            norm_stats(3, xf)
            for n in range(NT):
                me.link(nc.vector.tensor_scalar(xf[:, n, :], xf[:, n, :], mv[:, n, 0:1], rstd[:, n:n + 1], ALU.subtract,
                                                ALU.mult))
                me.link(nc.vector.tensor_tensor(out=xf[:, n, :], in0=xf[:, n, :], in1=gb[:, 0], op=ALU.mult))
                nc.vector.tensor_tensor(out=xf[:, n, :], in0=xf[:, n, :], in1=gb[:, 1], op=ALU.add).then_inc(x_xn, 1)
                if n > 0:
                    keep_xT(1, n - 1, 6)
            keep_xT(1, NT - 1, 6)
            for u in range(ET * B):
                e, b = u // B, u % B
                dve.wait_ge(f_lk, u + 1)
                nc.vector.tensor_reduce(mE[:, e, b:b + 1], PS[:, u % 4, :], AX_X, ALU.max, negate=True).then_inc(f_mE, 1)
            for u in range(ET * B):
                e, b = u // B, u % B
                dve.wait_ge(f_fs, u + 1)
                me.link(nc.vector.reciprocal(dE[:, e, b:b + 1], dE[:, e, b:b + 1]))
                nc.vector.tensor_scalar(FS[:, e, b * L:(b + 1) * L], FS[:, e, b * L:(b + 1) * L], dE[:, e, b:b + 1], None,
                                        ALU.mult).then_inc(f_fn, 1)
            for n in range(NT + 1):
                if n < NT:
                    dve.wait_ge(f_lt, n + 1)
                    nc.vector.tensor_reduce(mN[:, n:n + 1], PS[:, 4 + 2 * (n % 2):6 + 2 * (n % 2), :]
                                            .rearrange("p b c -> p (b c)"), AX_X, ALU.max, negate=True).then_inc(f_mN, 1)
                if n == 0:
                    continue
                for half in range(2):
                    v = 2 * (n - 1) + half
                    dve.wait_ge(f_ft, v + 1)
                    nc.vector.tensor_copy(FD[:, n - 1, half * L:(half + 1) * L], PS[:, v % 2, :]).then_inc(f_fk, 1)
                for half in range(2):
                    v = 2 * (n - 1) + half
                    dve.wait_ge(f_eh, v + 1)
                    nc.vector.tensor_copy(EC[:, 4 * half:4 * half + 4, (n - 1) * P:n * P],
                                          PS[:, 2 + v % 2, :].rearrange("p (e c) -> p e c", e=4)).then_inc(f_ek, 1)
            dve.wait_ge(f_e1, NT)
            nc.vector.reciprocal(dN[:, :], dN[:, :]).then_inc(f_dn, 1)

            def experts(i):
                for slot in range(2):
                    wait(dve, w_ld[slot], 64 * (i + 1))
                    dve.wait_ge(w_ge, 2 * i + slot + 1)
                    wait(dve, w_dn, 2 * i + slot - 1)
                    for f in range(FT):
                        ins = nc.vector.scalar_tensor_tensor(
                            out=hT[:, slot, f], in0=PS[:, 2 * slot + 1, f * P:(f + 1) * P],
                            scalar=bgu[:, slot, FT + f:FT + f + 1], in1=gel[:, slot, f], op0=ALU.add, op1=ALU.mult)
                    ins.then_inc(w_h, 1)
                for slot in range(2):
                    dve.wait_ge(w_dn, 2 * i + slot + 1)
                    for b in range(B):
                        nc.vector.tensor_tensor(out=eo[SL * slot:SL * (slot + 1), bass.ds(i, 1), b, :],
                                                in0=PS[SL * b:SL * (b + 1), 4 + slot:5 + slot, 0:D],
                                                in1=bdn[SL * b:SL * (b + 1), slot:slot + 1, :],
                                                op=ALU.add).then_inc(w_eo, 1)

            dve.wait_ge(f_ft, 2 * NT)
            experts(0)
            with dve.Fori(1, E // 2) as i:
                experts(i)
            dve.wait_ge(f_dn, 1)
            for n in range(NT):
                dve.wait_ge(w_cb, n + 1)
                nc.vector.scalar_tensor_tensor(out=xt2[:, n, :], in0=PS[:, 6 + n % 2, 0:D], scalar=dN[:, n:n + 1],
                                               in1=xt2[:, n, :], op0=ALU.mult, op1=ALU.add).then_inc(w_x, 1)


def kernel(**inputs):
    import numpy as np
    import concourse.bacc as bacc
    from concourse.bass_utils import run_bass_kernel_spmd as run

    a = {k: np.ascontiguousarray(v) for k, v in inputs.items()}

    def by_head(w):
        return w.reshape(KT, P, H, P).transpose(2, 1, 0, 3)

    def by_width(w):
        return w.T.reshape(KT, P, D).transpose(1, 0, 2)

    def by_group(w):
        cols = np.zeros((D, XH, 32), w.dtype)
        cols[:, :, :XD] = w.T.reshape(D, XH, XD)
        return cols.reshape(KT, P, XH * 32).transpose(1, 0, 2)

    rows_k = np.zeros((2, 4, 32), np.float32)
    rows_k[0, :, XD] = 1
    rows_k[1, :, XD + 1] = 1
    rows_q = np.zeros((1, 4, 32), np.float32)
    rows_q[0, :, XD] = XD ** 0.5
    rows_k, rows_q = rows_k.reshape(2, P), rows_q.reshape(1, P)

    conv = [np.concatenate([a[f"L0_attn_c{q}w"].reshape(H, P, 4), a[f"L0_attn_c{q}b"].reshape(H, P, 1)], axis=2)
            for q in "qkv"]
    given = {
        "x": a["x"],
        "w_qkva": np.stack([by_head(a[f"L0_attn_W{q}"]) for q in "qkva"], axis=2),
        "conv_pack": np.concatenate(conv + [a["L0_attn_ba"].reshape(H, P, 1)], axis=2),
        "wb": a["L0_attn_Wb"].reshape(KT, P, H).transpose(1, 0, 2),
        "bb": a["L0_attn_bb"].reshape(H, 1),
        "w_gate": by_head(a["L0_attn_Wg"]),
        "w_o": a["L0_attn_Wo"].reshape(H, P, D).transpose(1, 0, 2),
        "ln_gb": np.stack([a["L0_attn_ln_g"], a["L0_attn_ln_b"]], axis=1),
        "ctx_keys": a["ctx_1024"][:, :L].reshape(NT, P, D).transpose(1, 0, 2),
        "mask_rows": a["mask_BxS2_if1"][:, :L].reshape(1, B * L),
        "mask_cols": a["mask_BxS2_if1"][:, :L].reshape(NT, P).T,
        "rows_k": rows_k, "rows_q": rows_q,
        "xa_q": by_group(a["L0_xattn_Wq"]), "xa_k": by_group(a["L0_xattn_Wk"]),
        "xa_v": by_width(a["L0_xattn_Wv"]), "xa_o": by_width(a["L0_xattn_Wo"]),
        "slots": a["L0_ffn_slot_embeds"].reshape(ET, P, D).transpose(1, 0, 2),
        "slot_gb": np.stack([a["L0_ffn_slot_g"], a["L0_ffn_slot_b"]]),
        "norm_gb": np.stack([a["L0_ffn_norm_g"], a["L0_ffn_norm_b"]]),
        "scale": a["L0_ffn_scale"],
        "w_gate_up": np.stack([a[f"L0_ffn_W{q}"].reshape(E, KT, P, F).transpose(0, 2, 1, 3) for q in "gu"], axis=2),
        "w_down": a["L0_ffn_Wd"].reshape(E, FT, P, D).transpose(0, 2, 1, 3),
        "b_gu": np.concatenate([a[f"L0_ffn_b{q}"].reshape(E, FT, P).transpose(0, 2, 1) for q in "gu"], axis=2),
        "b_down": a["L0_ffn_bd"],
    }
    nc = bacc.Bacc("TRN2", target_bir_lowering=False, num_devices=1)
    arrays, args = {}, []
    for name, v in given.items():
        v = np.ascontiguousarray(v)
        arrays[name] = v
        args.append(nc.dram_tensor(name, v.shape, mybir.dt.from_np(v.dtype), kind="ExternalInput").ap())
    out = nc.dram_tensor("out", (B, L, D), F32, kind="ExternalOutput").ap()
    decoder_layer(nc, *args, out)
    return run(nc, [arrays], core_ids=[0]).results[0]["out"]
```

```python
from contextlib import ExitStack

import concourse.bass as bass
from concourse import mybir

F32 = mybir.dt.float32
BF16 = mybir.dt.bfloat16
I32 = mybir.dt.int32
ALU = mybir.AluOpType
ACT = mybir.ActivationFunctionType
AX_X = mybir.AxisListType.X

P = 128
B, L, D = 2, 512, 256
H = 8
NP = B * H
NT = B * L // P
KT = D // P
C = 8
NB = 4
CH = C * NB
NCH = L // CH
XH = 16
XD = D // XH
XG = XH // 4
QT_N = L // P
E, SL, F = 16, 64, 512
ES = E * SL
ET = ES // P
FT = F // P
WS = 4
MASKED = -1e30
EPS = 1e-5
S2 = 1.0 / P

OFF = [0]
for _s in range(C):
    OFF.append(OFF[-1] + NP * (C - _s))
TRI = OFF[C]
BANKS = [(0, 2), (2, 5), (5, 8)]


def wait(eng, sem, value):
    if isinstance(value, int) and value <= 0:
        return
    eng.wait_ge(sem, value)


class Steps:

    def __init__(self, eng, sem):
        self.eng, self.sem, self.start, self.k = eng, sem, 0, 0

    def at(self, start):
        self.start, self.k = start, 0

    def did(self, ins):
        ins.then_inc(self.sem, 1)
        self.k += 1

    def settle(self):
        wait(self.eng, self.sem, self.start + self.k)

    def link(self, ins):
        self.did(ins)
        self.settle()

    def total(self):
        return self.start + self.k


def decoder_layer(nc, x, w_qkva, conv_pack, wb, bb, w_gate, w_o, ln_gb, ctx_keys, mask_cols,
                  xa_q, xa_kv, xa_o, slots, slot_gb, norm_gb, scale, w_gate_up, w_down, b_gu, b_down, out):
    ctx = ExitStack()
    with ctx:
        def sb(name, shape, dt=F32):
            return ctx.enter_context(nc.sbuf_tensor(name, shape, dt))

        def sem(name):
            return ctx.enter_context(nc.semaphore(name))

        PS = ctx.enter_context(nc.psum_tensor("PS", [P, 8, 512], F32))

        ident = sb("ident", [P, P])
        ones = sb("ones", [P, P])
        avg = sb("avg", [P, P])
        eps_col = sb("eps_col", [P, 2])
        xT = sb("xT", [P, KT, B * L])
        stats = sb("stats", [P, NT, 6])
        mv = sb("mv", [P, NT, 2])
        std = sb("std", [P, NT])
        rstd = sb("rstd", [P, NT])
        lngb = sb("lngb", [P, 2])
        bb_sb = sb("bb_sb", [H, 1])
        KQ = sb("KQ", [P, 2, NP, L + 1])
        VO = sb("VO", [P, NP, L])
        A = sb("A", [P, NP, L])
        betaT = sb("betaT", [H, B, L])
        beta_m = sb("beta_m", [H, B, H, CH])
        own = sb("own", [C * NP, NP])
        own_h = sb("own_h", [C * NP, H])
        own_s = sb("own_s", [C * NP, C])

        SCR = 16160
        scratch = sb("scratch", [P, SCR])
        at = [0]

        def cut(n):
            at[0] += n
            assert at[0] <= SCR, at[0]
            return scratch[:, at[0] - n:at[0]]

        xt = cut(NT * D).rearrange("p (n d) -> p n d", n=NT)
        xn = cut(2 * D).rearrange("p (s d) -> p s d", s=2)
        wh = cut(2 * 4 * KT * P).rearrange("p (s q k c) -> p s q k c", s=2, q=4, k=KT)
        cw = cut(2 * 16).rearrange("p (s c) -> p s c", s=2)
        wb_sb = cut(KT * H).rearrange("p (k h) -> p k h", k=KT)
        acc = cut(4 * L).rearrange("p (s t) -> p s t", s=4)
        projections_end = at[0]
        at[0] = 0
        S = cut(NP * P).rearrange("p (n k) -> p n k", n=NP)
        ST = cut(NP * P).rearrange("p (n k) -> p n k", n=NP)
        KBb = cut(NP * CH).rearrange("p (i n s) -> p i n s", i=NB, n=NP)
        KBz = cut(2 * NB * NP * C).rearrange("p (b i n s) -> p b i n s", b=2, i=NB, n=NP)
        pick = cut(C * P).rearrange("p (s c) -> p s c", s=C)
        GS = [cut(2 * NP * C).rearrange("p (y n t) -> p y n t", y=2, n=NP) for _ in range(2)]
        N = cut(2 * TRI)
        assert at[0] >= projections_end
        Dt = [cut(TRI) for _ in range(2)]
        Pre = [cut(NP * (C + 1)).rearrange("p (n t) -> p n t", n=NP) for _ in range(2)]
        Suf = [cut(NP * C).rearrange("p (n s) -> p n s", n=NP) for _ in range(2)]
        Far = [cut(NP * (C + 1)).rearrange("p (n t) -> p n t", n=NP) for _ in range(2)]
        R = [cut(NP * 2 * (C + 1)).rearrange("p (n y t) -> p n y t", n=NP, y=2) for _ in range(2)]
        Pr = [cut(H * 2 * (C + 1)) for _ in range(B)]
        Ef = [p.rearrange("p (y h t) -> p y h t", y=2, h=H) for p in Pr]
        Wst = cut(NP * CH).rearrange("p (i n s) -> p i n s", i=NB, n=NP)
        turn = cut(NP * CH).rearrange("p (n s) -> p n s", n=NP)
        WTs = cut(NB * P).rearrange("p (j v) -> p j v", j=NB)
        WTo = cut(4 * P).rearrange("p (g v) -> p g v", g=4)
        KBT = cut(4 * P).rearrange("p (g v) -> p g v", g=4)
        REACH = [(NB - i) * C + 1 for i in range(NB)]
        GM = [cut(H * 2 * n) for n in REACH]
        Z = cut(NP * 2 * (CH + 1)).rearrange("p (n y t) -> p n y t", n=NP, y=2)

        def decays(y, s):
            return Dt[y][:, OFF[s]:OFF[s + 1]].rearrange("p (n t) -> p n t", n=NP)

        def bank_cols(t, g):
            lo, hi = (OFF[c] for c in BANKS[g])
            return t[:, 2 * lo:2 * hi].rearrange("p (y c) -> p y c", y=2)

        G = KQ[:, 0, :, 0:L]
        at[0] = 0
        xt2 = cut(NT * D).rearrange("p (n d) -> p n d", n=NT)
        wg_sb = cut(2 * KT * P).rearrange("p (s k c) -> p s k c", s=2, k=KT)
        wo_sb = cut(H * D).rearrange("p (h n) -> p h n", h=H)
        oc = cut(2 * L).rearrange("p (s t) -> p s t", s=2)
        sq = cut(2 * L).rearrange("p (s t) -> p s t", s=2)
        sd = cut(L)[0:NP]
        to_row = cut(NP * NP).rearrange("p (n c) -> p n c", n=NP)
        center = cut(P)

        consts = scratch[:, 15360:15360 + 3 * P // 2].bitcast(BF16)
        identb = consts[:, 0:P]
        late = consts[:, P:2 * P]
        early = consts[:, 2 * P:3 * P]
        mcol_i = sb("mcol_i", [P, NT], I32)
        mcol = sb("mcol", [P, NT])
        mpad = sb("mpad", [P, NT])
        Af, Vf = (t[:, :, :].rearrange("p n t -> p (n t)") for t in (A, VO))
        Kf = KQ[:, :, :, :].rearrange("p y n t -> p (y n t)")
        from_row = Kf[0:NP, 8208:8208 + NP * P].rearrange("r (n c) -> r n c", n=NP)
        ctxt = Af[:, 0:2048].rearrange("p (n d) -> p n d", n=NT)
        xwkv = Af[:, 2048:3072].rearrange("p (k c) -> p k c", k=KT)
        xwq = Af[:, 3072:3584].rearrange("p (k c) -> p k c", k=KT)
        ctxT = Af[:, 5120:7168].rearrange("p (k t) -> p k t", k=KT)
        xwo = Af[:, 7168:8192].rearrange("p (g c) -> p g c", g=XG)
        stack = [Kf[:, 8208:16400].bitcast(BF16).rearrange("p (h t) -> p h t", h=XH),
                 Kf[:, 0:8192].bitcast(BF16).rearrange("p (h t) -> p h t", h=XH)]
        nat = [scratch[:, 7680 + 1024 * i:8704 + 1024 * i].bitcast(BF16).rearrange("p (h c) -> p h c", h=XH)
               for i in range(2)]
        rest = scratch[:, 9728:10240].rearrange("p (s c) -> p s c", s=2)
        xV = scratch[:, 10240:14336].rearrange("p (n h c) -> p n h c", n=NT, h=XH)
        xM = scratch[:, 14336:14464].rearrange("p (n h) -> p n h", n=NT)
        mnat = scratch[:, 14464:14496].bitcast(BF16).rearrange("p (s h y) -> p s h y", s=2, y=2)
        mrest = sb("mrest", [P, 2, XH])
        spread_sum = scratch[:, 14496:14624]
        xn2 = scratch[:, 14848:15360].rearrange("p (s d) -> p s d", s=2)
        MT = scratch[0:2 * XH, 15552:16064].bitcast(BF16)
        own_max = Vf[0:2 * XH, 7168:8192].bitcast(BF16).rearrange("r (h c) -> r h c", h=XH)
        osb = scratch[:, 4608:5632].rearrange("p (s t) -> p s t", s=2)
        osum = scratch[:, 5632:6656].rearrange("p (s t) -> p s t", s=2)
        attT = [Vf[:, 5120:7168].rearrange("p (g t) -> p g t", g=XG), Af[:, 5120:7168].rearrange("p (g t) -> p g t", g=XG)]
        POFF = [0, 4 * 512, 4 * (512 + 384), 4 * (512 + 384 + 256), 4 * 1280]
        PT = [Vf[:, 0:POFF[4]], Af[:, 0:POFF[4]]]

        def probs(buf, j):
            return PT[buf][:, POFF[j]:POFF[j + 1]].rearrange("p (h t) -> p h t", h=4)

        se = scratch[:, 2048:4096].rearrange("p (n d) -> p n d", n=ET)
        xf = scratch[:, 2048:4096].rearrange("p (n d) -> p n d", n=NT)
        seT = scratch[:, 4096:6144].rearrange("p (k s) -> p k s", k=KT)
        we = [scratch[:, 6144:9216], scratch[:, 9216:12288], Kf[:, 4096:7168], Kf[:, 8192:11264]]
        wgu = [w[:, 0:2048].rearrange("p (y k f) -> p y k f", y=2, k=KT) for w in we]
        wdn = [w[:, 2048:3072].rearrange("p (f d) -> p f d", f=FT) for w in we]
        hT = scratch[:, 12288:13312].rearrange("p (s f c) -> p s f c", s=2, f=FT)
        gel = scratch[:, 13312:14336].rearrange("p (s f c) -> p s f c", s=2, f=FT)
        bdn = scratch[:, 14336:15360].rearrange("p (s d) -> p s d", s=WS)
        bgu = sb("bgu", [P, WS, 2 * FT])
        gb = scratch[:, 9216:10240].rearrange("p (y d) -> p y d", y=4)
        scl = sb("scl", [P, 1])
        LG = Kf[:, 0:8192].rearrange("p (e t) -> p e t", e=ET)
        FD = Kf[:, 8192:16384].rearrange("p (n s) -> p n s", n=NT)
        FS = Vf.rearrange("p (e t) -> p e t", e=ET)
        EC = Af.rearrange("p (e t) -> p e t", e=ET)
        E1 = we[1][:, 0:2048].rearrange("p (s c) -> p s c", s=2)
        slT = Kf[:, 0:4096].rearrange("p (k e c) -> p k e c", k=KT, e=E)
        eo = Vf[:, 0:4096].rearrange("p (e b d) -> p e b d", e=ET, b=B)
        mE = sb("mE", [P, ET, B])
        dE = sb("dE", [P, ET, B])
        mN = sb("mN", [P, NT])
        dN = sb("dN", [P, NT])

        s_x = [sem("s_x0"), sem("s_x1")]
        s_small = sem("s_small")
        s_cst = sem("s_cst")
        s_pool = sem("s_pool")
        s_dve = sem("s_dve")
        s_g0, s_g1 = sem("s_g0"), sem("s_g1")
        s_mv = sem("s_mv")
        s_std = sem("s_std")
        s_xn = sem("s_xn")
        s_xtp = sem("s_xtp")
        s_xT = sem("s_xT")
        s_wh = [sem("s_wh0"), sem("s_wh1")]
        s_bp = sem("s_bp")
        s_bs = sem("s_bs")
        s_beta = sem("s_beta")
        s_pa = sem("s_pa")
        s_sa = sem("s_sa")
        s_pq = sem("s_pq")
        s_pre = sem("s_pre")
        s_conv = sem("s_conv")
        s_silu = sem("s_silu")
        s_t0, s_t1 = sem("s_t0"), sem("s_t1")
        s_init = sem("s_init")
        p_bm = sem("p_bm")
        p_kb = sem("p_kb")
        p_gs = sem("p_gs")
        p_gm = sem("p_gm")
        p_d = sem("p_d")
        p_r = sem("p_r")
        p_ws = sem("p_ws")
        e_bb = sem("e_bb")
        e_g = sem("e_g")
        e_gs = sem("e_gs")
        e_gr = sem("e_gr")
        e_kt = sem("e_kt")
        e_wt = sem("e_wt")
        e_we = sem("e_we")
        e_ap = sem("e_ap")
        e_wo = sem("e_wo")
        e_dl = sem("e_dl")
        e_st = sem("e_st")
        e_z = sem("e_z")
        v_pk = sem("v_pk")
        v_n = sem("v_n")
        v_r = sem("v_r")
        v_w = sem("v_w")
        v_ef = sem("v_ef")
        v_s = sem("v_s")
        a_kt = sem("a_kt")
        a_bb = sem("a_bb")
        a_gs = sem("a_gs")
        a_gm = sem("a_gm")
        a_kz = sem("a_kz")
        a_ks = sem("a_ks")
        a_ws = sem("a_ws")
        a_wt = sem("a_wt")
        a_we = sem("a_we")
        a_o = sem("a_o")
        a_sa = sem("a_sa")
        a_wo = sem("a_wo")
        a_st = sem("a_st")
        a_z = sem("a_z")
        g_ld = [sem("g_ld0"), sem("g_ld1")]
        g_p = sem("g_p")
        g_s = sem("g_s")
        g_wo = sem("g_wo")
        g_x = sem("g_x")
        o_cst = sem("o_cst")
        o_m = sem("o_m")
        o_c = sem("o_c")
        o_q = sem("o_q")
        o_v = sem("o_v")
        o_d = sem("o_d")
        o_r = sem("o_r")
        o_b = sem("o_b")
        o_y = sem("o_y")
        o_g = sem("o_g")
        o_p = sem("o_p")
        o_x = sem("o_x")
        s_out = sem("s_out")
        x_ld = sem("x_ld")
        x_cst = sem("x_cst")
        x_mv = sem("x_mv")
        x_sd = sem("x_sd")
        x_xn = sem("x_xn")
        x_tp = sem("x_tp")
        x_xT = sem("x_xT")
        x_mk = sem("x_mk")
        x_ct = sem("x_ct")
        x_cT = sem("x_cT")
        x_kp = sem("x_kp")
        x_hi = sem("x_hi")
        x_r1 = sem("x_r1")
        x_mi = sem("x_mi")
        x_lo = sem("x_lo")
        x_tu = sem("x_tu")
        x_ea = sem("x_ea")
        x_ed = sem("x_ed")
        x_s = sem("x_s")
        x_mx = sem("x_mx")
        x_mt = sem("x_mt")
        x_q2 = sem("x_q2")
        x_mn = sem("x_mn")
        x_st = sem("x_st")
        x_e = sem("x_e")
        x_pv = sem("x_pv")
        x_o = sem("x_o")
        x_dn = sem("x_dn")
        x_at = sem("x_at")
        x_op = sem("x_op")
        x_x = sem("x_x")
        f_ld = sem("f_ld")
        f_se = sem("f_se")
        f_st = sem("f_st")
        f_sT = sem("f_sT")
        f_lg = sem("f_lg")
        f_lk = sem("f_lk")
        f_mE = sem("f_mE")
        f_fs = sem("f_fs")
        f_fn = sem("f_fn")
        f_ft = sem("f_ft")
        f_fk = sem("f_fk")
        f_lt = sem("f_lt")
        f_mN = sem("f_mN")
        f_e1 = sem("f_e1")
        f_eh = sem("f_eh")
        f_dn = sem("f_dn")
        f_ek = sem("f_ek")
        f_sp = sem("f_sp")
        f_sk = sem("f_sk")
        w_ld = [sem(f"w_ld{i}") for i in range(WS)]
        w_gu = sem("w_gu")
        w_ge = sem("w_ge")
        w_h = sem("w_h")
        w_dn = sem("w_dn")
        w_eo = sem("w_eo")
        w_cb = sem("w_cb")
        w_x = sem("w_x")

        x_tiles = x.rearrange("b (i p) d -> p (b i) d", p=P)
        out_tiles = out.rearrange("b (i p) d -> p (b i) d", p=P)
        LB = NB - 1
        STATE_BANKS = (6, 7, 4, 5)

        block = ctx.enter_context(nc.Block())

        @block.sync
        def _(sp):
            for b in range(B):
                sp.dma_start(xt[:, b * QT_N:(b + 1) * QT_N], x_tiles[:, b * QT_N:(b + 1) * QT_N]).then_inc(s_x[b], 16)
            sp.dma_start(wb_sb, wb).then_inc(s_small, 16)
            sp.dma_start(bb_sb[:, :], bb).then_inc(s_small, 16)
            sp.dma_start(lngb[:, :], ln_gb).then_inc(s_small, 16)

            def head_weights(h, slot):
                wait(sp, s_silu, (h - 1) * 6)
                sp.dma_start(wh[:, slot], w_qkva[h]).then_inc(s_wh[slot], 16)
                sp.dma_start(cw[:, slot], conv_pack[h]).then_inc(s_wh[slot], 16)

            head_weights(0, 0)
            head_weights(1, 1)
            with sp.Fori(1, H // 2) as i:
                for slot in range(2):
                    sp.wait_ge(s_silu, 12 * i + (slot - 1) * 6)
                    sp.dma_start(wh[:, slot], w_qkva[bass.ds(2 * i + slot, 1)].rearrange("a p q k c -> p (a q) k c")
                                 ).then_inc(s_wh[slot], 16)
                    sp.dma_start(cw[:, slot], conv_pack[bass.ds(2 * i + slot, 1)].rearrange("a p c -> p (a c)")
                                 ).then_inc(s_wh[slot], 16)
            sp.wait_ge(a_o, 2 * NCH * NB)
            sp.wait_ge(v_w, 2 * NCH * NB)
            for h in range(H):
                if h == 2:
                    sp.dma_start(xt2, x_tiles).then_inc(g_x, 16)
                    sp.dma_start(wo_sb, w_o).then_inc(g_wo, 16)
                wait(sp, g_p, 2 * (h - 1))
                sp.dma_start(wg_sb[:, h % 2], w_gate[h]).then_inc(g_ld[h % 2], 16)
            for dst, src in ((ctxt, ctx_keys), (xwkv, xa_kv), (xwq, xa_q), (xwo, xa_o), (mcol_i[:, :], mask_cols)):
                sp.dma_start(dst, src).then_inc(x_ld, 16)
            sp.wait_ge(x_tu, 8 * NT)
            sp.dma_start(se, slots).then_inc(f_ld, 16)
            sp.dma_start(gb[:, 0:2], norm_gb.partition_broadcast(P)).then_inc(f_ld, 16)
            sp.dma_start(gb[:, 2:4], slot_gb.partition_broadcast(P)).then_inc(f_ld, 16)
            sp.dma_start(scl[:, :], scale.partition_broadcast(P)).then_inc(f_ld, 16)

            def expert(e, slot):
                sp.dma_start(wgu[slot], w_gate_up[bass.ds(e, 1)].rearrange("a p y k f -> p (a y) k f")).then_inc(w_ld[slot], 16)
                sp.dma_start(wdn[slot], w_down[bass.ds(e, 1)].rearrange("a p f d -> p (a f) d")).then_inc(w_ld[slot], 16)
                sp.dma_start(bgu[:, slot], b_gu[bass.ds(e, 1)].rearrange("a p c -> p (a c)")).then_inc(w_ld[slot], 16)
                sp.dma_start(bdn[:, slot], b_down[bass.ds(e, 1), :].rearrange("a d -> (a d)").partition_broadcast(P)
                             ).then_inc(w_ld[slot], 16)

            sp.wait_ge(x_x, NT)
            expert(0, 0)
            sp.wait_ge(f_lt, NT)
            expert(2, 2)
            sp.wait_ge(f_eh, 2 * NT)
            expert(1, 1)
            sp.wait_ge(f_sp, 2 * B * KT)
            expert(3, 3)
            with sp.Fori(1, E // WS) as i:
                for slot in range(WS):
                    sp.wait_ge(w_eo, 2 * (WS * i + slot - WS + 1))
                    expert(WS * i + slot, slot)
            for n in range(0, NT, 2):
                sp.wait_ge(w_x, n + 2)
                sp.dma_start(out_tiles[:, n:n + 2], xt2[:, n:n + 2]).then_inc(s_out, 16)
            sp.wait_ge(s_out, 16 * (NT // 2))

        @block.gpsimd
        def _(pool):
            me = Steps(pool, s_pool)
            nc.gpsimd.memset(ones[:, :], 1.0).then_inc(s_cst, 1)
            nc.gpsimd.memset(avg[:, :], 1.0 / P).then_inc(s_cst, 1)
            nc.gpsimd.memset(eps_col[:, 0:1], EPS).then_inc(s_cst, 1)
            nc.gpsimd.memset(eps_col[:, 1:2], EPS * S2).then_inc(s_cst, 1)
            me.did(nc.gpsimd.memset(ident[:, :], 0.0))
            me.did(nc.gpsimd.memset(own[:, :], -1.0))
            me.settle()
            nc.gpsimd.affine_select(out=ident[:, :], in_=ident[:, :], compare_op=ALU.not_equal, fill=1.0,
                                    base=0, pattern=[[-1, P]], channel_multiplier=1).then_inc(s_cst, 1)
            me.link(nc.gpsimd.affine_select(out=own[:, :], in_=own[:, :], compare_op=ALU.is_ge, fill=0.0,
                                            base=0, pattern=[[-C, NP]], channel_multiplier=1))
            nc.gpsimd.affine_select(out=own[:, :], in_=own[:, :], compare_op=ALU.is_ge, fill=0.0,
                                    base=C - 1, pattern=[[C, NP]], channel_multiplier=-1).then_inc(s_cst, 1)
            pool.wait_ge(s_cst, 6)
            nc.gpsimd.tensor_tensor(out=own_h[:, :], in0=own[:, 0:H], in1=own[:, H:NP], op=ALU.add).then_inc(s_cst, 1)
            nc.gpsimd.memset(KQ[:, 0, :, L:L + 1], 0.0).then_inc(s_cst, 1)
            nc.gpsimd.memset(KQ[:, 1, :, 0:1], 0.0).then_inc(s_cst, 1)
            me.did(nc.gpsimd.memset(GM[0], 0.0))
            me.did(nc.gpsimd.memset(R[0], 0.0))
            for y in range(2):
                me.did(nc.gpsimd.memset(Dt[y], 1.0))
                me.did(nc.gpsimd.memset(Suf[y], 1.0))
                me.did(nc.gpsimd.memset(Pre[y], 1.0))
            me.settle()
            pool.wait_ge(s_xT, NT)
            nc.gpsimd.memset(S, 0.0).then_inc(s_init, 1)
            pool.wait_ge(s_silu, 6 * H)
            pool.wait_ge(s_sa, 2 * H)
            pool.wait_ge(s_bp, 1)
            me.link(nc.gpsimd.memset(KBz, 0.0))
            nc.gpsimd.memset(ST, 0.0).then_inc(s_init, 1)
            pool.wait_ge(s_beta, 1)

            def spread_beta(o):
                wait(pool, e_bb, o)
                for b in range(B):
                    ins = nc.gpsimd.tensor_tensor(
                        out=beta_m[:, b], in0=betaT[:, b:b + 1, bass.ds(o * CH, CH)].to_broadcast([H, H, CH]),
                        in1=ident[0:H, 0:H].unsqueeze(2).to_broadcast([H, H, CH]), op=ALU.mult)
                ins.then_inc(p_bm, 1)

            def beta_keys(o):
                wait(pool, a_bb, o + 1)
                by_pair = KBb.rearrange("p i n s -> p n i s")
                nc.gpsimd.tensor_tensor(out=by_pair, in1=by_pair,
                                        in0=KQ[:, 0, :, bass.ds(o * CH, CH)].rearrange("p n (i s) -> p n i s", i=NB),
                                        op=ALU.mult).then_inc(p_kb, 1)

            def decays_of(o, i, first=False):
                m, t0, y = o * NB + i, o * CH + i * C, i % 2

                def a(s, n):
                    return A[:, :, bass.ds(t0 + s, 1)].to_broadcast([P, NP, n])

                wait(pool, p_d, m)
                wait(pool, v_n, m - 1)
                wait(pool, v_w, 2 * (m - 1))
                if i == 1:
                    wait(pool, a_sa, o)
                for s in range(C - 2, -1, -1):
                    me.did(nc.gpsimd.tensor_tensor(out=decays(y, s)[:, :, 1:C - s], in0=decays(y, s + 1),
                                                   in1=a(s + 1, C - 1 - s), op=ALU.mult))
                    me.did(nc.gpsimd.tensor_tensor(out=Suf[y][:, :, s:s + 1], in0=Suf[y][:, :, s + 1:s + 2],
                                                   in1=a(s + 1, 1), op=ALU.mult))
                    me.settle()
                ins = nc.gpsimd.tensor_tensor(out=Pre[y][:, :, 1:C + 1], in0=decays(y, 0), in1=a(0, C), op=ALU.mult)
                if not first:
                    me.link(ins)
                    before = Pre[1 - y] if i == 1 else Far[1 - y]
                    ins = nc.gpsimd.tensor_tensor(out=Far[y], in0=Pre[y],
                                                  in1=before[:, :, C:C + 1].to_broadcast([P, NP, C + 1]), op=ALU.mult)
                ins.then_inc(p_d, 1)

            def own_gram(o, i):
                m, y = o * NB + i, i % 2
                wait(pool, a_gs, m + 1)
                nc.gpsimd.tensor_tensor(out=GS[y], in0=GS[y],
                                        in1=own[:, :].unsqueeze(1).unsqueeze(3).to_broadcast([P, 2, NP, C]),
                                        op=ALU.mult).then_inc(p_gs, 1)

            def later_gram(o, i, last):
                n = REACH[i] - C * last
                wait(pool, a_gm, o * NB + i + 1)
                gm = GM[i][:, 0:2 * H * n].rearrange("p (y h t) -> p y h t", y=2, h=H)
                nc.gpsimd.tensor_tensor(out=gm, in0=gm,
                                        in1=own_h[:, :].unsqueeze(1).unsqueeze(3).to_broadcast([P, 2, H, n]),
                                        op=ALU.mult).then_inc(p_gm, 1)

            def from_state(o, i):
                m, t0, y = o * NB + i, o * CH + i * C, i % 2
                wait(pool, a_z, 4 * o + 4)
                wait(pool, v_w, 2 * (m - 1))
                wait(pool, a_o, 2 * (m - 1))
                wait(pool, p_d, m + 1)
                me.link(nc.gpsimd.tensor_tensor(out=R[y], in0=Z[:, :, :, (i - 1) * C:i * C + 1],
                                                in1=Far[y].unsqueeze(2).to_broadcast([P, NP, 2, C + 1]), op=ALU.mult))
                nc.gpsimd.tensor_tensor(out=R[y][:, :, 0, 0:C], in0=R[y][:, :, 0, 0:C],
                                        in1=VO[:, :, bass.ds(t0, C)], op=ALU.subtract).then_inc(p_r, 1)

            def decay_errors(o, i):
                wait(pool, v_w, 2 * (o * NB + i))
                wait(pool, e_wt, o * NB + i)
                wait(pool, e_we, LB * o + i - 1)
                wait(pool, p_d, o * NB + i + 1)
                me.settle()
                nc.gpsimd.tensor_tensor(
                    out=Wst[:, 0:i], in0=Wst[:, 0:i],
                    in1=Pre[i % 2][:, :, C].unsqueeze(1).unsqueeze(3).to_broadcast([P, i, NP, C]),
                    op=ALU.mult).then_inc(p_ws, 1)

            def chunk(o, last=False):
                if not last:
                    spread_beta(o + 1)
                decays_of(o, 1)
                later_gram(o, 0, last)
                from_state(o, 1)
                own_gram(o, 2)
                later_gram(o, 1, last)

                decay_errors(o, 1)
                decays_of(o, 2)
                from_state(o, 2)
                own_gram(o, 3)
                later_gram(o, 2, last)
                if not last:
                    beta_keys(o + 1)

                decay_errors(o, 2)
                decays_of(o, 3)
                from_state(o, 3)
                if last:
                    return
                own_gram(o + 1, 0)
                later_gram(o, 3, last)

                decay_errors(o, 3)
                decays_of(o + 1, 0)
                from_state(o, 4)
                own_gram(o + 1, 1)

            spread_beta(0)
            decays_of(0, 0, first=True)
            beta_keys(0)
            own_gram(0, 0)
            own_gram(0, 1)
            first = me.total()
            me.at(first)
            chunk(0)
            per = me.k
            second = me.total()
            with pool.Fori(1, NCH - 1) as o:
                me.at(second + (o - 1) * per)
                chunk(o)
                assert me.k == per
            me.at(second + (NCH - 2) * per)
            chunk(NCH - 1, last=True)
            pool.wait_ge(a_o, 2 * NCH * NB)
            pool.wait_ge(v_w, 2 * NCH * NB)
            nc.gpsimd.tensor_tensor(out=center, in0=ident[:, :], in1=avg[:, :], op=ALU.subtract).then_inc(o_cst, 1)
            me.link(nc.gpsimd.memset(to_row, 0.0))
            nc.gpsimd.affine_select(out=to_row, in_=to_row, compare_op=ALU.not_equal, fill=1.0 / P,
                                    base=0, pattern=[[1, NP], [-1, NP]], channel_multiplier=0).then_inc(o_cst, 1)
            me.link(nc.gpsimd.memset(from_row, 0.0))
            nc.gpsimd.affine_select(out=from_row, in_=from_row, compare_op=ALU.not_equal, fill=1.0,
                                    base=0, pattern=[[-1, NP], [0, P]], channel_multiplier=1).then_inc(o_cst, 1)
            me.did(nc.gpsimd.memset(late[:, :], 0.0))
            me.did(nc.gpsimd.memset(early[:, :], 0.0))
            nc.gpsimd.tensor_copy(identb[:, :], ident[:, :]).then_inc(x_cst, 1)
            me.settle()
            nc.gpsimd.affine_select(out=late[:, :], in_=late[:, :], compare_op=ALU.is_ge, fill=MASKED,
                                    base=0, pattern=[[-1, P]], channel_multiplier=1).then_inc(x_cst, 1)
            nc.gpsimd.affine_select(out=early[:, :], in_=early[:, :], compare_op=ALU.is_ge, fill=MASKED,
                                    base=0, pattern=[[1, P]], channel_multiplier=-1).then_inc(x_cst, 1)
            for i in range(2):
                nc.gpsimd.memset(nat[i], 0.0).then_inc(x_cst, 1)
            nc.gpsimd.memset(xV, 0.0).then_inc(x_cst, 1)
            me.link(nc.gpsimd.memset(spread_sum, 0.0))
            nc.gpsimd.affine_select(out=spread_sum.rearrange("p (h c) -> p h c", h=4),
                                    in_=spread_sum.rearrange("p (h c) -> p h c", h=4), compare_op=ALU.not_equal, fill=1.0,
                                    base=-XD, pattern=[[-32, 4], [0, 32]], channel_multiplier=1).then_inc(x_cst, 1)
            pool.wait_ge(o_p, NT)
            me.link(nc.gpsimd.memset(own_max, 1.0))
            me.link(nc.gpsimd.affine_select(out=own_max, in_=own_max, compare_op=ALU.is_ge, fill=0.0,
                                            base=0, pattern=[[-2, XH], [0, P]], channel_multiplier=1))
            nc.gpsimd.affine_select(out=own_max, in_=own_max, compare_op=ALU.is_ge, fill=0.0,
                                    base=1, pattern=[[2, XH], [0, P]], channel_multiplier=-1).then_inc(x_cst, 1)

        @block.scalar
        def _(act):
            act.wait_ge(s_cst, 9)
            act.wait_ge(s_mv, NT)
            nc.scalar.activation(std[:, :], mv[:, :, 1], ACT.Sqrt, bias=eps_col[:, 0:1]).then_inc(s_std, 1)
            act.wait_ge(s_small, 48)
            act.wait_ge(s_bp, 1)
            nc.scalar.activation(betaT[:, :, :], PS[0:H, 0:B, :], ACT.Sigmoid, bias=bb_sb[:, 0:1]).then_inc(s_bs, 1)
            act.wait_ge(s_bs, 1)
            nc.scalar.mul(betaT[:, :, :], betaT[:, :, :], S2).then_inc(s_beta, 1)

            def activate(i, u):
                hh, b, q = u // 6, u // 3 % 2, u % 3
                n = b * H + 2 * i + hh
                dst = (KQ[:, 1, bass.ds(n, 1), 1:L + 1], KQ[:, 0, bass.ds(n, 1), 0:L], VO[:, bass.ds(n, 1), :])[q]
                wait(act, s_conv, i * 12 + u + 1)
                nc.scalar.activation(dst, acc[:, u % 4:u % 4 + 1, :], ACT.Silu).then_inc(s_silu, 1)

            def heads(i, load):
                for u in range(12 + 2):
                    if u in (0, 6):
                        hh = u // 6
                        wait(act, s_wh[hh], 32 * (i + 1))
                        for b in range(B):
                            wait(act, s_pa, 4 * i + 2 * hh + b + 1)
                            nc.scalar.activation(A[:, bass.ds(b * H + 2 * i + hh, 1), :], PS[:, 6 + b:7 + b, :],
                                                 ACT.Sigmoid, bias=cw[:, hh, 15:16]).then_inc(s_sa, 1)
                    if u < 12:
                        q = u % 3
                        wait(act, s_pq, 12 * i + u + 1)
                        wait(act, s_silu, 12 * i + u - 3)
                        nc.scalar.activation(acc[:, u % 4, :], PS[:, u % 6, :], ACT.Identity,
                                             scale=cw[:, u // 6, 5 * q + 3:5 * q + 4],
                                             bias=cw[:, u // 6, 5 * q + 4:5 * q + 5]).then_inc(s_pre, 1)
                    if u >= 2:
                        activate(i, u - 2)

            heads(0, False)
            with act.Fori(1, H // 2) as i:
                heads(i, True)

            def keys_by_batch(o):
                wait(act, p_kb, o + 1)
                wait(act, e_gr, o * NB)
                for b in range(B):
                    pairs = slice(b * H, (b + 1) * H)
                    ins = nc.scalar.activation(KBz[:, b, :, pairs], KBb[:, :, pairs], ACT.Copy)
                ins.then_inc(a_kz, 1)

            def beta(o):
                wait(act, e_bb, o + 1)
                wait(act, e_gs, o * NB)
                wait(act, a_kz, o)
                wait(act, a_ks, o)
                nc.scalar.activation(KBb.rearrange("p i n s -> p n i s"),
                                     PS[:, 3, :].rearrange("p (n i s) -> p n i s", n=NP, i=NB), ACT.Copy).then_inc(a_bb, 1)

            def own_gram(o, i):
                m, y = o * NB + i, i % 2
                wait(act, e_gs, m + 1)
                wait(act, e_g, m - 1)
                nc.scalar.activation(GS[y], PS[:, 7, 0:2 * NP * C].rearrange("p (y n t) -> p y n t", y=2, n=NP),
                                     ACT.Copy).then_inc(a_gs, 1)

            def later_gram(o, i, last):
                n = REACH[i] - C * last
                wait(act, e_gr, o * NB + i + 1)
                wait(act, e_ap, o * 2 * NB)
                if 2 * H * n <= 512:
                    nc.scalar.activation(GM[i][:, 0:2 * H * n], PS[:, 3, 0:2 * H * n], ACT.Copy).then_inc(a_gm, 1)
                else:
                    for q in range(2):
                        ins = nc.scalar.activation(
                            GM[i].rearrange("p (y h t) -> p y h t", y=2, h=H)[:, q:q + 1, :, q:q + n - 1],
                            PS[:, 3, q * 256:(q + 1) * 256].rearrange("p (y h t) -> p y h t", y=1, h=H), ACT.Copy)
                    ins.then_inc(a_gm, 1)

            def by_pair(dst, src):
                return nc.scalar.activation(dst.rearrange("p n (i s) -> p n i s", i=NB), src.rearrange("p i n s -> p n i s"),
                                            ACT.Copy)

            def errors_turned(o, i):
                m, t0, y = o * NB + i, o * CH + i * C, i % 2
                wait(act, e_wt, m + 1)
                wait(act, e_ap, o * 2 * NB)
                nc.scalar.activation(WTs[:, i], PS[:, 6, 3 * P:4 * P], ACT.Copy).then_inc(a_wt, 1)

            def outputs(o, i):
                m, t0, y = o * NB + i, o * CH + i * C, i % 2
                for b in range(B):
                    wait(act, v_r, 2 * m + b + 1)
                    nc.scalar.activation(VO[:, b * H:(b + 1) * H, bass.ds(t0, C)], R[y][:, b * H:(b + 1) * H, 1, 1:C + 1],
                                         ACT.Copy).then_inc(a_o, 1)

            def earlier_turned(o, i):
                wait(act, e_we, LB * o + i)
                wait(act, e_ap, 2 * (o * NB + i))
                nc.scalar.activation(WTs[:, 0:i], PS[:, 6, 0:i * P].rearrange("p (j v) -> p j v", j=i),
                                     ACT.Copy).then_inc(a_we, 1)

            def chunk(o, first=False, last=False):
                if not first:
                    wait(act, v_w, 2 * NB * o)
                    wait(act, p_ws, LB * o)
                    wait(act, e_kt, o)
                    by_pair(turn, Wst).then_inc(a_ws, 1)
                    wait(act, e_wo, o)
                    nc.scalar.activation(WTo, PS[:, 3, :].rearrange("p (g k) -> p g k", g=4), ACT.Copy).then_inc(a_wo, 1)
                if not last:
                    wait(act, p_kb, o + 1)
                    by_pair(turn, KBb).then_inc(a_ks, 1)
                    wait(act, e_kt, o + 1)
                    wait(act, e_dl, 4 * o)
                    nc.scalar.activation(KBT, PS[:, 3, :].rearrange("p (g k) -> p g k", g=4), ACT.Copy,
                                         scale=-1.0).then_inc(a_kt, 1)
                if not first:
                    for u in range(4):
                        wait(act, e_st, 4 * (o - 1) + u + 1)
                        wait(act, e_z, 4 * o)
                        nc.scalar.activation(ST[:, u:NP:4], PS[:, STATE_BANKS[u], :].rearrange("p (n k) -> p n k", n=4),
                                             ACT.Copy).then_inc(a_st, 1)
                later_gram(o, 0, last)
                n = CH + 1 - C * last
                for u in range(4):
                    wait(act, e_z, 4 * o + u + 1)
                    wait(act, p_r, NB * o)
                    nc.scalar.activation(Z[:, 4 * u:4 * u + 4, :, 0:n],
                                         PS[:, STATE_BANKS[u], 0:8 * n].rearrange("p (n y t) -> p n y t", n=4, y=2),
                                         ACT.Copy).then_inc(a_z, 1)
                own_gram(o, 2)
                later_gram(o, 1, last)
                errors_turned(o, 0)
                outputs(o, 0)

                own_gram(o, 3)
                later_gram(o, 2, last)
                if not last:
                    beta(o + 1)
                earlier_turned(o, 1)
                errors_turned(o, 1)
                outputs(o, 1)

                if not last:
                    own_gram(o + 1, 0)
                    later_gram(o, 3, last)
                earlier_turned(o, 2)
                errors_turned(o, 2)
                outputs(o, 2)
                if last:
                    outputs(o, NB - 1)
                    return
                wait(act, p_d, NB * (o + 1))
                wait(act, e_st, 4 * o)
                wait(act, v_s, 4 * o)
                act.wait_ge(s_init, 2)
                for n in range(NP):
                    ins = nc.scalar.activation(S[:, n], S[:, n], ACT.Copy, scale=Far[1][:, n, C:C + 1])
                ins.then_inc(a_sa, 1)
                own_gram(o + 1, 1)
                earlier_turned(o, 3)
                keys_by_batch(o + 1)
                errors_turned(o, 3)
                outputs(o, 3)

            act.wait_ge(s_init, 2)
            beta(0)
            own_gram(0, 0)
            own_gram(0, 1)
            keys_by_batch(0)
            chunk(0, first=True)
            with act.Fori(1, NCH - 1) as o:
                chunk(o)
            chunk(NCH - 1, last=True)

            for h in range(H):
                for n in (2 * h, 2 * h + 1):
                    act.wait_ge(o_c, n + 1)
                    wait(act, o_v, n - 1)
                    nc.scalar.activation(sq[:, n % 2], VO[:, n], ACT.Square).then_inc(o_q, 1)
                for b in range(B):
                    act.wait_ge(g_p, 2 * h + b + 1)
                    nc.scalar.activation(G[:, b * H + h], PS[:, 2 * (h % 2) + b, :], ACT.Sigmoid).then_inc(g_s, 1)
            act.wait_ge(o_v, NP)
            nc.scalar.activation(sd, PS[0:NP, 6, :], ACT.Sqrt, bias=eps_col[0:NP, 1:2]).then_inc(o_d, 1)

            def norm_std(r):
                act.wait_ge(x_mv, NT * (r + 1))
                nc.scalar.activation(std[:, :], mv[:, :, 1], ACT.Sqrt, bias=eps_col[:, 0:1]).then_inc(x_sd, 1)

            def high(t):
                r, n = t // NT, t % NT
                act.wait_ge(x_kp, t + 1)
                wait(act, x_tu, 4 * (t - 1))
                if t < 2:
                    act.wait_ge(x_cst, 6)
                src = PS[:, 6 + t % 2, 0:D].rearrange("p (h o c) -> p h o c", h=XH, o=1)
                parts = nat[t % 2][:, :, 0:6 * XD].rearrange("p h (y c) -> p h y c", y=6)
                if r == 0:
                    ins = nc.scalar.activation(parts[:, :, 0:3], src.to_broadcast([P, XH, 3, XD]), ACT.Copy)
                else:
                    nc.scalar.activation(parts[:, :, 0:4:3], src.to_broadcast([P, XH, 2, XD]), ACT.Copy, scale=XD ** -0.5)
                    ins = nc.scalar.activation(parts[:, :, 5:6], src, ACT.Copy, scale=XD ** -0.5)
                ins.then_inc(x_hi, 1)

            def middle(t):
                r = t // NT
                act.wait_ge(x_r1, t + 1)
                parts = nat[t % 2][:, :, 0:6 * XD].rearrange("p h (y c) -> p h y c", y=6)
                nc.scalar.activation(parts[:, :, 3:5] if r == 0 else parts[:, :, 1:5:3],
                                     rest[:, t % 2].rearrange("p (h o c) -> p h o c", h=XH, o=1)
                                     .to_broadcast([P, XH, 2, XD]), ACT.Copy).then_inc(x_mi, 1)

            def keep(t):
                r, n = t // NT, t % NT
                for q in range(2):
                    act.wait_ge(x_tu, 4 * t + q + 1)
                    nc.scalar.activation(stack[r][:, 4 * q:4 * q + 4, n * P:(n + 1) * P],
                                         PS[:, q, :].rearrange("p (h t) -> p h t", h=4), ACT.Copy).then_inc(x_ea, 1)

            for r in range(2):
                if r == 1:
                    norm_std(0)
                for t in range(r * NT, (r + 1) * NT):
                    high(t)
                    if t > r * NT:
                        keep(t - 1)
                    middle(t)
                keep((r + 1) * NT - 1)
            u = 0
            for k in range(B * XG):
                b, g = k // XG, k % XG
                if k == 1:
                    norm_std(1)
                if k >= 2:
                    act.wait_ge(x_pv, k - 1)
                for j in range(QT_N):
                    for half in range(2):
                        act.wait_ge(x_st, u + 1)
                        n = L - j * P
                        nc.scalar.activation(probs(k % 2, j)[:, 2 * half:2 * half + 2],
                                             PS[:, 2 * (u % 3):2 * (u % 3) + 2, 0:n], ACT.Exp).then_inc(x_e, 1)
                        u += 1
                for kk in ([k - 1] if k else []) + ([k] if k == B * XG - 1 else []):
                    act.wait_ge(x_pv, kk + 1)
                    wait(act, x_at, kk - 1)
                    nc.scalar.activation(osb[:, kk % 2], PS[:, 6 + kk % 2, :], ACT.Copy).then_inc(x_o, 1)
            norm_std(2)
            norm_std(3)
            for u in range(ET * B):
                e, b = u // B, u % B
                act.wait_ge(f_lg, u + 1)
                nc.scalar.activation(LG[:, e, b * L:(b + 1) * L], PS[:, u % 4, :], ACT.Copy).then_inc(f_lk, 1)
                act.wait_ge(f_mE, u + 1)
                nc.scalar.activation(FS[:, e, b * L:(b + 1) * L], PS[:, u % 4, :], ACT.Exp, bias=mE[:, e, b:b + 1],
                                     accum_out=dE[:, e, b:b + 1]).then_inc(f_fs, 1)
            for n in range(NT):
                act.wait_ge(f_mN, n + 1)
                wait(act, f_eh, 2 * (n - 1))
                nc.scalar.activation(E1[:, n % 2], PS[:, 4 + 2 * (n % 2):6 + 2 * (n % 2), :].rearrange("p b c -> p (b c)"),
                                     ACT.Exp, bias=mN[:, n:n + 1], accum_out=dN[:, n:n + 1]).then_inc(f_e1, 1)
            act.wait_ge(f_lt, NT)
            for u in range(2 * B * KT):
                b, k, half = u // 4, u // 2 % 2, u % 2
                act.wait_ge(f_sp, u + 1)
                nc.scalar.activation(slT[:, k, half * 8:(half + 1) * 8, b * SL:(b + 1) * SL],
                                     PS[:, u % 2, :].rearrange("p (e s) -> p e s", e=8), ACT.Copy).then_inc(f_sk, 1)

            def experts(i):
                for slot in range(WS):
                    e, half = WS * i + slot, slot % 2
                    act.wait_ge(w_ld[slot], 64 * (i + 1))
                    act.wait_ge(w_gu, e + 1)
                    wait(act, w_h, e - 1)
                    for f in range(FT):
                        ins = nc.scalar.activation(gel[:, half, f], PS[:, 2 * half, f * P:(f + 1) * P], ACT.Gelu,
                                                   bias=bgu[:, slot, f:f + 1])
                    ins.then_inc(w_ge, 1)

            experts(0)
            with act.Fori(1, E // WS) as i:
                experts(i)

        @block.tensor
        def _(pe):
            pe.wait_ge(s_cst, 9)
            for n in range(NT):
                pe.wait_ge(s_xn, n + 1)
                wait(pe, s_xT, n - 1)
                for k in range(KT):
                    ins = nc.tensor.transpose(PS[:, 6 + n % 2, k * P:(k + 1) * P], xn[:, n % 2, k * P:(k + 1) * P],
                                              ident[:, :])
                ins.then_inc(s_xtp, 1)
            pe.wait_ge(s_xT, NT)
            pe.wait_ge(s_small, 48)
            for b in range(B):
                for k in range(KT):
                    ins = nc.tensor.matmul(PS[0:H, b, :], wb_sb[:, k, :], xT[:, k, b * L:(b + 1) * L],
                                           start=(k == 0), stop=(k == KT - 1))
            ins.then_inc(s_bp, 1)

            def heads(i, first):
                for u in range(12):
                    hh, b, q = u // 6, u // 3 % 2, u % 3
                    if u % 6 == 0:
                        wait(pe, s_wh[hh], 32 * (i + 1))
                        for bb in range(B):
                            if not (first and hh == 0):
                                wait(pe, s_sa, 4 * i + 2 * hh + bb - 1)
                            for k in range(KT):
                                ins = nc.tensor.matmul(PS[:, 6 + bb, :], wh[:, hh, 3, k, :], xT[:, k, bb * L:(bb + 1) * L],
                                                       start=(k == 0), stop=(k == KT - 1))
                            ins.then_inc(s_pa, 1)
                    if first and u == 0:
                        pe.wait_ge(s_bs, 1)
                    wait(pe, s_conv, 12 * i + u - 5)
                    for k in range(KT):
                        ins = nc.tensor.matmul(PS[:, u % 6, :], wh[:, hh, q, k, :], xT[:, k, b * L:(b + 1) * L],
                                               start=(k == 0), stop=(k == KT - 1))
                    ins.then_inc(s_pq, 1)

            heads(0, True)
            with pe.Fori(1, H // 2) as i:
                heads(i, False)

            def beta_all(o):
                wait(pe, p_bm, o + 1)
                if not isinstance(o, int) or o > 0:
                    wait(pe, a_gm, (o - 1) * NB + 3)
                nc.tensor.matmul(PS[:, 3, :], ones[0:H, :], beta_m[:, :, :, :].rearrange("r b h s -> r (b h s)"),
                                 start=True, stop=True).then_inc(e_bb, 1)

            def own_gram(o, i):
                m = o * NB + i
                wait(pe, p_kb, o + 1)
                wait(pe, a_gs, m)
                if i == 2:
                    wait(pe, a_z, 4 * o + 4)
                nc.tensor.matmul(PS[:, 7, 0:2 * NP * C].rearrange("p (y n t) -> p y n t", y=2, n=NP),
                                 KBb[:, i].rearrange("p n s -> p (n s)"), KQ[:, :, :, bass.ds(o * CH + i * C + 1, C)],
                                 start=True, stop=True).then_inc(e_gs, 1)

            def later_gram(o, i, last):
                n = REACH[i] - C * last
                t0 = o * CH + (i + 1) * C
                wait(pe, a_kz, o + 1)
                wait(pe, a_gm, o * NB + i)
                if i == 0:
                    if last:
                        wait(pe, a_wo, o)
                    else:
                        wait(pe, a_kt, o + 1)
                if i == 3:
                    wait(pe, a_bb, o + 2)
                if 2 * H * n <= 512:
                    for b in range(B):
                        ins = nc.tensor.matmul(
                            PS[:, 3, 0:2 * H * n].rearrange("p (y h t) -> p y h t", y=2, h=H),
                            KBz[:, b, i].rearrange("p n s -> p (n s)"),
                            KQ[:, :, b * H:(b + 1) * H, bass.ds(t0, n)], start=(b == 0), stop=(b == B - 1))
                else:
                    for q in range(2):
                        for b in range(B):
                            ins = nc.tensor.matmul(
                                PS[:, 3, q * 256:(q + 1) * 256].rearrange("p (h t) -> p h t", h=H),
                                KBz[:, b, i].rearrange("p n s -> p (n s)"),
                                KQ[:, q, b * H:(b + 1) * H, bass.ds(t0 + q, n - 1)], start=(b == 0), stop=(b == B - 1),
                                skip_group_check=True)
                ins.then_inc(e_gr, 1)

            def dots(o, i):
                m, y = o * NB + i, i % 2
                wait(pe, p_gs, m + 1)
                wait(pe, v_n, m)
                for g, (s0, s1) in enumerate(BANKS):
                    width = OFF[s1] - OFF[s0]
                    for s in range(s0, s1):
                        ins = nc.tensor.matmul(
                            PS[:, g, 0:2 * width].rearrange("p (y c) -> p y c", y=2)[:, :, OFF[s] - OFF[s0]:OFF[s + 1] - OFF[s0]]
                            .rearrange("p y (n t) -> p y n t", n=NP),
                            pick[:, s, :], GS[y][:, :, :, s:C], start=True, stop=True)
                ins.then_inc(e_g, 1)

            def effects(o, i, last):
                m = o * NB + i
                if i > 0:
                    wait(pe, p_ws, LB * o + i)
                    wait(pe, a_wt, m)
                    for j in range(i):
                        ins = nc.tensor.transpose(PS[:, 6, j * P:(j + 1) * P],
                                                  Wst[:, j].rearrange("p n s -> p (n s)"), ident[:, :])
                    ins.then_inc(e_we, 1)
                for j in range(i + 1):
                    if j == 0:
                        wait(pe, v_ef, 2 * m)
                        wait(pe, a_z, 4 * o + 4)
                    if j == i:
                        wait(pe, v_w, 2 * m + 2)
                        if i > 0:
                            wait(pe, a_we, LB * o + i)
                        nc.tensor.transpose(PS[:, 6, 3 * P:4 * P], Wst[:, i].rearrange("p n s -> p (n s)"),
                                            ident[:, :]).then_inc(e_wt, 1)
                        wait(pe, a_wt, m + 1)
                        wait(pe, p_gm, m + 1)
                    else:
                        wait(pe, a_we, LB * o + i)
                    n = REACH[j] - C * last
                    for b in range(B):
                        rows = slice(C * H * b, C * H * (b + 1))
                        later = GM[j][rows, 0:2 * H * n].rearrange("p (y h t) -> p y h t", y=2, h=H)
                        ins = nc.tensor.matmul(
                            PS[:, 4 + b, 0:2 * H * (C + 1)].rearrange("p (y h t) -> p y h t", y=2, h=H), WTs[rows, j, :],
                            later[:, :, :, (i - j) * C:(i - j + 1) * C + 1], start=(j == 0), stop=(j == i),
                            tile_position=(C * H * b, 0), skip_group_check=True)
                        if j == i:
                            ins.then_inc(e_ap, 1)

            def chunk(o, first=False, last=False):
                if not first:
                    wait(pe, a_ws, o)
                    wait(pe, a_gm, NB * o)
                    for g in range(4):
                        ins = nc.tensor.transpose(PS[:, 3, g * P:(g + 1) * P],
                                                  turn[:, 4 * g:4 * g + 4, :].rearrange("p n s -> p (n s)"), ident[:, :])
                    ins.then_inc(e_wo, 1)
                dots(o, 1)
                wait(pe, a_gs, NB * o + 2)
                wait(pe, a_wt, NB * o)
                wait(pe, v_ef, 2 * NB * o)
                if not first:
                    wait(pe, a_wo, o)
                    wait(pe, a_kt, o)
                    for u in range(4):
                        for j in range(4):
                            ins = nc.tensor.matmul(PS[:, STATE_BANKS[u], j * P:(j + 1) * P],
                                                   WTo[CH * u:CH * (u + 1), j, :], KBT[CH * u:CH * (u + 1), j, :],
                                                   start=True, stop=True, tile_position=(CH * u, 0))
                        ins.then_inc(e_dl, 1)
                if not last:
                    wait(pe, a_ks, o + 1)
                    wait(pe, a_wo, o)
                    for g in range(4):
                        ins = nc.tensor.transpose(PS[:, 3, g * P:(g + 1) * P],
                                                  turn[:, 4 * g:4 * g + 4, :].rearrange("p n s -> p (n s)"), ident[:, :])
                    ins.then_inc(e_kt, 1)
                if not first:
                    for u in range(4):
                        wait(pe, v_s, 4 * (o - 1) + u + 1)
                        for j in range(4):
                            ins = nc.tensor.transpose(PS[:, STATE_BANKS[u], j * P:(j + 1) * P], S[:, 4 * j + u, :],
                                                      ident[:, :])
                        ins.then_inc(e_st, 1)
                later_gram(o, 0, last)
                n = CH + 1 - C * last
                wait(pe, a_st, 4 * o)
                for u in range(4):
                    for j in range(4):
                        pair = 4 * u + j
                        ins = nc.tensor.matmul(
                            PS[:, STATE_BANKS[u], j * 2 * n:(j + 1) * 2 * n].rearrange("p (y t) -> p y t", y=2),
                            ST[:, pair], KQ[:, :, pair, bass.ds(o * CH + C, n)], start=True, stop=True)
                    ins.then_inc(e_z, 1)
                own_gram(o, 2)
                later_gram(o, 1, last)
                effects(o, 0, last)

                dots(o, 2)
                own_gram(o, 3)
                later_gram(o, 2, last)
                if not last:
                    beta_all(o + 1)
                effects(o, 1, last)

                dots(o, 3)
                if not last:
                    own_gram(o + 1, 0)
                    later_gram(o, 3, last)
                effects(o, 2, last)
                if last:
                    return
                dots(o + 1, 0)
                own_gram(o + 1, 1)
                effects(o, 3, last)

            pe.wait_ge(s_beta, 1)
            pe.wait_ge(s_conv, 6 * H)
            pe.wait_ge(s_silu, 6 * H)
            pe.wait_ge(s_sa, 2 * H)
            pe.wait_ge(s_init, 2)
            beta_all(0)
            own_gram(0, 0)
            pe.wait_ge(v_pk, 1)
            dots(0, 0)
            own_gram(0, 1)
            chunk(0, first=True)
            with pe.Fori(1, NCH - 1) as o:
                chunk(o)
            chunk(NCH - 1, last=True)

            pe.wait_ge(a_o, 2 * NCH * NB)

            def less_mean(n):
                pe.wait_ge(o_cst, 1)
                wait(pe, o_c, n - 1)
                nc.tensor.matmul(PS[:, 4 + n % 2, :], center, VO[:, n], start=True, stop=True).then_inc(o_m, 1)

            def variance(n):
                pe.wait_ge(o_cst, 2)
                pe.wait_ge(o_q, n + 1)
                nc.tensor.matmul(PS[0:NP, 6, :], to_row[:, n, :], sq[:, n % 2], start=(n == 0),
                                 stop=(n == NP - 1)).then_inc(o_v, 1)

            for h in range(H):
                less_mean(2 * h)
                less_mean(2 * h + 1)
                pe.wait_ge(g_ld[h % 2], 16 * (h // 2 + 1))
                for b in range(B):
                    wait(pe, g_s, 2 * h + b - 3)
                    for k in range(KT):
                        ins = nc.tensor.matmul(PS[:, 2 * (h % 2) + b, :], wg_sb[:, h % 2, k, :], xT[:, k, b * L:(b + 1) * L],
                                               start=(k == 0), stop=(k == KT - 1))
                    ins.then_inc(g_p, 1)
                variance(2 * h)
                variance(2 * h + 1)
            pe.wait_ge(o_cst, 3)
            pe.wait_ge(g_s, NP)
            pe.wait_ge(o_r, 1)
            for n in range(NP):
                wait(pe, o_y, n - 3)
                nc.tensor.matmul(PS[:, n % 4, :], from_row[:, n, :], sd, start=True, stop=True).then_inc(o_b, 1)
            pe.wait_ge(g_wo, 16)
            pe.wait_ge(o_g, NP)
            for n in range(NT):
                b, i = n // (NT // B), n % (NT // B)
                wait(pe, o_x, n - 3)
                for h in range(H):
                    ins = nc.tensor.matmul(PS[:, n % 4, 0:D], VO[:, b * H + h, i * P:(i + 1) * P], wo_sb[:, h, :],
                                           start=(h == 0), stop=(h == H - 1))
                ins.then_inc(o_p, 1)

            pe.wait_ge(x_cst, 3)
            pe.wait_ge(x_ld, 16 * 5)
            for n in range(NT):
                wait(pe, x_cT, n - 1)
                for k in range(KT):
                    ins = nc.tensor.transpose(PS[:, 6 + n % 2, k * P:(k + 1) * P], ctxt[:, n, k * P:(k + 1) * P],
                                              ident[:, :])
                ins.then_inc(x_ct, 1)
            pe.wait_ge(x_cT, NT)
            def project(t):
                r, n = t // NT, t % NT
                wait(pe, x_lo, t - 1)
                src, w, width = (ctxT, xwkv, 2 * D) if r == 0 else (xT, xwq, D)
                for k in range(KT):
                    ins = nc.tensor.matmul(PS[:, 6 + t % 2, 0:width], src[:, k, n * P:(n + 1) * P], w[:, k, :],
                                           start=(k == 0), stop=(k == KT - 1))
                ins.then_inc(x_kp, 1)

            def turn_parts(t):
                pe.wait_ge(x_lo, t + 1)
                for q in range(4):
                    wait(pe, x_ea if q < 2 else x_ed, 2 * (t - 1) + q % 2 + 1)
                    for j in range(4):
                        ins = nc.tensor.matmul(PS[:, q, j * P:(j + 1) * P], nat[t % 2][:, 4 * q + j, :], identb[:, :],
                                               start=True, stop=True)
                    ins.then_inc(x_tu, 1)

            def stack_up(r):
                project(r * NT)
                for t in range(r * NT, (r + 1) * NT):
                    if t + 1 < (r + 1) * NT:
                        project(t + 1)
                    turn_parts(t)

            stack_up(0)

            def transpose_x(r, bank):
                for n in range(NT):
                    pe.wait_ge(x_xn, NT * r + n + 1)
                    wait(pe, x_xT, NT * r + n - 1)
                    for k in range(KT):
                        ins = nc.tensor.transpose(PS[:, bank + n % 2, k * P:(k + 1) * P],
                                                  (xn2[:, n % 2] if r == 0 else xf[:, n])[:, k * P:(k + 1) * P], ident[:, :])
                    ins.then_inc(x_tp, 1)
                pe.wait_ge(x_xT, NT * (r + 1))

            pe.wait_ge(x_lo, NT)
            transpose_x(0, 6)
            stack_up(1)
            pe.wait_ge(x_ea, 4 * NT)
            pe.wait_ge(x_ed, 4 * NT)
            u = 0
            for n in range(NT):
                b, i = n // QT_N, n % QT_N
                w = (i + 1) * P
                for pair in range(XH // 2):
                    wait(pe, x_mx, u - 2)
                    for j in range(2):
                        h, bank = 2 * pair + j, 2 * (u % 3) + j
                        nc.tensor.matmul(PS[:, bank, 0:w], stack[1][:, h, n * P:(n + 1) * P], stack[0][:, h, b * L:b * L + w],
                                         start=True, stop=False)
                        ins = nc.tensor.matmul(PS[:, bank, i * P:w], identb[:, :], late[:, :], start=False, stop=True)
                    ins.then_inc(x_s, 1)
                    u += 1
                if n > 0:
                    pe.wait_ge(x_mn, n)
                    wait(pe, x_q2, n - 2)
                    nc.tensor.matmul(PS[0:2 * XH, 6 + (n - 1) % 2, 0:P], mnat[:, (n - 1) % 2].rearrange("p h y -> p (h y)"),
                                     identb[:, :], start=True, stop=True).then_inc(x_mt, 1)
            pe.wait_ge(x_mn, NT)
            wait(pe, x_q2, NT - 2)
            nc.tensor.matmul(PS[0:2 * XH, 6 + (NT - 1) % 2, 0:P], mnat[:, (NT - 1) % 2].rearrange("p h y -> p (h y)"),
                             identb[:, :], start=True, stop=True).then_inc(x_mt, 1)
            pe.wait_ge(x_q2, NT)
            pe.wait_ge(x_cst, 8)

            def turned_scores(k):
                b, g = k // XG, k % XG
                for j in range(QT_N):
                    w = L - j * P
                    for half in range(2):
                        u = k * 2 * QT_N + 2 * j + half
                        wait(pe, x_e, u - 2)
                        for hh in range(2):
                            h, bank = 4 * g + 2 * half + hh, 2 * (u % 3) + hh
                            nc.tensor.matmul(PS[:, bank, 0:w], stack[0][:, h, b * L + j * P:b * L + (j + 1) * P],
                                             stack[1][:, h, b * L + j * P:(b + 1) * L], start=True, stop=False)
                            nc.tensor.matmul(PS[:, bank, 0:w], own_max[:, h, :], MT[:, b * L + j * P:(b + 1) * L],
                                             start=False, stop=False)
                            ins = nc.tensor.matmul(PS[:, bank, 0:P], identb[:, :], early[:, :], start=False, stop=True)
                        ins.then_inc(x_st, 1)

            def attended(k):
                b, g = k // XG, k % XG
                wait(pe, x_at, k - 1)
                for j in range(QT_N):
                    pe.wait_ge(x_e, k * 2 * QT_N + 2 * j + 2)
                    for hh in range(4):
                        ins = nc.tensor.matmul(PS[32 * hh:32 * hh + 32, 6 + k % 2, j * P:L], xV[:, b * QT_N + j, 4 * g + hh, :],
                                               probs(k % 2, j)[:, hh, :], start=(j == 0), stop=(j == QT_N - 1),
                                               tile_position=(0, 32 * hh), skip_group_check=True)
                ins.then_inc(x_pv, 1)

            def sums(k):
                pe.wait_ge(x_o, k + 1)
                nc.tensor.matmul(PS[:, 6 + k % 2, :], spread_sum, osb[:, k % 2], start=True, stop=True).then_inc(x_dn, 1)

            turned_scores(0)
            for k in range(B * XG):
                if k + 1 < B * XG:
                    turned_scores(k + 1)
                if k > 0:
                    sums(k - 1)
                attended(k)
            sums(B * XG - 1)
            pe.wait_ge(x_at, B * XG)
            for n in range(NT):
                b, i = n // QT_N, n % QT_N
                wait(pe, x_x, n - 1)
                for g in range(XG):
                    ins = nc.tensor.matmul(PS[:, 4 + n % 2, 0:D], attT[b][:, g, i * P:(i + 1) * P], xwo[:, g, :],
                                           start=(g == 0), stop=(g == XG - 1))
                ins.then_inc(x_op, 1)

            for n in range(ET):
                pe.wait_ge(f_se, n + 1)
                wait(pe, f_sT, n - 1)
                for k in range(KT):
                    ins = nc.tensor.transpose(PS[:, 6 + n % 2, k * P:(k + 1) * P], se[:, n, k * P:(k + 1) * P], ident[:, :])
                ins.then_inc(f_st, 1)
            pe.wait_ge(f_sT, ET)
            transpose_x(1, 6)
            for u in range(ET * B):
                e, b = u // B, u % B
                wait(pe, f_fs, u - 3)
                wait(pe, f_mE, u - 3)
                for k in range(KT):
                    ins = nc.tensor.matmul(PS[:, u % 4, :], seT[:, k, e * P:(e + 1) * P], xT[:, k, b * L:(b + 1) * L],
                                           start=(k == 0), stop=(k == KT - 1))
                ins.then_inc(f_lg, 1)
            pe.wait_ge(f_lk, ET * B)

            def logits_turned(n):
                wait(pe, f_e1, n - 1)
                wait(pe, f_mN, n - 1)
                for e in range(ET):
                    ins = nc.tensor.transpose(PS[:, 4 + 2 * (n % 2) + e // 4, (e % 4) * P:(e % 4 + 1) * P],
                                              LG[:, e, n * P:(n + 1) * P], ident[:, :])
                ins.then_inc(f_lt, 1)

            logits_turned(0)
            pe.wait_ge(f_fs, ET * B)
            for n in range(NT):
                if n + 1 < NT:
                    logits_turned(n + 1)
                for half in range(2):
                    v = 2 * n + half
                    wait(pe, f_fk, v - 1)
                    pe.wait_ge(f_fn, 8 * half + 8)
                    for e in range(4):
                        ins = nc.tensor.transpose(PS[:, v % 2, e * P:(e + 1) * P], FS[:, 4 * half + e, n * P:(n + 1) * P],
                                                  ident[:, :])
                    ins.then_inc(f_ft, 1)
                pe.wait_ge(f_e1, n + 1)
                for half in range(2):
                    v = 2 * n + half
                    wait(pe, f_ek, v - 1)
                    for e in range(4):
                        c0 = (4 * half + e) * P
                        ins = nc.tensor.transpose(PS[:, 2 + v % 2, e * P:(e + 1) * P], E1[:, n % 2, c0:c0 + P], ident[:, :])
                    ins.then_inc(f_eh, 1)
            pe.wait_ge(f_fk, 2 * NT)
            for u in range(2 * B * KT):
                b, k, half = u // 4, u // 2 % 2, u % 2
                wait(pe, f_sk, u - 1)
                for j in range(QT_N):
                    n = b * QT_N + j
                    ins = nc.tensor.matmul(PS[:, u % 2, :], xf[:, n, k * P:(k + 1) * P], FD[:, n, half * L:(half + 1) * L],
                                           start=(j == 0), stop=(j == QT_N - 1))
                ins.then_inc(f_sp, 1)
            pe.wait_ge(f_sk, 2 * B * KT)
            pe.wait_ge(f_ek, 2 * NT)

            def gate_up(i, slot):
                e, bank = WS * i + slot, 2 * (slot % 2)
                wait(pe, w_ld[slot], 64 * (i + 1))
                wait(pe, w_ge, e - 1)
                wait(pe, w_h, e - 1)
                for y in range(2):
                    for f in range(FT):
                        for k in range(KT):
                            ins = nc.tensor.matmul(PS[:, bank + y, f * P:(f + 1) * P],
                                                   wgu[slot][:, y, k, f * P:(f + 1) * P],
                                                   slT[:, k, bass.ds(e, 1), :].rearrange("p e c -> p (e c)"),
                                                   start=(k == 0), stop=(k == KT - 1))
                ins.then_inc(w_gu, 1)

            def down(i, slot):
                e, half = WS * i + slot, slot % 2
                wait(pe, w_h, e + 1)
                wait(pe, w_eo, 2 * (e - 1))
                for f in range(FT):
                    ins = nc.tensor.matmul(PS[:, 4 + half, 0:D], hT[:, half, f], wdn[slot][:, f, :], start=(f == 0),
                                           stop=(f == FT - 1))
                ins.then_inc(w_dn, 1)

            def experts(i):
                gate_up(i, 0)
                for slot in range(WS):
                    if slot + 1 < WS:
                        gate_up(i, slot + 1)
                    down(i, slot)

            experts(0)
            with pe.Fori(1, E // WS) as i:
                experts(i)
            for n in range(NT):
                b = n // QT_N
                pe.wait_ge(w_eo, 2 * E)
                wait(pe, w_x, n - 1)
                for e in range(ET):
                    ins = nc.tensor.matmul(PS[:, 6 + n % 2, 0:D], EC[:, e, n * P:(n + 1) * P], eo[:, e, b, :],
                                           start=(e == 0), stop=(e == ET - 1))
                ins.then_inc(w_cb, 1)

        @block.vector
        def _(dve):
            me = Steps(dve, s_dve)
            for n in range(NT):
                if n % QT_N == 0:
                    dve.wait_ge(s_x[n // QT_N], 16)
                me.did(nc.vector.bn_stats(stats[:, n, :], xt[:, n, :]))
            me.settle()
            for n in range(NT):
                nc.vector.bn_aggr(mv[:, n, :], stats[:, n, :]).then_inc(s_mv, 1)
            dve.wait_ge(s_std, 1)
            me.link(nc.vector.reciprocal(rstd[:, :], std[:, :]))
            dve.wait_ge(s_mv, NT)
            for n in range(NT):
                wait(dve, s_xtp, n - 1)
                nc.vector.tensor_scalar(xn[:, n % 2], xt[:, n, :], mv[:, n, 0:1], rstd[:, n:n + 1], ALU.subtract,
                                        ALU.mult).then_inc(s_xn, 1)
                if n > 0:
                    dve.wait_ge(s_xtp, n)
                    nc.vector.tensor_copy(xT[:, :, (n - 1) * P:n * P],
                                          PS[:, 6 + (n - 1) % 2, 0:KT * P].rearrange("p (k c) -> p k c", k=KT)
                                          ).then_inc(s_xT, 1)
            dve.wait_ge(s_xtp, NT)
            nc.vector.tensor_copy(xT[:, :, (NT - 1) * P:NT * P],
                                  PS[:, 6 + (NT - 1) % 2, 0:KT * P].rearrange("p (k c) -> p k c", k=KT)).then_inc(s_xT, 1)

            taps = [Steps(dve, s_t0), Steps(dve, s_t1)]

            def heads(i):
                for u0 in range(0, 12, 2):
                    for j in range(1, 4):
                        for u, st in ((u0, taps[0]), (u0 + 1, taps[1])):
                            hh, q = u // 6, u % 3
                            if j == 1:
                                wait(dve, s_pre, 12 * i + u + 1)
                            else:
                                st.settle()
                            ins = nc.vector.scalar_tensor_tensor(
                                out=acc[:, u % 4, j:L], in0=PS[:, u % 6, 0:L - j],
                                scalar=cw[:, hh, 5 * q + 3 - j:5 * q + 4 - j], in1=acc[:, u % 4, j:L], op0=ALU.mult,
                                op1=ALU.add)
                            if j < 3:
                                st.did(ins)
                            else:
                                ins.then_inc(s_conv, 1)

            heads(0)
            per = taps[0].k
            with dve.Fori(1, H // 2) as i:
                for st in taps:
                    st.at(i * per)
                heads(i)

            own_steps = [Steps(dve, s_g0), Steps(dve, s_g1)]
            STATE_AFTER = (2, 4, 5, 6)

            def decayed_dots(o, i):
                m, y = o * NB + i, i % 2
                wait(dve, e_g, m + 1)
                wait(dve, p_d, m + 1)
                for g, (s0, s1) in enumerate(BANKS):
                    width = OFF[s1] - OFF[s0]
                    ins = nc.vector.tensor_tensor(
                        out=bank_cols(N, g), in0=PS[:, g, 0:2 * width].rearrange("p (y c) -> p y c", y=2),
                        in1=Dt[y][:, OFF[s0]:OFF[s1]].unsqueeze(1).to_broadcast([P, 2, width]), op=ALU.mult)
                ins.then_inc(v_n, 1)

            def state_step(o, u):
                wait(dve, a_sa, o + 1)
                wait(dve, e_dl, 4 * o + u + 1)
                nc.vector.tensor_tensor(out=S[:, u:NP:4], in0=S[:, u:NP:4],
                                        in1=PS[:, STATE_BANKS[u], :].rearrange("p (n k) -> p n k", n=4),
                                        op=ALU.add).then_inc(v_s, 1)

            def solve(o, i, first=False):
                m, t0, y = o * NB + i, o * CH + i * C, i % 2
                r = [R[y][:, b * H:(b + 1) * H] for b in range(B)]
                wait(dve, p_d, m + 1)
                if first:
                    for b, st in enumerate(own_steps):
                        st.did(nc.vector.tensor_scalar(r[b][:, :, 0, 0:C], VO[:, b * H:(b + 1) * H, bass.ds(t0, C)], -1.0,
                                                       None, ALU.mult))
                else:
                    wait(dve, p_r, m)
                    for b, st in enumerate(own_steps):
                        wait(dve, e_ap, 2 * (m - 1) + b + 1)
                        nc.vector.tensor_tensor(
                            out=Ef[b], in0=PS[:, 4 + b, 0:2 * H * (C + 1)].rearrange("p (y h t) -> p y h t", y=2, h=H),
                            in1=Pre[y][:, b * H:(b + 1) * H].unsqueeze(1).to_broadcast([P, 2, H, C + 1]),
                            op=ALU.mult).then_inc(v_ef, 1)
                    for b, st in enumerate(own_steps):
                        wait(dve, v_ef, 2 * (m - 1) + b + 1)
                        st.did(nc.vector.tensor_tensor(out=r[b], in0=r[b], in1=Ef[b].rearrange("p y h t -> p h y t"),
                                                       op=ALU.add))
                dve.wait_ge(v_n, m + 1)
                for s in range(C):
                    n = C - s
                    g = [s0 <= s < s1 for s0, s1 in BANKS].index(True)
                    c0 = OFF[s] - OFF[BANKS[g][0]]
                    for b, st in enumerate(own_steps):
                        st.settle()
                        cols = bank_cols(N, g)[:, :, c0 + b * H * n:c0 + (b + 1) * H * n]
                        st.did(nc.vector.tensor_tensor(
                            out=Pr[b][:, 0:2 * H * n].rearrange("p (y h t) -> p y h t", y=2, h=H),
                            in0=cols.rearrange("p y (h t) -> p y h t", h=H),
                            in1=r[b][:, :, 0, s:s + 1].unsqueeze(1).to_broadcast([P, 2, H, n]), op=ALU.mult))
                    for b, st in enumerate(own_steps):
                        st.settle()
                        dst = r[b][:, :, :, s + 1:C + 1].rearrange("p h y t -> p y h t")
                        ins = nc.vector.tensor_tensor(
                            out=dst, in0=dst, in1=Pr[b][:, 0:2 * H * n].rearrange("p (y h t) -> p y h t", y=2, h=H),
                            op=ALU.subtract)
                        if s < C - 1:
                            st.did(ins)
                        else:
                            ins.then_inc(v_r, 1)
                    if i == 0 and not first and s in STATE_AFTER:
                        state_step(o - 1, STATE_AFTER.index(s))
                if i == 0:
                    wait(dve, a_ws, o)
                    wait(dve, e_we, LB * o)
                    wait(dve, e_wt, NB * o)
                for b in range(B):
                    dve.wait_ge(v_r, 2 * m + b + 1)
                    nc.vector.tensor_tensor(out=Wst[:, i, b * H:(b + 1) * H], in0=r[b][:, :, 0, 0:C],
                                            in1=Suf[y][:, b * H:(b + 1) * H], op=ALU.mult).then_inc(v_w, 1)

            def chunk(o, first=False, last=False):
                for i in range(NB):
                    solve(o, i, first and i == 0)
                    if i < NB - 1:
                        decayed_dots(o, i + 1)
                if not last:
                    decayed_dots(o + 1, 0)

            dve.wait_ge(s_cst, 9)
            me.link(nc.vector.tensor_reduce(own_s[:, :], ident[:, :].rearrange("p (n s) -> p s n", n=NP), AX_X, ALU.add,
                                            negate=True))
            dve.wait_ge(s_silu, 6 * H)
            dve.wait_ge(s_init, 2)
            nc.vector.tensor_copy(pick, own_s[:, :].unsqueeze(2).to_broadcast([P, C, P])).then_inc(v_pk, 1)
            decayed_dots(0, 0)
            chunk(0, first=True)
            first_steps = [st.total() for st in own_steps]
            per = [2 * C * NB] * B
            with dve.Fori(1, NCH - 1) as o:
                for st, k, k0 in zip(own_steps, per, first_steps):
                    st.at(k0 + (o - 1) * k)
                chunk(o)
                assert [st.k for st in own_steps] == per
            for st, k, k0 in zip(own_steps, per, first_steps):
                st.at(k0 + (NCH - 2) * k)
            chunk(NCH - 1, last=True)

            for n in range(NP):
                dve.wait_ge(o_m, n + 1)
                nc.vector.tensor_copy(VO[:, n], PS[:, 4 + n % 2, :]).then_inc(o_c, 1)
            dve.wait_ge(o_d, 1)
            nc.vector.reciprocal(sd, sd).then_inc(o_r, 1)
            for n in range(NP + 1):
                if n < NP:
                    dve.wait_ge(o_b, n + 1)
                    wait(dve, o_g, n - 1)
                    nc.vector.scalar_tensor_tensor(out=oc[:, n % 2], in0=VO[:, n], scalar=lngb[:, 0:1], in1=PS[:, n % 4, :],
                                                   op0=ALU.mult, op1=ALU.mult).then_inc(o_y, 1)
                if n > 0:
                    k = n - 1
                    dve.wait_ge(o_y, k + 1)
                    dve.wait_ge(g_s, 2 * (k % H) + k // H + 1)
                    nc.vector.scalar_tensor_tensor(out=VO[:, k], in0=oc[:, k % 2], scalar=lngb[:, 1:2], in1=G[:, k],
                                                   op0=ALU.add, op1=ALU.mult).then_inc(o_g, 1)
            dve.wait_ge(g_x, 16)
            for n in range(NT):
                dve.wait_ge(o_p, n + 1)
                nc.vector.tensor_tensor(out=xt2[:, n, :], in0=xt2[:, n, :], in1=PS[:, n % 4, 0:D],
                                        op=ALU.add).then_inc(o_x, 1)

            def moments(src, n):
                me.did(nc.vector.bn_stats(stats[:, n, :], src[:, n, :]))

            def mean_var():
                me.settle()
                for n in range(NT):
                    nc.vector.bn_aggr(mv[:, n, :], stats[:, n, :]).then_inc(x_mv, 1)

            def norm_scale(r):
                dve.wait_ge(x_sd, r + 1)
                me.link(nc.vector.reciprocal(rstd[:, :], std[:, :]))
                dve.wait_ge(x_mv, NT * (r + 1))

            def norm_stats(r, src):
                for n in range(NT):
                    moments(src, n)
                mean_var()
                norm_scale(r)

            def keep_xT(r, n, bank):
                dve.wait_ge(x_tp, NT * r + n + 1)
                nc.vector.tensor_copy(xT[:, :, n * P:(n + 1) * P],
                                      PS[:, bank + n % 2, 0:KT * P].rearrange("p (k c) -> p k c", k=KT)).then_inc(x_xT, 1)

            dve.wait_ge(x_ld, 16 * 5)
            dve.wait_ge(x_cst, 6)
            me.link(nc.vector.tensor_scalar(mpad[:, :], mcol_i[:, :], 0, -MASKED, ALU.not_equal, ALU.mult))
            nc.vector.tensor_scalar(mpad[:, :], mpad[:, :], MASKED, None, ALU.add).then_inc(x_mk, 1)
            nc.vector.tensor_scalar(mcol[:, :], mcol_i[:, :], 0, None, ALU.not_equal).then_inc(x_mk, 1)
            dve.wait_ge(x_mk, 2)
            nc.vector.tensor_copy(xV[:, :, :, 16:17], mcol[:, :].unsqueeze(2).unsqueeze(3).to_broadcast([P, NT, XH, 1])
                                  ).then_inc(x_mk, 1)
            for n in range(NT):
                dve.wait_ge(x_ct, n + 1)
                nc.vector.tensor_copy(ctxT[:, :, n * P:(n + 1) * P],
                                      PS[:, 6 + n % 2, 0:KT * P].rearrange("p (k c) -> p k c", k=KT)).then_inc(x_cT, 1)
            def split(t):
                r, n = t // NT, t % NT
                dve.wait_ge(x_hi, t + 1)
                wait(dve, x_mi, t - 1)
                parts = nat[t % 2][:, :, 0:6 * XD].rearrange("p h (y c) -> p h y c", y=6)
                nc.vector.scalar_tensor_tensor(
                    out=rest[:, t % 2].rearrange("p (h c) -> p h c", h=XH),
                    in0=PS[:, 6 + t % 2, 0:D].rearrange("p (h c) -> p h c", h=XH), scalar=1.0 if r == 0 else XD ** -0.5,
                    in1=parts[:, :, 0], op0=ALU.mult, op1=ALU.subtract).then_inc(x_r1, 1)
                if r == 0:
                    nc.vector.tensor_scalar(xV[:, n, :, 0:XD], PS[:, 6 + t % 2, D:2 * D].rearrange("p (h c) -> p h c", h=XH),
                                            mcol[:, n:n + 1], None, ALU.mult)
                    nc.vector.tensor_copy(nat[t % 2][:, :, 6 * XD:6 * XD + 1],
                                          mpad[:, n:n + 1].unsqueeze(2).to_broadcast([P, XH, 1]))
                elif n < 2:
                    nc.vector.memset(nat[t % 2][:, :, 6 * XD:6 * XD + 1], 1.0)

            def low(t):
                r = t // NT
                dve.wait_ge(x_mi, t + 1)
                dve.wait_ge(x_r1, t + 1)
                parts = nat[t % 2][:, :, 0:6 * XD].rearrange("p h (y c) -> p h y c", y=6)
                nc.vector.tensor_tensor(out=parts[:, :, 5] if r == 0 else parts[:, :, 2],
                                        in0=rest[:, t % 2].rearrange("p (h c) -> p h c", h=XH),
                                        in1=parts[:, :, 3] if r == 0 else parts[:, :, 1], op=ALU.subtract).then_inc(x_lo, 1)

            def keep(t):
                r, n = t // NT, t % NT
                for q in range(2, 4):
                    dve.wait_ge(x_tu, 4 * t + q + 1)
                    nc.vector.tensor_copy(stack[r][:, 4 * q:4 * q + 4, n * P:(n + 1) * P],
                                          PS[:, q, :].rearrange("p (h t) -> p h t", h=4)).then_inc(x_ed, 1)

            def stack_up(r):
                for t in range(r * NT, (r + 1) * NT):
                    split(t)
                    if t > r * NT:
                        keep(t - 1)
                    low(t)
                keep((r + 1) * NT - 1)

            stack_up(0)
            dve.wait_ge(o_x, NT)
            norm_stats(0, xt2)
            for n in range(NT):
                wait(dve, x_tp, n - 1)
                nc.vector.tensor_scalar(xn2[:, n % 2], xt2[:, n, :], mv[:, n, 0:1], rstd[:, n:n + 1], ALU.subtract,
                                        ALU.mult).then_inc(x_xn, 1)
                if n > 0:
                    keep_xT(0, n - 1, 6)
            keep_xT(0, NT - 1, 6)
            stack_up(1)
            u = 0

            def keep_maxima(n):
                dve.wait_ge(x_mt, n + 1)
                nc.vector.tensor_copy(MT[:, n * P:(n + 1) * P], PS[0:2 * XH, 6 + n % 2, 0:P]).then_inc(x_q2, 1)

            for n in range(NT):
                w = (n % QT_N + 1) * P
                for pair in range(XH // 2):
                    dve.wait_ge(x_s, u + 1)
                    nc.vector.tensor_reduce(xM[:, n, 2 * pair:2 * pair + 2], PS[:, 2 * (u % 3):2 * (u % 3) + 2, 0:w], AX_X,
                                            ALU.max, negate=True).then_inc(x_mx, 1)
                    u += 1
                dve.wait_ge(x_mx, u)
                wait(dve, x_mt, n - 1)
                me.link(nc.vector.tensor_copy(mnat[:, n % 2, :, 0], xM[:, n, :]))
                nc.vector.tensor_tensor(out=mnat[:, n % 2, :, 1], in0=xM[:, n, :], in1=mnat[:, n % 2, :, 0],
                                        op=ALU.subtract).then_inc(x_mn, 1)
                if n > 0:
                    keep_maxima(n - 1)
            keep_maxima(NT - 1)

            dve.wait_ge(f_ld, 64)

            def affine(t, n, y):
                me.link(nc.vector.tensor_tensor(out=t[:, n, :], in0=t[:, n, :], in1=gb[:, y], op=ALU.mult))
                me.link(nc.vector.tensor_tensor(out=t[:, n, :], in0=t[:, n, :], in1=gb[:, y + 1], op=ALU.add))

            norm_stats(1, se)
            for n in range(ET):
                me.link(nc.vector.tensor_scalar(se[:, n, :], se[:, n, :], mv[:, n, 0:1], rstd[:, n:n + 1], ALU.subtract,
                                                ALU.mult))
                affine(se, n, 2)
                nc.vector.tensor_scalar(se[:, n, :], se[:, n, :], scl[:, 0:1], None, ALU.mult).then_inc(f_se, 1)
            for k in range(B * XG):
                b, g = k // XG, k % XG
                dve.wait_ge(x_dn, k + 1)
                me.link(nc.vector.reciprocal(osum[:, k % 2], PS[:, 6 + k % 2, :]))
                nc.vector.tensor_tensor(out=attT[b][:, g, :], in0=osb[:, k % 2], in1=osum[:, k % 2],
                                        op=ALU.mult).then_inc(x_at, 1)
            for n in range(NT):
                dve.wait_ge(x_op, n + 1)
                nc.vector.tensor_tensor(out=xt2[:, n, :], in0=xt2[:, n, :], in1=PS[:, 4 + n % 2, 0:D],
                                        op=ALU.add).then_inc(x_x, 1)
                if n > 0:
                    dve.wait_ge(x_x, n)
                    moments(xt2, n - 1)
            dve.wait_ge(x_x, NT)
            moments(xt2, NT - 1)
            mean_var()

            for n in range(ET):
                dve.wait_ge(f_st, n + 1)
                nc.vector.tensor_copy(seT[:, :, n * P:(n + 1) * P],
                                      PS[:, 6 + n % 2, 0:KT * P].rearrange("p (k c) -> p k c", k=KT)).then_inc(f_sT, 1)
            norm_scale(2)
            for n in range(NT):
                me.did(nc.vector.tensor_scalar(xf[:, n, :], xt2[:, n, :], mv[:, n, 0:1], rstd[:, n:n + 1], ALU.subtract,
                                               ALU.mult))
            me.settle()
            norm_stats(3, xf)
            for n in range(NT):
                me.link(nc.vector.tensor_scalar(xf[:, n, :], xf[:, n, :], mv[:, n, 0:1], rstd[:, n:n + 1], ALU.subtract,
                                                ALU.mult))
                me.link(nc.vector.tensor_tensor(out=xf[:, n, :], in0=xf[:, n, :], in1=gb[:, 0], op=ALU.mult))
                nc.vector.tensor_tensor(out=xf[:, n, :], in0=xf[:, n, :], in1=gb[:, 1], op=ALU.add).then_inc(x_xn, 1)
                if n > 0:
                    keep_xT(1, n - 1, 6)
            keep_xT(1, NT - 1, 6)
            for u in range(ET * B):
                e, b = u // B, u % B
                dve.wait_ge(f_lk, u + 1)
                nc.vector.tensor_reduce(mE[:, e, b:b + 1], PS[:, u % 4, :], AX_X, ALU.max, negate=True).then_inc(f_mE, 1)
            for u in range(ET * B):
                e, b = u // B, u % B
                dve.wait_ge(f_fs, u + 1)
                me.link(nc.vector.reciprocal(dE[:, e, b:b + 1], dE[:, e, b:b + 1]))
                nc.vector.tensor_scalar(FS[:, e, b * L:(b + 1) * L], FS[:, e, b * L:(b + 1) * L], dE[:, e, b:b + 1], None,
                                        ALU.mult).then_inc(f_fn, 1)
            for n in range(NT + 1):
                if n < NT:
                    dve.wait_ge(f_lt, n + 1)
                    nc.vector.tensor_reduce(mN[:, n:n + 1], PS[:, 4 + 2 * (n % 2):6 + 2 * (n % 2), :]
                                            .rearrange("p b c -> p (b c)"), AX_X, ALU.max, negate=True).then_inc(f_mN, 1)
                if n == 0:
                    continue
                for half in range(2):
                    v = 2 * (n - 1) + half
                    dve.wait_ge(f_ft, v + 1)
                    nc.vector.tensor_copy(FD[:, n - 1, half * L:(half + 1) * L], PS[:, v % 2, :]).then_inc(f_fk, 1)
                for half in range(2):
                    v = 2 * (n - 1) + half
                    dve.wait_ge(f_eh, v + 1)
                    nc.vector.tensor_copy(EC[:, 4 * half:4 * half + 4, (n - 1) * P:n * P],
                                          PS[:, 2 + v % 2, :].rearrange("p (e c) -> p e c", e=4)).then_inc(f_ek, 1)
            dve.wait_ge(f_e1, NT)
            nc.vector.reciprocal(dN[:, :], dN[:, :]).then_inc(f_dn, 1)

            def gated(i, slot):
                e, half = WS * i + slot, slot % 2
                wait(dve, w_ld[slot], 64 * (i + 1))
                dve.wait_ge(w_ge, e + 1)
                wait(dve, w_dn, e - 1)
                for f in range(FT):
                    ins = nc.vector.scalar_tensor_tensor(
                        out=hT[:, half, f], in0=PS[:, 2 * half + 1, f * P:(f + 1) * P],
                        scalar=bgu[:, slot, FT + f:FT + f + 1], in1=gel[:, half, f], op0=ALU.add, op1=ALU.mult)
                ins.then_inc(w_h, 1)

            def outputs(i, slot):
                e, half = WS * i + slot, slot % 2
                dve.wait_ge(w_dn, e + 1)
                for b in range(B):
                    nc.vector.tensor_tensor(out=eo[SL * half:SL * (half + 1), bass.ds(WS // 2 * i + slot // 2, 1), b, :],
                                            in0=PS[SL * b:SL * (b + 1), 4 + half:5 + half, 0:D],
                                            in1=bdn[SL * b:SL * (b + 1), slot:slot + 1, :],
                                            op=ALU.add).then_inc(w_eo, 1)

            def experts(i):
                gated(i, 0)
                for slot in range(WS):
                    if slot + 1 < WS:
                        gated(i, slot + 1)
                    outputs(i, slot)

            dve.wait_ge(f_ft, 2 * NT)
            experts(0)
            with dve.Fori(1, E // WS) as i:
                experts(i)
            dve.wait_ge(f_dn, 1)
            for n in range(NT):
                dve.wait_ge(w_cb, n + 1)
                nc.vector.scalar_tensor_tensor(out=xt2[:, n, :], in0=PS[:, 6 + n % 2, 0:D], scalar=dN[:, n:n + 1],
                                               in1=xt2[:, n, :], op0=ALU.mult, op1=ALU.add).then_inc(w_x, 1)


def kernel(**inputs):
    import numpy as np
    import concourse.bacc as bacc
    from concourse.bass_utils import run_bass_kernel_spmd as run

    a = {k: np.ascontiguousarray(v) for k, v in inputs.items()}

    def by_head(w):
        return w.reshape(KT, P, H, P).transpose(2, 1, 0, 3)

    def by_width(w):
        return w.T.reshape(KT, P, D).transpose(1, 0, 2)

    def by_group(w):
        rows = np.zeros((XH, 32, D), w.dtype)
        rows[:, :XD] = w.T.reshape(XH, XD, D)
        return rows.reshape(XG, P, D).transpose(1, 0, 2)

    conv = [np.concatenate([a[f"L0_attn_c{q}w"].reshape(H, P, 4), a[f"L0_attn_c{q}b"].reshape(H, P, 1)], axis=2)
            for q in "qkv"]
    given = {
        "x": a["x"],
        "w_qkva": np.stack([by_head(a[f"L0_attn_W{q}"]) for q in "qkva"], axis=2),
        "conv_pack": np.concatenate(conv + [a["L0_attn_ba"].reshape(H, P, 1)], axis=2),
        "wb": a["L0_attn_Wb"].reshape(KT, P, H).transpose(1, 0, 2),
        "bb": a["L0_attn_bb"].reshape(H, 1),
        "w_gate": by_head(a["L0_attn_Wg"]),
        "w_o": a["L0_attn_Wo"].reshape(H, P, D).transpose(1, 0, 2),
        "ln_gb": np.stack([a["L0_attn_ln_g"], a["L0_attn_ln_b"]], axis=1),
        "ctx_keys": a["ctx_1024"][:, :L].reshape(NT, P, D).transpose(1, 0, 2),
        "mask_cols": a["mask_BxS2_if1"][:, :L].reshape(NT, P).T,
        "xa_q": by_width(a["L0_xattn_Wq"]),
        "xa_kv": np.concatenate([by_width(a["L0_xattn_Wk"]), by_width(a["L0_xattn_Wv"])], axis=2),
        "xa_o": by_group(a["L0_xattn_Wo"]),
        "slots": a["L0_ffn_slot_embeds"].reshape(ET, P, D).transpose(1, 0, 2),
        "slot_gb": np.stack([a["L0_ffn_slot_g"], a["L0_ffn_slot_b"]]),
        "norm_gb": np.stack([a["L0_ffn_norm_g"], a["L0_ffn_norm_b"]]),
        "scale": a["L0_ffn_scale"],
        "w_gate_up": np.stack([a[f"L0_ffn_W{q}"].reshape(E, KT, P, F).transpose(0, 2, 1, 3) for q in "gu"], axis=2),
        "w_down": a["L0_ffn_Wd"].reshape(E, FT, P, D).transpose(0, 2, 1, 3),
        "b_gu": np.concatenate([a[f"L0_ffn_b{q}"].reshape(E, FT, P).transpose(0, 2, 1) for q in "gu"], axis=2),
        "b_down": a["L0_ffn_bd"],
    }
    nc = bacc.Bacc("TRN2", target_bir_lowering=False, num_devices=1)
    arrays, args = {}, []
    for name, v in given.items():
        v = np.ascontiguousarray(v)
        arrays[name] = v
        args.append(nc.dram_tensor(name, v.shape, mybir.dt.from_np(v.dtype), kind="ExternalInput").ap())
    out = nc.dram_tensor("out", (B, L, D), F32, kind="ExternalOutput").ap()
    decoder_layer(nc, *args, out)
    return run(nc, [arrays], core_ids=[0]).results[0]["out"]
```
